# Optimizing a Trainium2 kernel written in Bass

```python
import numpy as np
import jax
import jax.numpy as jnp

def _softmax(x, axis=-1):
    return jax.nn.softmax(x, axis=axis)

def _gelu(x):
    return jax.nn.gelu(x, approximate=True)

def _silu(x):
    return jax.nn.silu(x)

def _sigmoid(x):
    return jax.nn.sigmoid(x)

def _layernorm(x, axis=-1, eps=1e-05):
    m = jnp.mean(x, axis=axis, keepdims=True)
    v = jnp.var(x, axis=axis, keepdims=True)
    return (x - m) / jnp.sqrt(v + eps)

def _scatter_add(tgt, idx, src, axis=0):
    return tgt.at[idx].add(src)

def _segment_sum(src, seg, n):
    return jax.ops.segment_sum(src, seg, n)
kernel_name = 'mk_audio_tower_d2_tok_audfeat256_r4_a3af2e'

def setup_inputs(seed: int=0):
    np.random.seed(seed)
    _w = jnp.asarray

    def _rec_inputs():
        import jax
        import jax.numpy as jnp
        _rk = jax.random.key(seed)
        x = 7.22013e-05 + 1.00017 * jax.random.normal(jax.random.fold_in(_rk, 1), (16, 750, 128), jnp.float32)
        return x
    x = _rec_inputs()

    def _L0_tok_setup():
        import jax, jax.numpy as jnp
        import numpy as np
        FILTER_SIZE = 8
        INPUT_DIM = 128
        KERNEL_SIZE = 64
        key = jax.random.key(seed)
        k1, k2, k3, k4 = jax.random.split(key, 4)
        user_batch = jax.random.normal(k1, (32, 512, INPUT_DIM), dtype=jnp.float32)
        filt = jax.random.uniform(k2, (FILTER_SIZE, INPUT_DIM), dtype=jnp.float32)
        W_k = jax.random.uniform(k3, (FILTER_SIZE * INPUT_DIM, KERNEL_SIZE), dtype=jnp.float32)
        b_k = jax.random.uniform(k4, (KERNEL_SIZE,), dtype=jnp.float32)
        return {'user_batch': user_batch, 'filt': filt, 'W_k': W_k, 'b_k': b_k}
    _L0_tok_all = _L0_tok_setup()
    _L0_tok_in = {k: v for k, v in _L0_tok_all.items() if k in ('filt', 'W_k', 'b_k')}
    del _L0_tok_all

    def _L0_attn_setup():
        import jax, jax.numpy as jnp
        import numpy as np
        B, L, H, N = (16, 2048, 64, 128)

        def _lru_forward(inputs, Wi, bi, Wo, bo, params_log):
            b, l_seq, _ = inputs.shape
            n = params_log.shape[1]
            u = inputs @ Wi.T + bi
            params = jnp.exp(params_log)
            nu, theta, gamma = (params[0], params[1], params[2])
            u_c = jax.lax.complex(u[..., :n], u[..., n:])
            log2_L = int(np.ceil(np.log2(l_seq)))
            P = 2 ** log2_L
            x = jnp.pad(u_c, ((0, 0), (0, P - l_seq), (0, 0)))
            for i in range(1, log2_L + 1):
                l = 2 ** i
                x = x.reshape(b * P // l, l, n)
                x1, x2 = (x[:, :l // 2], x[:, l // 2:])
                pos = jnp.arange(1, l // 2 + 1, dtype=jnp.float32)
                lambs = jnp.exp(jax.lax.complex(-pos[:, None] * nu, pos[:, None] * theta))
                x2 = x2 + lambs * x1[:, -1:]
                x = jnp.concatenate([x1, x2], axis=1).reshape(b, P, n)
            x = x[:, :l_seq] * gamma
            y = jnp.concatenate([jnp.real(x), jnp.imag(x)], axis=-1)
            return y @ Wo.T + bo
        key = jax.random.key(seed)
        k = jax.random.split(key, 5)
        inputs = jax.random.normal(k[0], (B, L, H), dtype=jnp.float32)
        Wi = jax.random.normal(k[1], (2 * N, H), dtype=jnp.float32) / np.sqrt(H).astype(np.float32)
        bi = jnp.zeros((2 * N,), jnp.float32)
        Wo = jax.random.normal(k[2], (H, 2 * N), dtype=jnp.float32) / np.sqrt(2 * N).astype(np.float32)
        bo = jnp.zeros((H,), jnp.float32)
        r_min, r_max = (0.9, 0.999)
        u1 = jax.random.uniform(k[3], (N,), dtype=jnp.float32)
        u2 = jax.random.uniform(k[4], (N,), dtype=jnp.float32)
        nu_log = jnp.log(-0.5 * jnp.log(u1 * (r_max ** 2 - r_min ** 2) + r_min ** 2))
        theta_log = jnp.log(u2 * 2.0 * np.pi)
        gamma_log = jnp.log(jnp.sqrt(1.0 - jnp.exp(-jnp.exp(nu_log)) ** 2))
        params_log = jnp.stack([nu_log, theta_log, gamma_log])
        return {'inputs': inputs, 'Wi': Wi, 'bi': bi, 'Wo': Wo, 'bo': bo, 'params_log': params_log}
    _L0_attn_all = _L0_attn_setup()
    _L0_attn_in = {k: v for k, v in _L0_attn_all.items() if k in ('Wi', 'bi', 'Wo', 'bo', 'params_log')}
    del _L0_attn_all

    def _L0_ffn_setup():
        import jax, jax.numpy as jnp
        import numpy as np
        DIM = 64
        HEADS = 8
        NUM_KEYS = 64
        NUM_KV = NUM_KEYS ** 2
        PK_TOPK = 16
        FINAL_TOPK = 16
        DIM_KEY = DIM // 2
        P = 2

        def _pk(x, Wq_pk, pk_keys):
            b, n, _ = x.shape
            q = (x @ Wq_pk).reshape(b, n, P, HEADS, DIM_KEY).transpose(2, 0, 1, 3, 4)
            sim = jnp.einsum('pbnhd,pkhd->pbnhk', q, pk_keys)
            scores, idx = jax.lax.top_k(sim, PK_TOPK)
            idx0 = idx[0]
            idx1 = idx[1] * NUM_KEYS
            index = (idx0[..., :, None] + idx1[..., None, :]).reshape(b, n, HEADS, PK_TOPK * PK_TOPK)
            score = (scores[0][..., :, None] + scores[1][..., None, :]).reshape(b, n, HEADS, PK_TOPK * PK_TOPK)
            final_scores, pk_idx = jax.lax.top_k(score, FINAL_TOPK)
            final_indices = jnp.take_along_axis(index, pk_idx, axis=-1)
            final_scores = jax.nn.softmax(final_scores, axis=-1)
            return (final_scores, final_indices)
        key = jax.random.key(seed)
        ks = jax.random.split(key, 7)
        b, n = (2, 256)
        std = 0.02
        x = jax.random.normal(ks[0], (b, n, DIM), dtype=jnp.float32)
        Wq_pk = jax.random.normal(ks[1], (DIM, P * HEADS * DIM_KEY), dtype=jnp.float32) * std
        pk_keys = jax.random.normal(ks[2], (P, NUM_KEYS, HEADS, DIM_KEY), dtype=jnp.float32) * std
        Wq = jax.random.normal(ks[3], (DIM, HEADS * DIM), dtype=jnp.float32) * std
        keys_table = jax.random.normal(ks[4], (NUM_KV * HEADS, DIM), dtype=jnp.float32) * std
        values_table = jax.random.normal(ks[5], (NUM_KV * HEADS, DIM), dtype=jnp.float32) * std
        Wo = jax.random.normal(ks[6], (DIM * HEADS, DIM), dtype=jnp.float32) * std
        return {'x': x, 'Wq_pk': Wq_pk, 'pk_keys': pk_keys, 'Wq': Wq, 'keys_table': keys_table, 'values_table': values_table, 'Wo': Wo}
    _L0_ffn_all = _L0_ffn_setup()
    _L0_ffn_in = {k: v for k, v in _L0_ffn_all.items() if k in ('Wq_pk', 'pk_keys', 'Wq', 'keys_table', 'values_table', 'Wo')}
    del _L0_ffn_all

    def _L1_attn_setup():
        import jax, jax.numpy as jnp
        import numpy as np
        N_HASHES = 4
        N_BUCKETS = 8
        NUM_HEADS = 8
        LN_EPS = 1e-05

        def layer_norm(x, g, b):
            m = jnp.mean(x, axis=-1, keepdims=True)
            v = jnp.mean(jnp.square(x - m), axis=-1, keepdims=True)
            return (x - m) * jax.lax.rsqrt(v + LN_EPS) * g + b
        key = jax.random.key(seed)
        ks = jax.random.split(key, 8)
        B, N, C = (16, 2048, 64)
        dff = 4 * C
        w = 0.05
        return {'x': jax.random.normal(ks[0], (B, N, C), jnp.float32), 'rotations': jax.random.normal(ks[1], (1, C, N_HASHES, N_BUCKETS // 2), jnp.float32), 'norm1_g': jnp.ones((C,), jnp.float32), 'norm1_b': jnp.zeros((C,), jnp.float32), 'q_w': jax.random.normal(ks[2], (C, C), jnp.float32) * w, 'kv_w': jax.random.normal(ks[3], (C, 2 * C), jnp.float32) * w, 'norm2_g': jnp.ones((C,), jnp.float32), 'norm2_b': jnp.zeros((C,), jnp.float32), 'fc1_w': jax.random.normal(ks[4], (C, dff), jnp.float32) * w, 'fc1_b': jnp.zeros((dff,), jnp.float32), 'fc2_w': jax.random.normal(ks[5], (dff, C), jnp.float32) * w, 'fc2_b': jnp.zeros((C,), jnp.float32)}
    _L1_attn_all = _L1_attn_setup()
    _L1_attn_in = {k: v for k, v in _L1_attn_all.items() if k in ('rotations', 'norm1_g', 'norm1_b', 'q_w', 'kv_w', 'norm2_g', 'norm2_b', 'fc1_w', 'fc1_b', 'fc2_w', 'fc2_b')}
    del _L1_attn_all

    def _L1_ffn_setup():
        import jax, jax.numpy as jnp
        import numpy as np
        B, S, H, F, E, K = (8, 1024, 64, 128, 16, 2)
        EPS = 1e-05
        key = jax.random.key(seed)
        ks = jax.random.split(key, 9)
        sc = 0.02
        return {'x': jax.random.normal(ks[0], (B, S, H), dtype=jnp.float32), 'gate_w': jax.random.normal(ks[1], (H, E), dtype=jnp.float32) * sc, 'gate_b': jnp.zeros((E,), dtype=jnp.float32), 'w1': jax.random.normal(ks[2], (E, H, F), dtype=jnp.float32) * sc, 'b1': jnp.zeros((E, F), dtype=jnp.float32), 'w2': jax.random.normal(ks[3], (E, F, H), dtype=jnp.float32) * sc, 'b2': jnp.zeros((E, H), dtype=jnp.float32), 'gamma': jnp.ones((H,), dtype=jnp.float32), 'beta': jnp.zeros((H,), dtype=jnp.float32)}
    _L1_ffn_all = _L1_ffn_setup()
    _L1_ffn_in = {k: v for k, v in _L1_ffn_all.items() if k in ('gate_w', 'gate_b', 'w1', 'b1', 'w2', 'b2', 'gamma', 'beta')}
    del _L1_ffn_all
    return {'x': x, 'L0_tok_filt': _L0_tok_in['filt'], 'L0_tok_W_k': _L0_tok_in['W_k'], 'L0_tok_b_k': _L0_tok_in['b_k'], 'L0_attn_Wi': _L0_attn_in['Wi'], 'L0_attn_bi': _L0_attn_in['bi'], 'L0_attn_Wo': _L0_attn_in['Wo'], 'L0_attn_bo': _L0_attn_in['bo'], 'L0_attn_params_log': _L0_attn_in['params_log'], 'L0_ffn_Wq_pk': _L0_ffn_in['Wq_pk'], 'L0_ffn_pk_keys': _L0_ffn_in['pk_keys'], 'L0_ffn_Wq': _L0_ffn_in['Wq'], 'L0_ffn_keys_table': _L0_ffn_in['keys_table'], 'L0_ffn_values_table': _L0_ffn_in['values_table'], 'L0_ffn_Wo': _L0_ffn_in['Wo'], 'L1_attn_rotations': _L1_attn_in['rotations'], 'L1_attn_norm1_g': _L1_attn_in['norm1_g'], 'L1_attn_norm1_b': _L1_attn_in['norm1_b'], 'L1_attn_q_w': _L1_attn_in['q_w'], 'L1_attn_kv_w': _L1_attn_in['kv_w'], 'L1_attn_norm2_g': _L1_attn_in['norm2_g'], 'L1_attn_norm2_b': _L1_attn_in['norm2_b'], 'L1_attn_fc1_w': _L1_attn_in['fc1_w'], 'L1_attn_fc1_b': _L1_attn_in['fc1_b'], 'L1_attn_fc2_w': _L1_attn_in['fc2_w'], 'L1_attn_fc2_b': _L1_attn_in['fc2_b'], 'L1_ffn_gate_w': _L1_ffn_in['gate_w'], 'L1_ffn_gate_b': _L1_ffn_in['gate_b'], 'L1_ffn_w1': _L1_ffn_in['w1'], 'L1_ffn_b1': _L1_ffn_in['b1'], 'L1_ffn_w2': _L1_ffn_in['w2'], 'L1_ffn_b2': _L1_ffn_in['b2'], 'L1_ffn_gamma': _L1_ffn_in['gamma'], 'L1_ffn_beta': _L1_ffn_in['beta']}

def reference(x, L0_tok_filt, L0_tok_W_k, L0_tok_b_k, L0_attn_Wi, L0_attn_bi, L0_attn_Wo, L0_attn_bo, L0_attn_params_log, L0_ffn_Wq_pk, L0_ffn_pk_keys, L0_ffn_Wq, L0_ffn_keys_table, L0_ffn_values_table, L0_ffn_Wo, L1_attn_rotations, L1_attn_norm1_g, L1_attn_norm1_b, L1_attn_q_w, L1_attn_kv_w, L1_attn_norm2_g, L1_attn_norm2_b, L1_attn_fc1_w, L1_attn_fc1_b, L1_attn_fc2_w, L1_attn_fc2_b, L1_ffn_gate_w, L1_ffn_gate_b, L1_ffn_w1, L1_ffn_b1, L1_ffn_w2, L1_ffn_b2, L1_ffn_gamma, L1_ffn_beta):
    import jax
    import jax.numpy as jnp

    def _L0_tok_ref(user_batch, filt, W_k, b_k):
        import jax, jax.numpy as jnp
        import numpy as np
        FILTER_SIZE = 8
        INPUT_DIM = 128
        KERNEL_SIZE = 64
        B, L, D = user_batch.shape
        F = filt.shape[0]
        n_win = L - F
        idx = jnp.arange(n_win)[:, None] + jnp.arange(F)[None, :]
        windows = user_batch[:, idx, :]
        W = W_k.reshape(F, D, -1)
        out = jnp.einsum('blfd,fd,fdk->blk', windows, filt, W)
        return jax.nn.relu(out + b_k)

    def _L0_attn_ref(inputs, Wi, bi, Wo, bo, params_log):
        import jax, jax.numpy as jnp
        import numpy as np
        B, L, H, N = (16, 2048, 64, 128)

        def _lru_forward(inputs, Wi, bi, Wo, bo, params_log):
            b, l_seq, _ = inputs.shape
            n = params_log.shape[1]
            u = inputs @ Wi.T + bi
            params = jnp.exp(params_log)
            nu, theta, gamma = (params[0], params[1], params[2])
            u_c = jax.lax.complex(u[..., :n], u[..., n:])
            log2_L = int(np.ceil(np.log2(l_seq)))
            P = 2 ** log2_L
            x = jnp.pad(u_c, ((0, 0), (0, P - l_seq), (0, 0)))
            for i in range(1, log2_L + 1):
                l = 2 ** i
                x = x.reshape(b * P // l, l, n)
                x1, x2 = (x[:, :l // 2], x[:, l // 2:])
                pos = jnp.arange(1, l // 2 + 1, dtype=jnp.float32)
                lambs = jnp.exp(jax.lax.complex(-pos[:, None] * nu, pos[:, None] * theta))
                x2 = x2 + lambs * x1[:, -1:]
                x = jnp.concatenate([x1, x2], axis=1).reshape(b, P, n)
            x = x[:, :l_seq] * gamma
            y = jnp.concatenate([jnp.real(x), jnp.imag(x)], axis=-1)
            return y @ Wo.T + bo
        return _lru_forward(inputs, Wi, bi, Wo, bo, params_log)

    def _L0_ffn_ref(x, Wq_pk, pk_keys, Wq, keys_table, values_table, Wo):
        import jax, jax.numpy as jnp
        import numpy as np
        DIM = 64
        HEADS = 8
        NUM_KEYS = 64
        NUM_KV = NUM_KEYS ** 2
        PK_TOPK = 16
        FINAL_TOPK = 16
        DIM_KEY = DIM // 2
        P = 2

        def _pk(x, Wq_pk, pk_keys):
            b, n, _ = x.shape
            q = (x @ Wq_pk).reshape(b, n, P, HEADS, DIM_KEY).transpose(2, 0, 1, 3, 4)
            sim = jnp.einsum('pbnhd,pkhd->pbnhk', q, pk_keys)
            scores, idx = jax.lax.top_k(sim, PK_TOPK)
            idx0 = idx[0]
            idx1 = idx[1] * NUM_KEYS
            index = (idx0[..., :, None] + idx1[..., None, :]).reshape(b, n, HEADS, PK_TOPK * PK_TOPK)
            score = (scores[0][..., :, None] + scores[1][..., None, :]).reshape(b, n, HEADS, PK_TOPK * PK_TOPK)
            final_scores, pk_idx = jax.lax.top_k(score, FINAL_TOPK)
            final_indices = jnp.take_along_axis(index, pk_idx, axis=-1)
            final_scores = jax.nn.softmax(final_scores, axis=-1)
            return (final_scores, final_indices)
        b, n, d = x.shape
        q = (x @ Wq).reshape(b, n, HEADS, DIM) * DIM ** (-0.5)
        kv_scores, indices = _pk(x, Wq_pk, pk_keys)
        offsets = jnp.arange(HEADS, dtype=indices.dtype) * NUM_KV
        ind = indices + offsets[None, None, :, None]
        k = jnp.einsum('bnhk,bnhkd->bnhd', kv_scores, keys_table[ind])
        v = jnp.einsum('bnhk,bnhkd->bnhd', kv_scores, values_table[ind])
        sim = jnp.einsum('bihd,bjhd->bhij', q, k)
        neg = -jnp.finfo(sim.dtype).max
        causal = jnp.tril(jnp.ones((n, n), dtype=bool))
        sim = jnp.where(causal, sim, neg)
        attn = jax.nn.softmax(sim, axis=-1)
        out = jnp.einsum('bhij,bjhd->bhid', attn, v)
        out = out.transpose(0, 2, 1, 3).reshape(b, n, HEADS * DIM)
        return out @ Wo

    def _L1_attn_ref(x, rotations, norm1_g, norm1_b, q_w, kv_w, norm2_g, norm2_b, fc1_w, fc1_b, fc2_w, fc2_b):
        import jax, jax.numpy as jnp
        import numpy as np
        N_HASHES = 4
        N_BUCKETS = 8
        NUM_HEADS = 8
        LN_EPS = 1e-05

        def layer_norm(x, g, b):
            m = jnp.mean(x, axis=-1, keepdims=True)
            v = jnp.mean(jnp.square(x - m), axis=-1, keepdims=True)
            return (x - m) * jax.lax.rsqrt(v + LN_EPS) * g + b
        B, N, C = x.shape
        H = NUM_HEADS
        Dh = C // H
        scale = Dh ** (-0.5)
        x_ = layer_norm(x, norm1_g, norm1_b)
        q = (x_ @ q_w).reshape(B, N, H, Dh).transpose(0, 2, 1, 3)
        rotated = jnp.einsum('btf,fhi->bhti', x_, rotations[0])
        rotated = jnp.concatenate([rotated, -rotated], axis=-1)
        buckets = jnp.argmax(rotated, axis=-1)
        one_hot = jax.nn.one_hot(buckets, N_BUCKETS, dtype=x.dtype)
        sum_buckets = jnp.sum(one_hot, axis=2)
        pooled = jnp.einsum('bnf,bhni->bhif', x_, one_hot)
        pooled = pooled / (jax.lax.stop_gradient(sum_buckets)[..., None] + 1e-20)
        rp_x = pooled.reshape(B, N_HASHES * N_BUCKETS, C)
        sumb = jax.lax.stop_gradient(sum_buckets.reshape(B, N_HASHES * N_BUCKETS))
        M = N_HASHES * N_BUCKETS
        kv = (rp_x @ kv_w).reshape(B, M, 2, H, Dh).transpose(2, 0, 3, 1, 4)
        k, v = (kv[0], kv[1])
        attn = jnp.einsum('bhnd,bhmd->bhnm', q, k) * scale
        mask = (sumb >= 1)[:, None, None, :]
        attn = jnp.where(mask, attn, -jnp.finfo(attn.dtype).max)
        attn = jax.nn.softmax(attn, axis=-1)
        out = jnp.einsum('bhnm,bhmd->bnhd', attn, v).reshape(B, N, C)
        x = x + out
        y = layer_norm(x, norm2_g, norm2_b)
        h = jax.nn.gelu(y @ fc1_w + fc1_b, approximate=False)
        y = h @ fc2_w + fc2_b
        return x + y

    def _L1_ffn_ref(x, gate_w, gate_b, w1, b1, w2, b2, gamma, beta):
        import jax, jax.numpy as jnp
        import numpy as np
        B, S, H, F, E, K = (8, 1024, 64, 128, 16, 2)
        EPS = 1e-05
        gate_logits = x @ gate_w + gate_b
        topk_vals, topk_idx = jax.lax.top_k(gate_logits, K)
        topk_w = jax.nn.softmax(topk_vals, axis=-1)
        h = jax.nn.relu(jnp.einsum('bsh,ehf->bsef', x, w1) + b1)
        expert_out = jnp.einsum('bsef,efh->bseh', h, w2) + b2
        sel = jnp.take_along_axis(expert_out, topk_idx[:, :, :, None], axis=2)
        moe = jnp.sum(topk_w[..., None] * sel, axis=2)
        y = x + moe
        mu = jnp.mean(y, axis=-1, keepdims=True)
        var = jnp.var(y, axis=-1, keepdims=True)
        return (y - mu) / jnp.sqrt(var + EPS) * gamma + beta
    h = _L0_tok_ref(x, L0_tok_filt, L0_tok_W_k, L0_tok_b_k)
    h = h + _L0_attn_ref(_layernorm(h, axis=-1), L0_attn_Wi, L0_attn_bi, L0_attn_Wo, L0_attn_bo, L0_attn_params_log)
    h = h + _L0_ffn_ref(_layernorm(h, axis=-1), L0_ffn_Wq_pk, L0_ffn_pk_keys, L0_ffn_Wq, L0_ffn_keys_table, L0_ffn_values_table, L0_ffn_Wo)
    h = h + _L1_attn_ref(_layernorm(h, axis=-1), L1_attn_rotations, L1_attn_norm1_g, L1_attn_norm1_b, L1_attn_q_w, L1_attn_kv_w, L1_attn_norm2_g, L1_attn_norm2_b, L1_attn_fc1_w, L1_attn_fc1_b, L1_attn_fc2_w, L1_attn_fc2_b)
    h = h + _L1_ffn_ref(_layernorm(h, axis=-1), L1_ffn_gate_w, L1_ffn_gate_b, L1_ffn_w1, L1_ffn_b1, L1_ffn_w2, L1_ffn_b2, L1_ffn_gamma, L1_ffn_beta)
    return h

_drawn_inputs = setup_inputs


def setup_inputs(seed=0):
    import zlib

    import numpy as np

    out = dict(_drawn_inputs(seed))
    spreads = {'L0_attn_bi': (0.0, 0.328),
     'L0_attn_bo': (0.0, 0.369),
     'L1_attn_norm1_g': (1.0, 0.6),
     'L1_attn_norm1_b': (0.0, 0.8),
     'L1_attn_norm2_g': (1.0, 0.6),
     'L1_attn_norm2_b': (0.0, 0.8),
     'L1_attn_fc1_b': (0.0, 0.8),
     'L1_attn_fc2_b': (0.0, 0.57),
     'L1_ffn_gate_b': (0.0, 0.8),
     'L1_ffn_b1': (0.0, 0.8),
     'L1_ffn_b2': (0.0, 0.8),
     'L1_ffn_gamma': (1.0, 0.6),
     'L1_ffn_beta': (0.0, 0.765)}
    factors = {'L0_ffn_Wq_pk': 8.0,
     'L0_ffn_pk_keys': 8.0,
     'L0_ffn_Wq': 57.304,
     'L0_ffn_keys_table': 64.0,
     'L0_ffn_values_table': 8.0,
     'L0_ffn_Wo': 8.0,
     'L1_attn_rotations': 8.0,
     'L1_attn_q_w': 8.0,
     'L1_attn_kv_w': 6.407,
     'L1_ffn_gate_w': 7.773,
     'L1_ffn_w1': 8.0,
     'L1_ffn_w2': 8.0}
    for name, (base, spread) in spreads.items():
        noise = np.random.default_rng([zlib.crc32(name.encode()), seed]).standard_normal(out[name].shape)
        drawn = base * np.exp(spread * noise) if base else spread * noise
        out[name] = jnp.asarray(drawn.astype(out[name].dtype))
    for name, factor in factors.items():
        out[name] = (out[name] * factor).astype(out[name].dtype)
    return out
```

```python
import math
from contextlib import ExitStack

import numpy as np

import concourse.bass as bass
from concourse import mybir

ALU = mybir.AluOpType
ACT = mybir.ActivationFunctionType
AX = mybir.AxisListType
F32 = mybir.dt.float32
I32 = mybir.dt.int32
U32 = mybir.dt.uint32

P = 128
D_IN = 128
C = 64
TAPS = 8
NST = 128
HEADS = 8
NKEY = 64
TOPK = 16
HASHES, BUCKETS = 4, 8
M_LSH = HASHES * BUCKETS
DH_LSH = C // HEADS
DFF = 4 * C
EXPERTS, FEXP = 16, 128
EPS = 1e-5
NEG = -1e30
LOWEST = -3.0e38
ROUND = 12582912.0
TWO_PI = 2.0 * math.pi

CAND_LEN = [TOPK // (a + 1) for a in range(TOPK)]
CAND_OFF = [sum(CAND_LEN[:a]) for a in range(TOPK)]
NCAND = sum(CAND_LEN)
CAND_RUNS = []
for _a, _n in enumerate(CAND_LEN):
    if CAND_RUNS and CAND_RUNS[-1][2] == _n:
        CAND_RUNS[-1][1] += 1
    else:
        CAND_RUNS.append([_a, 1, _n])

RING = 4


class Steps:

    def __init__(self, sem, per):
        self.sem, self.per, self.b, self.n = sem, per, 0, 0

    def begin(self, b):
        self.b, self.n = b, 0

    def up(self):
        self.n += 1
        return 1

    def now(self):
        return self.b * self.per + self.n

    def end(self):
        assert self.n == self.per, (self.n, self.per)


def audio_tower(nc, x, filt, w_k, b_k, wi_t, bi, wo_t, bo, lru_log, wqpk_t, keys_t, wq, kv_rows, wo_pk,
                rot, n1g, n1b, q_w, kv_w, n2g, n2b, fc1_w, fc1_b, fc2_w, fc2_b,
                gate_w, gate_b, w1, b1, w2, b2, gamma, beta, out, h1_dram, n1t_dram):
    B, L, _ = x.shape
    N = L - TAPS
    NT = -(-N // P)
    NP_ = NT * P
    TAIL = N - (NT - 1) * P
    XTAIL = L - (NT - 1) * P
    HALF = NP_ // 2
    assert HALF <= 512 and NCAND == 50

    with ExitStack() as ctx:
        def sb(name, shape, dt=F32):
            return ctx.enter_context(nc.sbuf_tensor(name, shape, dt))

        ps = ctx.enter_context(nc.psum_tensor("ps", [P, 8 * 512], F32))

        def bank(i, n, rows=P, off=0):
            return ps[0:rows, i * 512 + off:i * 512 + off + n]

        ident = sb("ident", [P, P])
        causal = sb("causal", [P, P])
        ones_row = sb("ones_row", [1, P])
        wc = sb("wc", [P, TAPS, C])
        filt_c = sb("filt_c", [P, TAPS])
        bk_row = sb("bk_row", [1, C])
        wi_aug = sb("wi_aug", [C + 1, 2 * NST])
        wo_g = sb("wo_g", [P, 2, C])
        bo_row = sb("bo_row", [1, C])
        logs = sb("logs", [P, 3])
        lam = sb("lam", [P, 4])
        small = sb("small", [P, 12])
        small_i = sb("small_i", [P, 4], I32)
        cos_t = sb("cos_t", [P, NP_])
        sin_t = sb("sin_t", [P, NP_])
        w_sim = sb("w_sim", [C, 2 * HEADS * NKEY])
        wq_s = sb("wq_s", [C, HEADS * C])
        wo_f = sb("wo_f", [P, HEADS * C // P, C])
        n1gb = sb("n1gb", [P, 2, C])
        n2gb = sb("n2gb", [P, 2, C])
        ngb = sb("ngb", [P, 2, C])
        rot_s = sb("rot_s", [C, HASHES * BUCKETS // 2])
        qw_s = sb("qw_s", [C, C])
        kvw_s = sb("kvw_s", [C, 2 * C])
        head_mask = sb("head_mask", [C, HEADS])
        v_mask = sb("v_mask", [P, 2, C])
        fc1_s = sb("fc1_s", [C, DFF])
        fc1b_c = sb("fc1b_c", [P, 2])
        fc2_s = sb("fc2_s", [P, 2, C])
        fc2b_row = sb("fc2b_row", [1, C])
        gate_aug = sb("gate_aug", [C + 1, EXPERTS])
        w1_aug = sb("w1_aug", [C + 1, EXPERTS, FEXP])
        w2_s = sb("w2_s", [P, EXPERTS, C])
        b2_row = sb("b2_row", [1, EXPERTS, C])
        iota_c = sb("iota_c", [P, NCAND])
        iota_e = sb("iota_e", [P, EXPERTS])
        rank8 = sb("rank8", [P, BUCKETS])
        head_base = sb("head_base", [P, HEADS])
        valid = sb("valid", [P, NT])

        xrow = sb("xrow", [P, NT, D_IN])
        xt = sb("xt", [P, NP_ + TAPS])
        h0 = sb("h0", [P, NT, C])
        z = sb("z", [P, NT, C])
        zt = sb("zt", [C + 1, NP_])
        wide = sb("wide", [P, 6, NP_])
        h1a = sb("h1a", [P, NT, C])
        n1t = sb("n1t", [C, NP_])
        lnv = sb("lnv", [P, 4, NT])

        tv = sb("tv", [P, 2 * HEADS, TOPK])
        ti = sb("ti", [P, 2 * HEADS, TOPK], U32)
        tif = sb("tif", [P, 2 * HEADS, TOPK])
        cs = sb("cs", [P, HEADS, NCAND])
        ci = sb("ci", [P, HEADS, NCAND])
        cs2 = sb("cs2", [P, HEADS, NCAND])
        fs = sb("fs", [P, HEADS, TOPK])
        fe = sb("fe", [P, HEADS, TOPK])
        fp = sb("fp", [P, HEADS, TOPK], U32)
        fpf = sb("fpf", [P, HEADS, TOPK])
        fsum = sb("fsum", [P, 2, HEADS])
        row_i = sb("row_i", [P, NT, HEADS * TOPK], U32)
        row_w = sb("row_w", [P, NT, HEADS * TOPK])
        ONEHOT = HEADS // 2 * TOPK * NCAND
        flat = wide[:, :, :].rearrange("p a n -> p (a n)")
        onehot = flat[:, 0:ONEHOT]
        trest = flat[:, ONEHOT:ONEHOT + 2 * HEADS * NKEY].rearrange("p (g k) -> p g k", k=NKEY)

        ring = sb("ring", [P, RING, TOPK, 2 * C])
        kv = sb("kv", [P, NT, 2, HEADS, C])

        kt = sb("kt", [P, HEADS // 2, NP_])
        v = sb("v", [P, NT, HEADS, C])
        h1c = sb("h1c", [P, NT, C])
        lt = sb("lt", [C + 1, NP_])
        n1tc = lt
        qt = sb("qt", [P, HEADS // 2, P])
        prob = sb("prob", [P, 2, NP_])
        probt = sb("probt", [P, 2, NP_])
        nmax = sb("nmax", [P, HEADS])
        rsum = sb("rsum", [P, HEADS])
        rinv = sb("rinv", [P, HEADS])
        on = sb("on", [P, HEADS * C])
        ot = sb("ot", [P, HEADS // 2, P])
        n2 = sb("n2", [P, NT, C])
        xh = sb("xh", [P, NT, C + 1])
        tmp = sb("tmp", [P, NT, C])
        ln2 = sb("ln2", [P, 4, NT])
        rots = sb("rots", [P, NT, HASHES, BUCKETS])
        oneh = sb("oneh", [P, NT, HASHES, BUCKETS])
        rmx = sb("rmx", [P, NT, HASHES])
        pool_s = sb("pool_s", [M_LSH, C + 1])
        pinv = sb("pinv", [M_LSH, 2])
        rpt = sb("rpt", [C + 1, M_LSH])
        rpt4 = sb("rpt4", [C, 4, M_LSH])
        kbd = sb("kbd", [C + 1, HEADS, M_LSH])
        vbd = sb("vbd", [P, 2, C])
        lp = prob[:, 0, 0:HEADS * M_LSH].rearrange("p (h m) -> p h m", m=M_LSH)
        lpt = probt[:, 0, 0:2 * P].rearrange("p (g t) -> p g t", g=2)
        lqt = kt[0:C + 1, 0, :]
        lmx = sb("lmx", [P, 3, HEADS])
        hidden = prob
        hexp = probt
        gl = sb("gl", [P, NT, EXPERTS])
        gtop = sb("gtop", [P, NT, 8])
        gidx = sb("gidx", [P, NT, 8], U32)
        gidf = sb("gidf", [P, NT, 8])
        gw = sb("gw", [P, 4, NT])
        coef = sb("coef", [P, NT, EXPERTS])
        coef2 = sb("coef2", [P, NT, EXPERTS])
        moe = on[:, 0:NT * C].rearrange("p (t c) -> p t c", c=C)
        sq2 = ot[:, :, :].rearrange("p g n -> p (g n)")[:, 0:NT * C].rearrange("p (t c) -> p t c", c=C)
        outb = sb("outb", [P, NT, C])

        rises = {}

        def sem(name, rise=None):
            rises[name] = rise
            return ctx.enter_context(nc.semaphore(name))

        x_loaded = sem("x_loaded", 32)
        x_turned = sem("x_turned", 2)
        xt_ready = sem("xt_ready", 2)
        conv_done = sem("conv_done", 1)
        h0_ready = sem("h0_ready", 1)
        z_ready = sem("z_ready", 1)
        z_turned = sem("z_turned", 2)
        zt_ready = sem("zt_ready", 2)
        u_done = sem("u_done", 1)
        y_ready = sem("y_ready", 1)
        lru_done = sem("lru_done", 1)
        h1_ready = sem("h1_ready", 1)
        n1_ready = sem("n1_ready", 1)
        n1_turned = sem("n1_turned", 2)
        n1t_ready = sem("n1t_ready", 2)
        a_stored = sem("a_stored", 32)
        sims_done = sem("sims_done", NT)
        sims_used = sem("sims_used", NT)
        soft_in = sem("soft_in", NT)
        soft_exp = sem("soft_exp", NT)
        rows_ready = sem("rows_ready", NT)
        kv_ready = sem("kv_ready", NT)
        k_turned = sem("k_turned", NT)
        kt_ready = sem("kt_ready", NT)
        v_ready = sem("v_ready", 1)
        c_loaded = sem("c_loaded", 32)
        c_used = sem("c_used", 1)
        q_done = sem("q_done", NT)
        qt_ready = sem("qt_ready", NT)
        s_done = sem("s_done", NT * HEADS)
        max_ready = sem("max_ready", NT * HEADS)
        p_ready = sem("p_ready", NT * HEADS)
        p_turned = sem("p_turned", NT * HEADS)
        pt_ready = sem("pt_ready", NT * HEADS)
        o_done = sem("o_done", NT * HEADS)
        on_ready = sem("on_ready", NT)
        on_turned = sem("on_turned", NT)
        ot_ready = sem("ot_ready", NT)
        ffn_done = sem("ffn_done", 1)
        xh_ready = sem("xh_ready", 1)
        lt_turned = sem("lt_turned", 6)
        lt_ready = sem("lt_ready", 6)
        rot_done = sem("rot_done", 1)
        oneh_ready = sem("oneh_ready", 1)
        pooled = sem("pooled", 1)
        pool_ready = sem("pool_ready", 1)
        rp_turned = sem("rp_turned", 1)
        rpt_ready = sem("rpt_ready", 2)
        kvl_done = sem("kvl_done", 1)
        kbd_ready = sem("kbd_ready", 1)
        lq_done = sem("lq_done", 1)
        lqt_ready = sem("lqt_ready", 1)
        logit_done = sem("logit_done", NT)
        lmax_ready = sem("lmax_ready", NT)
        lexp_ready = sem("lexp_ready", NT)
        lp_turned = sem("lp_turned", NT)
        lpt_ready = sem("lpt_ready", NT)
        lo_done = sem("lo_done", NT)
        y2_ready = sem("y2_ready", 1)
        fc1_done = sem("fc1_done", 2)
        hid_ready = sem("hid_ready", 2)
        fc2_done = sem("fc2_done", 1)
        n3_ready = sem("n3_ready", 1)
        gate_done = sem("gate_done", 1)
        gsoft_in = sem("gsoft_in", 1)
        gsoft_out = sem("gsoft_out", 1)
        e_hid = sem("e_hid", EXPERTS)
        e_relu = sem("e_relu", EXPERTS)
        e_out = sem("e_out", EXPERTS)
        e_used = sem("e_used", EXPERTS)
        out_ready = sem("out_ready", 1)
        out_stored = sem("out_stored", 32)
        std = [sem("std0", 1), sem("std1", 1), sem("std2", 5)]
        root = [sem("root0", 1), sem("root1", 1), sem("root2", 5)]
        vec_a, vec_t = sem("vec_a", STEPS["vec_a"]), sem("vec_t", STEPS["vec_t"])
        vec_g, vec_c = sem("vec_g", STEPS["vec_g"]), sem("vec_c", STEPS["vec_c"])
        gathered = [sem(f"gathered{i}") for i in range(RING)]
        ring_free = [sem(f"ring_free{i}") for i in range(RING)]
        w_loaded = sem("w_loaded")
        set_vec, set_act, set_pe, set_pool = sem("set_vec"), sem("set_act"), sem("set_pe"), sem("set_pool")
        gate_pe, gate_pool, gate_vec = sem("gate_pe"), sem("gate_pool"), sem("gate_vec")

        def at(s, b, n):
            return b * rises[s.name] + n

        def after(s, b):
            return at(s, b, rises[s.name])

        def apart(e, count, b):
            if not isinstance(b, int):
                e.sem_inc(count, 1)

        block = ctx.enter_context(nc.Block())

        def is_first(b):
            return isinstance(b, int) and b == 0

        def pipeline(e, stage_a, topk, weigh, kv_final, rest):
            def turn_of(i, ahead=True, gather=True, behind=True):
                if ahead:
                    stage_a(i + 1)
                for t in range(NT):
                    if gather:
                        weigh(i, t, 0)
                    if behind:
                        rest(i - 1, t)
                    if gather:
                        weigh(i, t, 1)
                    if ahead:
                        topk(i + 1, t)
                if gather:
                    kv_final(i)

            stage_a(0)
            for t in range(NT):
                topk(0, t)
            turn_of(0, ahead=B > 1, behind=False)
            if B > 2:
                with e.Fori(1, B - 1) as i:
                    turn_of(i)
            if B > 1:
                turn_of(B - 1, ahead=False)
            turn_of(B, ahead=False, gather=False)

        weights = [
            (filt_c[:, :], filt),
            (wc[:, :, :], w_k.rearrange("(f d) k -> d f k", d=D_IN)),
            (bk_row[:, :], b_k), (wi_aug[0:C, :], wi_t), (wi_aug[C:C + 1, :], bi),
            (wo_g[:, :, :], wo_t.rearrange("(r n) c -> n r c", n=NST)), (bo_row[:, :], bo),
            (logs[:, :], lru_log), (wq_s[:, :], wq),
            (wo_f[:, :, :], wo_pk.rearrange("(g p) c -> p g c", p=P)),
            (ring[0:32, 0, 0:8, :].rearrange("p a b -> p (a b)"), wqpk_t.rearrange("g d c -> d g c")),
            (ring[0:32, 0, 8:16, :].rearrange("p a b -> p (a b)"), keys_t.rearrange("g d k -> d g k")),
            (n1gb[:, 0, :], n1g.to_broadcast([P, C])), (n1gb[:, 1, :], n1b.to_broadcast([P, C])),
            (n2gb[:, 0, :], n2g.to_broadcast([P, C])), (n2gb[:, 1, :], n2b.to_broadcast([P, C])),
            (ngb[:, 0, :], gamma.to_broadcast([P, C])), (ngb[:, 1, :], beta.to_broadcast([P, C])),
            (rot_s[:, :], rot), (qw_s[:, :], q_w), (kvw_s[:, :], kv_w), (fc1_s[:, :], fc1_w),
            (fc1b_c[:, :], fc1_b),
            (fc2_s[:, :, :], fc2_w.rearrange("(g p) c -> p g c", p=P)), (fc2b_row[:, :], fc2_b),
            (gate_aug[0:C, :], gate_w), (gate_aug[C:C + 1, :], gate_b),
            (w1_aug[0:C, :, :], w1.rearrange("e h f -> h e f")), (w1_aug[C:C + 1, :, :], b1),
            (w2_s[:, :, :], w2.rearrange("e f h -> f e h")), (b2_row[:, :, :], b2),
        ]
        ALL_W = 16 * len(weights)

        @block.sync
        def _(sp):
            for dst, src in weights:
                sp.dma_start(dst, src).then_inc(w_loaded, 16)
            sp.wait_ge(set_vec, SET_ZEROED)

            def load_x(b):
                sp.dma_start(xrow[:, 0:NT - 1, :], x[bass.ds(b, 1), 0:(NT - 1) * P, :].rearrange(
                    "o (t p) d -> p (o t) d", p=P)).then_inc(x_loaded, 16)
                sp.dma_start(xrow[0:XTAIL, NT - 1, :], x[bass.ds(b, 1), (NT - 1) * P:L, :].rearrange(
                    "o p d -> (o p) d")).then_inc(x_loaded, 16)

            def load_a(b):
                if not is_first(b):
                    sp.wait_ge(x_turned, after(x_turned, b - 1))
                load_x(b)

            def store_a(b):
                sp.wait_ge(h1_ready, after(h1_ready, b))
                sp.dma_start(h1_dram[bass.ds(b, 1), :, :, :].rearrange("o p t c -> (o p) t c"),
                             h1a[:, :, :]).then_inc(a_stored, 16)
                sp.wait_ge(n1t_ready, after(n1t_ready, b))
                sp.dma_start(n1t_dram[bass.ds(b, 1), :, :].rearrange("o c n -> (o c) n"),
                             n1t[:, :]).then_inc(a_stored, 16)

            def load_c(b):
                sp.wait_ge(a_stored, after(a_stored, b))
                if not is_first(b):
                    sp.wait_ge(c_used, after(c_used, b - 1))
                sp.dma_start(h1c[:, :, :], h1_dram[bass.ds(b, 1), :, :, :].rearrange("o p t c -> (o p) t c")
                             ).then_inc(c_loaded, 16)
                sp.dma_start(n1tc[0:C, :], n1t_dram[bass.ds(b, 1), :, :].rearrange("o c n -> (o c) n")
                             ).then_inc(c_loaded, 16)

            def store_out(b):
                sp.wait_ge(out_ready, after(out_ready, b))
                sp.dma_start(out[bass.ds(b, 1), 0:(NT - 1) * P, :].rearrange("o (t p) c -> p (o t) c", p=P),
                             outb[:, 0:NT - 1, :]).then_inc(out_stored, 16)
                sp.dma_start(out[bass.ds(b, 1), (NT - 1) * P:N, :].rearrange("o p c -> (o p) c"),
                             outb[0:TAIL, NT - 1, :]).then_inc(out_stored, 16)

            def turn_of(i, ahead=True, behind=True):
                if ahead:
                    load_a(i + 1)
                if behind:
                    load_c(i - 1)
                if ahead:
                    store_a(i + 1)
                if behind:
                    store_out(i - 1)

            load_a(0)
            store_a(0)
            turn_of(0, ahead=B > 1, behind=False)
            if B > 2:
                with sp.Fori(1, B - 1) as i:
                    turn_of(i)
            if B > 1:
                turn_of(B - 1, ahead=False)
            turn_of(B, ahead=False)
            sp.wait_ge(out_stored, after(out_stored, B - 1))
            sp.wait_ge(a_stored, after(a_stored, B - 1))

        @block.gpsimd
        def _(pool):
            g = nc.gpsimd
            n = [0]

            def one(ins):
                ins.then_inc(set_pool, 1)
                n[0] += 1

            one(g.memset(ident[:, :], 1.0))
            one(g.memset(causal[:, :], 0.0))
            one(g.memset(head_mask[:, :], 1.0))
            one(g.memset(v_mask[:, :, :], 1.0))
            one(g.memset(valid[:, :], 1.0))
            one(g.iota(cos_t[:, :], pattern=[[1, NP_]], base=0, channel_multiplier=0,
                       allow_small_or_imprecise_dtypes=True))
            one(g.iota(iota_c[:, :], pattern=[[1, NCAND]], base=0, channel_multiplier=0,
                       allow_small_or_imprecise_dtypes=True))
            one(g.iota(iota_e[:, :], pattern=[[1, EXPERTS]], base=0, channel_multiplier=0,
                       allow_small_or_imprecise_dtypes=True))
            one(g.iota(rank8[:, :], pattern=[[-1, BUCKETS]], base=BUCKETS, channel_multiplier=0,
                       allow_small_or_imprecise_dtypes=True))
            one(g.iota(head_base[:, :], pattern=[[NKEY * NKEY, HEADS]], base=0, channel_multiplier=0,
                       allow_small_or_imprecise_dtypes=True))
            pool.wait_ge(set_pool, n[0])
            one(g.affine_select(out=ident[:, :], in_=ident[:, :], compare_op=ALU.is_equal, fill=0.0, base=0,
                                pattern=[[-1, P]], channel_multiplier=1))
            one(g.affine_select(out=causal[:, :], in_=causal[:, :], compare_op=ALU.is_ge, fill=NEG, base=0,
                                pattern=[[-1, P]], channel_multiplier=1))
            one(g.affine_select(out=head_mask[:, :], in_=head_mask[:, :], compare_op=ALU.is_ge, fill=0.0, base=0,
                                pattern=[[-DH_LSH, HEADS]], channel_multiplier=1))
            one(g.affine_select(out=v_mask[:, :, :].rearrange("p g (h d) -> p g h d", d=DH_LSH),
                                in_=v_mask[:, :, :].rearrange("p g (h d) -> p g h d", d=DH_LSH),
                                compare_op=ALU.is_ge, fill=0.0, base=0,
                                pattern=[[P, 2], [-M_LSH, HEADS], [0, DH_LSH]], channel_multiplier=1))
            one(g.affine_select(out=valid[:, :], in_=valid[:, :], compare_op=ALU.is_ge, fill=0.0, base=N - 1,
                                pattern=[[-P, NT]], channel_multiplier=-1))
            pool.wait_ge(set_pool, n[0])
            one(g.affine_select(out=head_mask[:, :], in_=head_mask[:, :], compare_op=ALU.is_ge, fill=0.0,
                                base=DH_LSH - 1, pattern=[[DH_LSH, HEADS]], channel_multiplier=-1))
            one(g.affine_select(out=v_mask[:, :, :].rearrange("p g (h d) -> p g h d", d=DH_LSH),
                                in_=v_mask[:, :, :].rearrange("p g (h d) -> p g h d", d=DH_LSH),
                                compare_op=ALU.is_ge, fill=0.0, base=M_LSH - 1,
                                pattern=[[-P, 2], [M_LSH, HEADS], [0, DH_LSH]], channel_multiplier=-1))
            assert n[0] == SET_POOL
            pool.wait_ge(set_pool, SET_POOL)
            pool.wait_ge(set_vec, SET_VEC)

            def body(b):
                for t in range(NT):
                    rows = P if t < NT - 1 else TAIL
                    pool.wait_ge(rows_ready, at(rows_ready, b, t + 1))
                    pool.sem_inc(gate_pool, 1)
                    for h in range(HEADS):
                        use, slot = divmod(t * HEADS + h, RING)
                        pool.wait_ge(ring_free[slot], b * (NT * HEADS // RING) + use + 1)
                        pool.sem_inc(gate_pool, 1)
                        for r in range(TOPK):
                            j = h * TOPK + r
                            g.indirect_dma_start(ring[0:rows, slot, r, :], None, kv_rows,
                                                 bass.IndirectOffsetOnAxis(ap=row_i[0:rows, t, j:j + 1], axis=0)
                                                 ).then_inc(gathered[slot], 16)

            body(0)
            if B > 1:
                with pool.Fori(1, B) as b:
                    body(b)

        @block.scalar
        def _(act):
            a = nc.scalar
            act.wait_ge(set_vec, SET_ANGLE)
            a.activation(sin_t[:, :], sin_t[:, :], ACT.Sin, scale=6.2831845).then_inc(set_act, 1)
            a.activation(cos_t[:, :], cos_t[:, :], ACT.Sin, scale=6.2831845).then_inc(set_act, 1)
            act.wait_ge(set_pe, 2)
            a.activation(w_sim[:, :], bank(0, 1024, C), ACT.Copy).then_inc(set_act, 1)

            def copy_turned(turned, copied, dst, rows, b, base=0):
                act.wait_ge(turned, at(turned, b, base + 1))
                a.activation(dst[0:rows, 0:512], bank(0, 512, rows), ACT.Copy).then_inc(copied, 1)
                act.wait_ge(turned, at(turned, b, base + 2))
                a.activation(dst[0:rows, 512:NP_], bank(1, NP_ - 512, rows), ACT.Copy).then_inc(copied, 1)

            def take_root(i, buf, b, n):
                act.wait_ge(std[i], at(std[i], b, n))
                a.activation(buf[:, 2, :], buf[:, 1, :], ACT.Sqrt).then_inc(root[i], 1)

            def stage_a(b):
                copy_turned(x_turned, xt_ready, xt, P, b)
                act.wait_ge(conv_done, after(conv_done, b))
                a.activation(h0[:, :, :].rearrange("p t c -> p (t c)"), bank(2, NT * C), ACT.Relu
                             ).then_inc(h0_ready, 1)
                take_root(0, lnv, b, 1)
                copy_turned(z_turned, zt_ready, zt, C, b)
                take_root(1, lnv, b, 1)
                if not is_first(b):
                    act.wait_ge(a_stored, after(a_stored, b - 1))
                copy_turned(n1_turned, n1t_ready, n1t, C, b)

            def topk(b, t):
                act.wait_ge(soft_in, at(soft_in, b, t + 1))
                a.activation(fe[:, :, :], fe[:, :, :], ACT.Exp).then_inc(soft_exp, 1)

            def kv_final(b):
                for t in range(NT):
                    act.wait_ge(k_turned, at(k_turned, b, t + 1))
                    a.activation(kt[:, :, t * P:(t + 1) * P],
                                 bank(t % 2, 512).rearrange("p (g n) -> p g n", g=HEADS // 2),
                                 ACT.Copy).then_inc(kt_ready, 1)
                a.activation(v[:, :, :, :].rearrange("p t h c -> p t (h c)"),
                             kv[:, :, 1, :, :].rearrange("p t h c -> p t (h c)"),
                             ACT.Copy).then_inc(v_ready, 1)

            def attention(b, i):
                n = (i + 1) * P
                act.wait_ge(q_done, at(q_done, b, i + 1))
                a.activation(qt[:, :, :].rearrange("p g n -> p (g n)"), bank(0, 512), ACT.Copy,
                             scale=C ** -0.5).then_inc(qt_ready, 1)
                for h in range(HEADS + 1):
                    if h < HEADS:
                        u = i * HEADS + h
                        act.wait_ge(max_ready, at(max_ready, b, u + 1))
                        if u >= 2:
                            act.wait_ge(p_turned, at(p_turned, b, u - 1))
                        a.activation(prob[:, u % 2, 0:n], bank(2 + 2 * (u % 2), n), ACT.Exp,
                                     bias=nmax[:, h:h + 1], accum_out=rsum[:, h:h + 1]
                                     ).then_inc(p_ready, 1)
                    if h > 0:
                        u = i * HEADS + h - 1
                        act.wait_ge(p_turned, at(p_turned, b, u + 1))
                        if u >= 2:
                            act.wait_ge(o_done, at(o_done, b, u - 1))
                        a.activation(probt[:, u % 2, 0:n], bank(0, n), ACT.Copy).then_inc(pt_ready, 1)
                act.wait_ge(on_turned, at(on_turned, b, i + 1))
                a.activation(ot[:, :, :].rearrange("p g n -> p (g n)"), bank(0, 512), ACT.Copy
                             ).then_inc(ot_ready, 1)

            def lsh_a(b):
                take_root(2, ln2, b, 1)
                take_root(2, ln2, b, 2)
                copy_turned(lt_turned, lt_ready, lt, C, b, 0)
                act.wait_ge(rp_turned, after(rp_turned, b))
                a.activation(rpt[:, :], bank(5, M_LSH, C + 1), ACT.Copy).then_inc(rpt_ready, 1)
                a.activation(rpt4[:, :, :], bank(5, M_LSH, C).unsqueeze(1).to_broadcast([C, 4, M_LSH]), ACT.Copy
                             ).then_inc(rpt_ready, 1)
                act.wait_ge(lq_done, after(lq_done, b))
                a.activation(lqt[0:C, :].rearrange("c (g n) -> c g n", g=2),
                             ps[0:C, 1024:2048].rearrange("c (g n) -> c g n", g=2)[:, :, 0:HALF],
                             ACT.Copy, scale=DH_LSH ** -0.5).then_inc(lqt_ready, 1)

            def lsh_b(b):
                for t in range(NT):
                    act.wait_ge(lmax_ready, at(lmax_ready, b, t + 1))
                    a.activation(lp, lp, ACT.Exp).then_inc(lexp_ready, 1)
                    act.wait_ge(lp_turned, at(lp_turned, b, t + 1))
                    a.activation(probt[:, 0, 0:2 * P], bank(0, 2 * P), ACT.Copy).then_inc(lpt_ready, 1)

            def mlp(b):
                take_root(2, ln2, b, 3)
                copy_turned(lt_turned, lt_ready, lt, C, b, 2)
                for f in range(2):
                    act.wait_ge(fc1_done, at(fc1_done, b, f + 1))
                    a.activation(hidden[:, f, :].rearrange("p (g n) -> p g n", g=2),
                                 ps[:, 1024 * (1 + f):1024 * (2 + f)].rearrange("p (g n) -> p g n", g=2)[:, :, 0:HALF],
                                 ACT.Gelu, bias=fc1b_c[:, f:f + 1]).then_inc(hid_ready, 1)

            def moe_a(b):
                take_root(2, ln2, b, 4)
                copy_turned(lt_turned, lt_ready, lt, C, b, 4)
                act.wait_ge(gsoft_in, after(gsoft_in, b))
                a.activation(gw[:, 1, :], gw[:, 0, :], ACT.Exp).then_inc(gsoft_out, 1)

            def moe_b(b):
                for e in range(EXPERTS):
                    act.wait_ge(e_hid, at(e_hid, b, e + 1))
                    if e >= 2:
                        act.wait_ge(e_out, at(e_out, b, e - 1))
                    k = 2 + 2 * (e % 2)
                    a.activation(hexp[:, e % 2, :].rearrange("p (g n) -> p g n", g=2),
                                 ps[:, 512 * k:512 * (k + 2)].rearrange("p (g n) -> p g n", g=2)[:, :, 0:HALF],
                                 ACT.Relu).then_inc(e_relu, 1)
                take_root(2, ln2, b, 5)

            def rest(b, t):
                if t == 0:
                    attention(b, 0)
                    attention(b, 1)
                    attention(b, 2)
                elif t == 1:
                    attention(b, 3)
                    attention(b, 4)
                elif t == 2:
                    attention(b, 5)
                    lsh_a(b)
                elif t == 3:
                    lsh_b(b)
                elif t == 4:
                    mlp(b)
                    moe_a(b)
                else:
                    moe_b(b)

            pipeline(act, stage_a, topk, lambda i, t, half: None, kv_final, rest)

        @block.tensor
        def _(pe):
            mm = nc.tensor.matmul
            pe.wait_ge(set_pool, SET_POOL)
            pe.wait_ge(w_loaded, ALL_W)
            pe.wait_ge(set_vec, SET_VEC - 1)
            wqb = ring[0:32, 0, 0:8, :].rearrange("p a b -> p (a b)")
            kyb = ring[0:32, 0, 8:16, :].rearrange("p a b -> p (a b)")
            for g in range(2 * HEADS):
                last = mm(ps[0:C, g * C:(g + 1) * C], wqb[:, g * C:(g + 1) * C], kyb[:, g * C:(g + 1) * C],
                          start=True, stop=True)
                if g == HEADS - 1:
                    last.then_inc(set_pe, 1)
            last.then_inc(set_pe, 1)
            pe.wait_ge(set_act, 3)

            def turn(src, rows_out, done):
                for t in range(NT):
                    last = nc.tensor.transpose(bank(t // 4, P, rows_out, (t % 4) * P), src(t), ident[:, :])
                    if t == 3 or t == NT - 1:
                        last.then_inc(done, 1)

            def stage_a(b):
                pe.wait_ge(x_loaded, after(x_loaded, b))
                apart(pe, gate_pe, b)
                turn(lambda t: xrow[:, t, :], P, x_turned)
                pe.wait_ge(xt_ready, after(xt_ready, b))
                apart(pe, gate_pe, b)
                for t in range(NT):
                    o = bank(2, C, P, t * C)
                    for f in range(TAPS):
                        mm(o, xt[:, t * P + f:t * P + f + P], wc[:, f, :], start=(f == 0), stop=False)
                    last = mm(o, ones_row[:, :], bk_row[:, :], start=False, stop=True)
                last.then_inc(conv_done, 1)
                pe.wait_ge(z_ready, after(z_ready, b))
                apart(pe, gate_pe, b)
                turn(lambda t: z[:, t, :], C, z_turned)
                pe.wait_ge(zt_ready, after(zt_ready, b))
                apart(pe, gate_pe, b)
                for r in range(2):
                    for c in range(2):
                        last = mm(bank(2 + 2 * r + c, HALF), wi_aug[:, r * NST:(r + 1) * NST],
                                  zt[:, c * HALF:(c + 1) * HALF], start=True, stop=True)
                last.then_inc(u_done, 1)
                pe.wait_ge(y_ready, after(y_ready, b))
                apart(pe, gate_pe, b)
                for t in range(NT):
                    o = bank(2, C, P, t * C)
                    for r in range(2):
                        mm(o, wide[:, r, t * P:(t + 1) * P], wo_g[:, r, :], start=(r == 0), stop=False)
                    last = mm(o, ones_row[:, :], bo_row[:, :], start=False, stop=True)
                last.then_inc(lru_done, 1)
                pe.wait_ge(n1_ready, after(n1_ready, b))
                apart(pe, gate_pe, b)
                turn(lambda t: z[:, t, :], C, n1_turned)
                pe.wait_ge(n1t_ready, after(n1t_ready, b))
                apart(pe, gate_pe, b)

            def topk(b, t):
                for p in range(2):
                    last = mm(bank(4 + p, 512), n1t[:, t * P:(t + 1) * P], w_sim[:, p * 512:(p + 1) * 512],
                              start=True, stop=True)
                last.then_inc(sims_done, 1)
                pe.wait_ge(sims_used, at(sims_used, b, t + 1))
                apart(pe, gate_pe, b)

            def kv_final(b):
                for t in range(NT):
                    pe.wait_ge(kv_ready, at(kv_ready, b, t + 1))
                    apart(pe, gate_pe, b)
                    if t >= 2:
                        pe.wait_ge(kt_ready, at(kt_ready, b, t - 1))
                        apart(pe, gate_pe, b)
                    for g in range(HEADS // 2):
                        last = nc.tensor.transpose(bank(t % 2, P, P, g * P), kv[:, t, 0, 2 * g:2 * g + 2, :].rearrange("p h c -> p (h c)"),
                                                   ident[:, :])
                    last.then_inc(k_turned, 1)
                pe.wait_ge(kt_ready, after(kt_ready, b))
                apart(pe, gate_pe, b)

            def attention(b, i):
                n = (i + 1) * P
                if i == 0:
                    pe.wait_ge(c_loaded, after(c_loaded, b))
                    apart(pe, gate_pe, b)
                    pe.wait_ge(sims_used, after(sims_used, b))
                    apart(pe, gate_pe, b)
                    pe.wait_ge(kt_ready, after(kt_ready, b))
                    apart(pe, gate_pe, b)
                    pe.wait_ge(v_ready, after(v_ready, b))
                    apart(pe, gate_pe, b)
                if i > 0:
                    pe.wait_ge(ot_ready, at(ot_ready, b, i))
                    apart(pe, gate_pe, b)
                for g in range(HEADS // 2):
                    last = mm(bank(0, P, P, g * P), wq_s[:, g * P:(g + 1) * P], n1tc[0:C, i * P:(i + 1) * P],
                              start=True, stop=True)
                last.then_inc(q_done, 1)
                pe.wait_ge(qt_ready, at(qt_ready, b, i + 1))
                apart(pe, gate_pe, b)

                def scores(h):
                    u = i * HEADS + h
                    if u >= 2:
                        pe.wait_ge(p_ready, at(p_ready, b, u - 1))
                        apart(pe, gate_pe, b)
                    r, g, s = C * (h % 2), h // 2, 2 + 2 * (u % 2)
                    for c0 in range(0, n, 512):
                        c1 = min(n, c0 + 512)
                        mm(bank(s, c1 - c0, P, c0), qt[r:r + C, g, :], kt[r:r + C, g, c0:c1],
                           start=True, stop=False, skip_group_check=True)
                    mm(bank(s, P, P, i * P), ident[:, :], causal[:, :], start=False, stop=True,
                       skip_group_check=True).then_inc(s_done, 1)

                def turn_probs(h):
                    u = i * HEADS + h
                    pe.wait_ge(p_ready, at(p_ready, b, u + 1))
                    apart(pe, gate_pe, b)
                    if u >= 1:
                        pe.wait_ge(pt_ready, at(pt_ready, b, u))
                        apart(pe, gate_pe, b)
                    for j in range(i + 1):
                        last = nc.tensor.transpose(bank(0, P, P, j * P), prob[:, u % 2, j * P:(j + 1) * P],
                                                   ident[:, :])
                    last.then_inc(p_turned, 1)

                def values(h):
                    u = i * HEADS + h
                    pe.wait_ge(pt_ready, at(pt_ready, b, u + 1))
                    apart(pe, gate_pe, b)
                    for j in range(i + 1):
                        last = mm(bank(6, C, P, h * C), probt[:, u % 2, j * P:(j + 1) * P], v[:, j, h, :],
                                  start=(j == 0), stop=(j == i))
                    last.then_inc(o_done, 1)

                scores(0)
                if i >= 1:
                    pe.wait_ge(on_ready, at(on_ready, b, i))
                    apart(pe, gate_pe, b)
                for h in range(HEADS):
                    if h + 1 < HEADS:
                        scores(h + 1)
                    turn_probs(h)
                    if h >= 1:
                        values(h - 1)
                values(HEADS - 1)
                pe.wait_ge(on_ready, at(on_ready, b, i + 1))
                apart(pe, gate_pe, b)
                for g in range(HEADS // 2):
                    last = nc.tensor.transpose(bank(0, P, P, g * P), on[:, g * P:(g + 1) * P], ident[:, :])
                last.then_inc(on_turned, 1)
                pe.wait_ge(ot_ready, at(ot_ready, b, i + 1))
                apart(pe, gate_pe, b)
                for g in range(HEADS // 2):
                    last = mm(bank(7, C, P, i * C), ot[:, g, :], wo_f[:, g, :], start=(g == 0),
                              stop=(g == HEADS // 2 - 1))
                if i == NT - 1:
                    last.then_inc(ffn_done, 1)

            def lsh_a(b):
                pe.wait_ge(xh_ready, after(xh_ready, b))
                apart(pe, gate_pe, b)
                turn(lambda t: xh[:, t, 0:C], C, lt_turned)
                pe.wait_ge(lt_ready, at(lt_ready, b, 2))
                apart(pe, gate_pe, b)
                for t in range(NT):
                    last = mm(bank(4, 16, P, t * 16), lt[0:C, t * P:(t + 1) * P], rot_s[:, :], start=True, stop=True)
                last.then_inc(rot_done, 1)
                pe.wait_ge(oneh_ready, after(oneh_ready, b))
                apart(pe, gate_pe, b)
                for t in range(NT):
                    last = mm(bank(5, C + 1, M_LSH), oneh[:, t, :, :].rearrange("p i j -> p (i j)"), xh[:, t, :],
                              start=(t == 0), stop=(t == NT - 1))
                last.then_inc(pooled, 1)
                for c in range(2):
                    last = mm(bank(2 + c, HALF, C), qw_s[:, :], lt[0:C, c * HALF:(c + 1) * HALF],
                              start=True, stop=True)
                last.then_inc(lq_done, 1)
                pe.wait_ge(pool_ready, after(pool_ready, b))
                apart(pe, gate_pe, b)
                nc.tensor.transpose(bank(5, M_LSH, C + 1), pool_s[:, :], ident[0:M_LSH, 0:M_LSH]
                                    ).then_inc(rp_turned, 1)
                pe.wait_ge(rpt_ready, after(rpt_ready, b))
                apart(pe, gate_pe, b)
                mm(bank(5, M_LSH, C), kvw_s[:, 0:C], rpt[0:C, :], start=True, stop=True)
                mm(bank(6, C), rpt4[:, :, :].rearrange("c a m -> c (a m)"), kvw_s[:, C:2 * C],
                   start=True, stop=True).then_inc(kvl_done, 1)
                pe.wait_ge(kbd_ready, after(kbd_ready, b))
                apart(pe, gate_pe, b)
                pe.wait_ge(lqt_ready, after(lqt_ready, b))
                apart(pe, gate_pe, b)

            def lsh_b(b):
                def logits(t):
                    if t >= 2:
                        pe.wait_ge(lmax_ready, at(lmax_ready, b, t - 1))
                        apart(pe, gate_pe, b)
                    mm(bank(4 + t % 2, HEADS * M_LSH), lqt[:, t * P:(t + 1) * P],
                       kbd[:, :, :].rearrange("c h m -> c (h m)"), start=True, stop=True
                       ).then_inc(logit_done, 1)

                logits(0)
                for t in range(NT):
                    if t + 1 < NT:
                        logits(t + 1)
                    pe.wait_ge(lexp_ready, at(lexp_ready, b, t + 1))
                    apart(pe, gate_pe, b)
                    for g in range(2):
                        last = nc.tensor.transpose(bank(0, P, P, g * P), prob[:, 0, g * P:(g + 1) * P], ident[:, :])
                    last.then_inc(lp_turned, 1)
                    pe.wait_ge(lpt_ready, at(lpt_ready, b, t + 1))
                    apart(pe, gate_pe, b)
                    for g in range(2):
                        last = mm(bank(6, C, P, t * C), lpt[:, g, :], vbd[:, g, :], start=(g == 0), stop=(g == 1))
                    last.then_inc(lo_done, 1)

            def mlp(b):
                pe.wait_ge(y2_ready, after(y2_ready, b))
                apart(pe, gate_pe, b)
                turn(lambda t: tmp[:, t, :], C, lt_turned)
                pe.wait_ge(lt_ready, at(lt_ready, b, 4))
                apart(pe, gate_pe, b)
                for f in range(2):
                    for c in range(2):
                        last = mm(bank(2 + 2 * f + c, HALF), fc1_s[:, f * P:(f + 1) * P],
                                  lt[0:C, c * HALF:(c + 1) * HALF], start=True, stop=True)
                    last.then_inc(fc1_done, 1)
                pe.wait_ge(hid_ready, after(hid_ready, b))
                apart(pe, gate_pe, b)
                for t in range(NT):
                    for f in range(2):
                        mm(bank(6, C, P, t * C), hidden[:, f, t * P:(t + 1) * P], fc2_s[:, f, :],
                           start=(f == 0), stop=False)
                    last = mm(bank(6, C, P, t * C), ones_row[:, :], fc2b_row[:, :], start=False, stop=True)
                last.then_inc(fc2_done, 1)

            def moe_a(b):
                pe.wait_ge(n3_ready, after(n3_ready, b))
                apart(pe, gate_pe, b)
                turn(lambda t: n2[:, t, :], C, lt_turned)
                pe.wait_ge(lt_ready, at(lt_ready, b, 6))
                apart(pe, gate_pe, b)
                for t in range(NT):
                    last = mm(bank(7, EXPERTS, P, t * EXPERTS), lt[:, t * P:(t + 1) * P], gate_aug[:, :],
                              start=True, stop=True)
                last.then_inc(gate_done, 1)

            def moe_b(b):
                def expert_in(e):
                    if e >= 2:
                        pe.wait_ge(e_relu, at(e_relu, b, e - 1))
                        apart(pe, gate_pe, b)
                    for c in range(2):
                        last = mm(bank(2 + 2 * (e % 2) + c, HALF), w1_aug[:, e, :],
                                  lt[:, c * HALF:(c + 1) * HALF], start=True, stop=True)
                    last.then_inc(e_hid, 1)

                expert_in(0)
                for e in range(EXPERTS):
                    if e + 1 < EXPERTS:
                        expert_in(e + 1)
                    pe.wait_ge(e_relu, at(e_relu, b, e + 1))
                    apart(pe, gate_pe, b)
                    if e == 1:
                        pe.wait_ge(gsoft_in, after(gsoft_in, b))
                        apart(pe, gate_pe, b)
                    if e >= 2:
                        pe.wait_ge(e_used, at(e_used, b, e - 1))
                        apart(pe, gate_pe, b)
                    for t in range(NT):
                        o = bank(6 + e % 2, C, P, t * C)
                        mm(o, hexp[:, e % 2, t * P:(t + 1) * P], w2_s[:, e, :], start=True, stop=False)
                        last = mm(o, ones_row[:, :], b2_row[:, e, :], start=False, stop=True)
                    last.then_inc(e_out, 1)

            def rest(b, t):
                if t == 0:
                    attention(b, 0)
                    attention(b, 1)
                    attention(b, 2)
                elif t == 1:
                    attention(b, 3)
                    attention(b, 4)
                elif t == 2:
                    attention(b, 5)
                    lsh_a(b)
                elif t == 3:
                    lsh_b(b)
                elif t == 4:
                    mlp(b)
                    moe_a(b)
                else:
                    moe_b(b)

            pipeline(pe, stage_a, topk, lambda i, t, half: None, kv_final, rest)

        @block.vector
        def _(dve):
            vv = nc.vector
            TT, TS, STT = vv.tensor_tensor, vv.tensor_scalar, vv.scalar_tensor_tensor
            zeroed = [0]

            def first(ins):
                ins.then_inc(set_vec, 1)
                zeroed[0] += 1

            first(vv.memset(xrow[:, :, :], 0.0))
            assert zeroed[0] == SET_ZEROED
            first(vv.memset(xt[:, :], 0.0))
            first(vv.memset(ones_row[:, :], 1.0))
            first(vv.memset(zt[C:C + 1, :], 1.0))
            first(vv.memset(lt[C:C + 1, :], 1.0))
            first(vv.memset(xh[:, :, C:C + 1], 1.0))
            first(vv.memset(ring[:, 1:RING, :, :], 0.0))
            dve.wait_ge(w_loaded, ALL_W)
            dve.wait_ge(set_pool, SET_POOL)

            def exact_exp(dst, src, a, n, r, p, whole):
                first(TS(n, src, 1.0 / math.log(2.0), ROUND, ALU.mult, ALU.add))
                dve.wait_ge(set_vec, zeroed[0])
                first(TS(n, n, -ROUND, None, ALU.add))
                dve.wait_ge(set_vec, zeroed[0])
                first(STT(out=r, in0=n, scalar=-0.693359375, in1=src, op0=ALU.mult, op1=ALU.add))
                dve.wait_ge(set_vec, zeroed[0])
                first(STT(out=r, in0=n, scalar=2.12194440e-4, in1=r, op0=ALU.mult, op1=ALU.add))
                dve.wait_ge(set_vec, zeroed[0])
                first(TS(p, r, 1.0 / math.factorial(8), 1.0 / math.factorial(7), ALU.mult, ALU.add))
                for k in range(6, -1, -1):
                    dve.wait_ge(set_vec, zeroed[0])
                    first(TT(p, p, r, ALU.mult))
                    dve.wait_ge(set_vec, zeroed[0])
                    first(TS(p, p, 1.0 / math.factorial(k), None, ALU.add))
                first(TS(n, n, 127.0, 8388608.0, ALU.add, ALU.mult))
                dve.wait_ge(set_vec, zeroed[0])
                first(vv.tensor_copy(whole, n))
                dve.wait_ge(set_vec, zeroed[0])
                first(TT(dst, p, whole.bitcast(F32), ALU.mult))
                dve.wait_ge(set_vec, zeroed[0])

            exact_exp(lam[:, 0:3], logs[:, :], None, small[:, 0:3], small[:, 3:6], small[:, 6:9], small_i[:, 0:3])
            first(TS(small[:, 9:10], lam[:, 0:1], -1.0, None, ALU.mult))
            dve.wait_ge(set_vec, zeroed[0])
            exact_exp(lam[:, 3:4], small[:, 9:10], None, small[:, 0:1], small[:, 3:4], small[:, 6:7],
                      small_i[:, 0:1])
            hi, lo = small[:, 10:11], small[:, 11:12]
            HI_ROUND = 1.5 * 2.0 ** 11
            first(TS(hi, lam[:, 1:2], 1.0 / TWO_PI, HI_ROUND, ALU.mult, ALU.add))
            dve.wait_ge(set_vec, zeroed[0])
            first(TS(hi, hi, -HI_ROUND, None, ALU.add))
            dve.wait_ge(set_vec, zeroed[0])
            first(STT(out=lo, in0=hi, scalar=-6.28125, in1=lam[:, 1:2], op0=ALU.mult, op1=ALU.add))
            dve.wait_ge(set_vec, zeroed[0])
            first(STT(out=lo, in0=hi, scalar=-(TWO_PI - 6.28125), in1=lo, op0=ALU.mult, op1=ALU.add))
            dve.wait_ge(set_vec, zeroed[0])
            first(TS(lo, lo, 1.0 / TWO_PI, None, ALU.mult))
            dve.wait_ge(set_vec, zeroed[0])

            def to_turn(dst, scratch):
                first(TS(scratch, dst, ROUND, None, ALU.add))
                dve.wait_ge(set_vec, zeroed[0])
                first(TS(scratch, scratch, -ROUND, None, ALU.add))
                dve.wait_ge(set_vec, zeroed[0])
                first(TT(dst, dst, scratch, ALU.subtract))
                dve.wait_ge(set_vec, zeroed[0])

            w0, w1_, w2_ = wide[:, 0, :], wide[:, 1, :], wide[:, 2, :]
            first(TS(w0, cos_t[:, :], hi, None, ALU.mult))
            dve.wait_ge(set_vec, zeroed[0])
            to_turn(w0, w2_)
            first(STT(out=sin_t[:, :], in0=cos_t[:, :], scalar=lo, in1=w0, op0=ALU.mult, op1=ALU.add))
            dve.wait_ge(set_vec, zeroed[0])
            to_turn(sin_t[:, :], w2_)
            first(TS(cos_t[:, :], sin_t[:, :], 0.25, None, ALU.add))
            dve.wait_ge(set_vec, zeroed[0])
            to_turn(cos_t[:, :], w2_)
            assert zeroed[0] == SET_ANGLE, zeroed[0]
            first(TT(wc[:, :, :], wc[:, :, :], filt_c[:, :].unsqueeze(2).to_broadcast([P, TAPS, C]), ALU.mult))
            first(TS(wo_g[:, :, :], wo_g[:, :, :], lam[:, 2:3], None, ALU.mult))
            assert zeroed[0] == SET_VEC - 1, zeroed[0]
            dve.wait_ge(set_pe, 2)
            first(vv.memset(ring[:, 0, :, :], 0.0))
            dve.wait_ge(set_act, 2)
            for s in ring_free:
                dve.sem_inc(s, 1)

            va = Steps(vec_a, STEPS["vec_a"])
            vt = Steps(vec_t, STEPS["vec_t"])
            vg = Steps(vec_g, STEPS["vec_g"])
            vc = Steps(vec_c, STEPS["vec_c"])

            def norm(st, x_in, xo, sq, buf, i, n, b):
                vv.tensor_reduce(buf[:, 0, :], x_in, AX.X, ALU.add).then_inc(st.sem, st.up())
                dve.wait_ge(st.sem, st.now())
                TS(buf[:, 0, :], buf[:, 0, :], -1.0 / C, None, ALU.mult).then_inc(st.sem, st.up())
                dve.wait_ge(st.sem, st.now())
                TT(xo, x_in, buf[:, 0, :].unsqueeze(2).to_broadcast([P, NT, C]), ALU.add).then_inc(st.sem, st.up())
                dve.wait_ge(st.sem, st.now())
                TT(sq, xo, xo, ALU.mult).then_inc(st.sem, st.up())
                dve.wait_ge(st.sem, st.now())
                vv.tensor_reduce(buf[:, 1, :], sq, AX.X, ALU.add).then_inc(st.sem, st.up())
                dve.wait_ge(st.sem, st.now())
                TS(buf[:, 1, :], buf[:, 1, :], 1.0 / C, EPS, ALU.mult, ALU.add).then_inc(std[i], 1)
                dve.wait_ge(root[i], at(root[i], b, n))
                vv.reciprocal(buf[:, 3, :], buf[:, 2, :]).then_inc(st.sem, st.up())
                dve.wait_ge(st.sem, st.now())
                return TT(xo, xo, buf[:, 3, :].unsqueeze(2).to_broadcast([P, NT, C]), ALU.mult)

            def stage_a(b):
                va.begin(b)
                sq = wide[:, 5, 0:NT * C].rearrange("p (t c) -> p t c", c=C)
                dve.wait_ge(h0_ready, after(h0_ready, b))
                norm(va, h0[:, :, :], z[:, :, :], sq, lnv, 0, 1, b).then_inc(z_ready, 1)
                dve.wait_ge(u_done, after(u_done, b))
                halves = lambda x: x.rearrange("p (g n) -> p g n", g=2)
                ur = halves(ps[:, 1024:2048])[:, :, 0:HALF]
                ui = halves(ps[:, 2048:3072])[:, :, 0:HALF]
                cos_h, sin_h = halves(cos_t[:, :]), halves(sin_t[:, :])
                w = [wide[:, k, :] for k in range(6)]
                TT(halves(w[2]), ur, cos_h, ALU.mult).then_inc(vec_a, va.up())
                TT(halves(w[3]), ui, sin_h, ALU.mult).then_inc(vec_a, va.up())
                TT(halves(w[4]), ui, cos_h, ALU.mult).then_inc(vec_a, va.up())
                TT(halves(w[5]), ur, sin_h, ALU.mult).then_inc(vec_a, va.up())
                dve.wait_ge(vec_a, va.now())
                TT(w[2], w[2], w[3], ALU.add).then_inc(vec_a, va.up())
                TT(w[4], w[4], w[5], ALU.subtract).then_inc(vec_a, va.up())
                dve.wait_ge(vec_a, va.now())
                decay = lam[:, 3:4].to_broadcast([P, NP_])
                vv.tensor_tensor_scan(w[3], decay, w[2], 0.0, ALU.mult, ALU.add).then_inc(vec_a, va.up())
                vv.tensor_tensor_scan(w[5], decay, w[4], 0.0, ALU.mult, ALU.add).then_inc(vec_a, va.up())
                dve.wait_ge(vec_a, va.now())
                TT(w[0], w[3], cos_t[:, :], ALU.mult).then_inc(vec_a, va.up())
                TT(w[2], w[5], sin_t[:, :], ALU.mult).then_inc(vec_a, va.up())
                TT(w[1], w[3], sin_t[:, :], ALU.mult).then_inc(vec_a, va.up())
                TT(w[4], w[5], cos_t[:, :], ALU.mult).then_inc(vec_a, va.up())
                dve.wait_ge(vec_a, va.now())
                TT(w[0], w[0], w[2], ALU.subtract).then_inc(vec_a, va.up())
                TT(w[1], w[1], w[4], ALU.add).then_inc(y_ready, 1)
                dve.wait_ge(lru_done, after(lru_done, b))
                if not is_first(b):
                    dve.wait_ge(a_stored, after(a_stored, b - 1))
                TT(h1a[:, :, :], h0[:, :, :], bank(2, NT * C).rearrange("p (t c) -> p t c", c=C),
                   ALU.add).then_inc(h1_ready, 1)
                dve.wait_ge(h1_ready, after(h1_ready, b))
                norm(va, h1a[:, :, :], z[:, :, :], sq, lnv, 1, 1, b).then_inc(n1_ready, 1)
                va.end()

            def topk(b, t):
                if t == 0:
                    vt.begin(b)
                dve.wait_ge(sims_done, at(sims_done, b, t + 1))
                apart(dve, gate_vec, b)
                sims = [bank(4, NKEY, P, g * NKEY) for g in range(2 * HEADS)]
                for g in range(2 * HEADS):
                    vv.max(tv[:, g, 0:8], sims[g]).then_inc(vec_t, vt.up())
                dve.wait_ge(vec_t, vt.now())
                apart(dve, gate_vec, b)
                for g in range(2 * HEADS):
                    vv.max_index(ti[:, g, 0:8], tv[:, g, 0:8], sims[g]).then_inc(vec_t, vt.up())
                for g in range(2 * HEADS):
                    ins = vv.match_replace(trest[:, g, :], tv[:, g, 0:8], sims[g], LOWEST)
                    if g < 2 * HEADS - 1:
                        ins.then_inc(vec_t, vt.up())
                ins.then_inc(sims_used, 1)
                dve.wait_ge(sims_used, at(sims_used, b, t + 1))
                apart(dve, gate_vec, b)
                for g in range(2 * HEADS):
                    vv.max(tv[:, g, 8:16], trest[:, g, :]).then_inc(vec_t, vt.up())
                dve.wait_ge(vec_t, vt.now())
                apart(dve, gate_vec, b)
                for g in range(2 * HEADS):
                    vv.max_index(ti[:, g, 8:16], tv[:, g, 8:16], trest[:, g, :]).then_inc(vec_t, vt.up())
                dve.wait_ge(vec_t, vt.now())
                vv.tensor_copy(tif[:, :, :], ti[:, :, :]).then_inc(vec_t, vt.up())
                dve.wait_ge(vec_t, vt.now())
                STT(out=tif[:, HEADS:2 * HEADS, :], in0=tif[:, HEADS:2 * HEADS, :], scalar=float(NKEY),
                            in1=head_base[:, :].unsqueeze(2).to_broadcast([P, HEADS, TOPK]),
                            op0=ALU.mult, op1=ALU.add).then_inc(vec_t, vt.up())
                dve.wait_ge(vec_t, vt.now())
                for dst, src in ((cs, tv), (ci, tif)):
                    for a0, na, ln in CAND_RUNS:
                        off = CAND_OFF[a0]
                        TT(dst[:, :, off:off + na * ln].rearrange("p h (a l) -> p h a l", l=ln),
                                   src[:, 0:HEADS, a0:a0 + na].unsqueeze(3).to_broadcast([P, HEADS, na, ln]),
                                   src[:, HEADS:2 * HEADS, 0:ln].unsqueeze(2).to_broadcast([P, HEADS, na, ln]),
                                   ALU.add).then_inc(vec_t, vt.up())
                dve.wait_ge(vec_t, vt.now())
                apart(dve, gate_vec, b)
                for h in range(HEADS):
                    vv.max(fs[:, h, 0:8], cs[:, h, :]).then_inc(vec_t, vt.up())
                dve.wait_ge(vec_t, vt.now())
                apart(dve, gate_vec, b)
                for h in range(HEADS):
                    vv.max_index(fp[:, h, 0:8], fs[:, h, 0:8], cs[:, h, :]).then_inc(vec_t, vt.up())
                for h in range(HEADS):
                    vv.match_replace(cs2[:, h, :], fs[:, h, 0:8], cs[:, h, :], LOWEST).then_inc(vec_t, vt.up())
                dve.wait_ge(vec_t, vt.now())
                apart(dve, gate_vec, b)
                for h in range(HEADS):
                    vv.max(fs[:, h, 8:16], cs2[:, h, :]).then_inc(vec_t, vt.up())
                dve.wait_ge(vec_t, vt.now())
                apart(dve, gate_vec, b)
                for h in range(HEADS):
                    vv.max_index(fp[:, h, 8:16], fs[:, h, 8:16], cs2[:, h, :]).then_inc(vec_t, vt.up())
                TT(fe[:, :, :], fs[:, :, :], fs[:, :, 0:1].to_broadcast([P, HEADS, TOPK]),
                   ALU.subtract).then_inc(soft_in, 1)
                dve.wait_ge(soft_in, at(soft_in, b, t + 1))
                vv.tensor_copy(fpf[:, :, :], fp[:, :, :]).then_inc(vec_t, vt.up())
                dve.wait_ge(vec_t, vt.now())
                HH = HEADS // 2
                for k in range(2):
                    oh = onehot.rearrange("p (h r c) -> p h r c", h=HH, c=NCAND)
                    hs = slice(k * HH, (k + 1) * HH)
                    TT(oh, fpf[:, hs, :].unsqueeze(3).to_broadcast([P, HH, TOPK, NCAND]),
                               iota_c[:, :].unsqueeze(1).unsqueeze(1).to_broadcast([P, HH, TOPK, NCAND]),
                               ALU.is_equal).then_inc(vec_t, vt.up())
                    dve.wait_ge(vec_t, vt.now())
                    TT(oh, oh, ci[:, hs, :].unsqueeze(2).to_broadcast([P, HH, TOPK, NCAND]), ALU.mult).then_inc(vec_t, vt.up())
                    dve.wait_ge(vec_t, vt.now())
                    vv.tensor_reduce(fpf[:, hs, :], oh, AX.X, ALU.add).then_inc(vec_t, vt.up())
                    dve.wait_ge(vec_t, vt.now())
                dve.wait_ge(soft_exp, at(soft_exp, b, t + 1))
                vv.tensor_reduce(fsum[:, 0, :], fe[:, :, :], AX.X, ALU.add).then_inc(vec_t, vt.up())
                dve.wait_ge(vec_t, vt.now())
                vv.reciprocal(fsum[:, 1, :], fsum[:, 0, :]).then_inc(vec_t, vt.up())
                dve.wait_ge(vec_t, vt.now())
                TT(row_w[:, t, :].rearrange("p (h r) -> p h r", r=TOPK), fe[:, :, :],
                           fsum[:, 1, :].unsqueeze(2).to_broadcast([P, HEADS, TOPK]), ALU.mult).then_inc(vec_t, vt.up())
                vv.tensor_copy(row_i[:, t, :], fpf[:, :, :].rearrange("p h r -> p (h r)")
                               ).then_inc(rows_ready, 1)
                if t == NT - 1:
                    vt.end()

            def weigh(b, t, half):
                if t == 0 and half == 0:
                    vg.begin(b)
                    if not is_first(b):
                        dve.wait_ge(k_turned, after(k_turned, b - 1))
                        dve.wait_ge(v_ready, after(v_ready, b - 1))
                dve.wait_ge(rows_ready, at(rows_ready, b, t + 1))
                for h in range(half * HEADS // 2, (half + 1) * HEADS // 2):
                    use, slot = divmod(t * HEADS + h, RING)
                    dve.wait_ge(gathered[slot], (b * (NT * HEADS // RING) + use + 1) * 16 * TOPK)
                    TT(ring[:, slot, :, :], ring[:, slot, :, :],
                               row_w[:, t, h * TOPK:(h + 1) * TOPK].unsqueeze(2).to_broadcast([P, TOPK, 2 * C]),
                               ALU.mult).then_inc(vec_g, vg.up())
                    dve.wait_ge(vec_g, vg.now())
                    vv.tensor_reduce(kv[:, t, :, h, :],
                                             ring[:, slot, :, :].rearrange("p r (k c) -> p k c r", k=2),
                                             AX.X, ALU.add).then_inc(vec_g, vg.up())
                    dve.wait_ge(vec_g, vg.now())
                    dve.sem_inc(ring_free[slot], 1)
                if half == 1:
                    dve.sem_inc(kv_ready, 1)
                if t == NT - 1 and half == 1:
                    vg.end()

            def attention(b, i):
                n = (i + 1) * P
                if i == 0:
                    vc.begin(b)
                for h in range(HEADS):
                    u = i * HEADS + h
                    dve.wait_ge(s_done, at(s_done, b, u + 1))
                    vv.tensor_reduce(nmax[:, h:h + 1], bank(2 + 2 * (u % 2), n), AX.X, ALU.max, negate=True
                                     ).then_inc(max_ready, 1)
                dve.wait_ge(p_ready, at(p_ready, b, (i + 1) * HEADS))
                vv.reciprocal(rinv[:, :], rsum[:, :]).then_inc(vec_c, vc.up())
                dve.wait_ge(vec_c, vc.now())
                dve.wait_ge(o_done, at(o_done, b, (i + 1) * HEADS))
                if i > 0:
                    dve.wait_ge(on_turned, at(on_turned, b, i))
                TT(on[:, :].rearrange("p (h c) -> p h c", c=C), bank(6, 512).rearrange("p (h c) -> p h c", c=C),
                   rinv[:, :].unsqueeze(2).to_broadcast([P, HEADS, C]), ALU.mult).then_inc(on_ready, 1)

            tiles = lambda x: x.rearrange("p (t c) -> p t c", c=C)

            def lsh_a(b):
                dve.wait_ge(ffn_done, after(ffn_done, b))
                vv.memset(lqt[C:C + 1, :], 1.0).then_inc(vec_c, vc.up())
                TT(h1c[:, :, :], h1c[:, :, :], tiles(bank(7, NT * C)), ALU.add).then_inc(vec_c, vc.up())
                dve.wait_ge(vec_c, vc.now())
                norm(vc, h1c[:, :, :], n2[:, :, :], sq2[:, :, :], ln2, 2, 1, b).then_inc(vec_c, vc.up())
                dve.wait_ge(vec_c, vc.now())
                norm(vc, n2[:, :, :], xh[:, :, 0:C], sq2[:, :, :], ln2, 2, 2, b).then_inc(vec_c, vc.up())
                dve.wait_ge(vec_c, vc.now())
                TT(xh[:, :, 0:C], xh[:, :, 0:C], n1gb[:, 0:1, :].to_broadcast([P, NT, C]), ALU.mult).then_inc(vec_c, vc.up())
                dve.wait_ge(vec_c, vc.now())
                TT(xh[:, :, 0:C], xh[:, :, 0:C], n1gb[:, 1:2, :].to_broadcast([P, NT, C]), ALU.add
                   ).then_inc(xh_ready, 1)
                dve.wait_ge(rot_done, after(rot_done, b))
                rp = bank(4, NT * 16).rearrange("p (t i j) -> p t i j", t=NT, j=BUCKETS // 2)
                vv.tensor_copy(rots[:, :, :, 0:4], rp).then_inc(vec_c, vc.up())
                TS(rots[:, :, :, 4:8], rp, -1.0, None, ALU.mult).then_inc(vec_c, vc.up())
                dve.wait_ge(vec_c, vc.now())
                vv.tensor_reduce(rmx[:, :, :], rots[:, :, :, :], AX.X, ALU.max).then_inc(vec_c, vc.up())
                dve.wait_ge(vec_c, vc.now())
                full = [P, NT * HASHES, BUCKETS]
                r3 = rots[:, :, :, :].rearrange("p t i j -> p (t i) j")
                o3 = oneh[:, :, :, :].rearrange("p t i j -> p (t i) j")
                m3 = rmx[:, :, :].rearrange("p t i -> p (t i)").unsqueeze(2).to_broadcast(full)
                k3 = rank8[:, :].unsqueeze(1).to_broadcast(full)
                TT(o3, r3, m3, ALU.is_equal).then_inc(vec_c, vc.up())
                dve.wait_ge(vec_c, vc.now())
                TT(r3, o3, k3, ALU.mult).then_inc(vec_c, vc.up())
                dve.wait_ge(vec_c, vc.now())
                vv.tensor_reduce(rmx[:, :, :], rots[:, :, :, :], AX.X, ALU.max).then_inc(vec_c, vc.up())
                dve.wait_ge(vec_c, vc.now())
                TT(o3, r3, m3, ALU.is_equal).then_inc(vec_c, vc.up())
                dve.wait_ge(vec_c, vc.now())
                TT(oneh[:, NT - 1, :, :], oneh[:, NT - 1, :, :],
                   valid[:, NT - 1:NT].unsqueeze(2).to_broadcast([P, HASHES, BUCKETS]), ALU.mult
                   ).then_inc(oneh_ready, 1)
                dve.wait_ge(pooled, after(pooled, b))
                cnt = bank(5, 1, M_LSH, C)
                TS(pinv[:, 0:1], cnt, 1e-20, None, ALU.add).then_inc(vec_c, vc.up())
                TS(pool_s[:, C:C + 1], cnt, 1.0, NEG, ALU.is_lt, ALU.mult).then_inc(vec_c, vc.up())
                dve.wait_ge(vec_c, vc.now())
                vv.reciprocal(pinv[:, 1:2], pinv[:, 0:1]).then_inc(vec_c, vc.up())
                dve.wait_ge(vec_c, vc.now())
                TS(pool_s[:, 0:C], bank(5, C, M_LSH), pinv[:, 1:2], None, ALU.mult).then_inc(pool_ready, 1)
                dve.wait_ge(rpt_ready, after(rpt_ready, b))
                vv.tensor_copy(kbd[C:C + 1, :, :],
                                       rpt[C:C + 1, :].unsqueeze(1).to_broadcast([1, HEADS, M_LSH])).then_inc(vec_c, vc.up())
                dve.wait_ge(kvl_done, after(kvl_done, b))
                TT(kbd[0:C, :, :], bank(5, M_LSH, C).unsqueeze(1).to_broadcast([C, HEADS, M_LSH]),
                           head_mask[:, :].unsqueeze(2).to_broadcast([C, HEADS, M_LSH]), ALU.mult).then_inc(vec_c, vc.up())
                TT(vbd[:, :, :], bank(6, C).unsqueeze(1).to_broadcast([P, 2, C]), v_mask[:, :, :], ALU.mult
                   ).then_inc(kbd_ready, 1)

            def lsh_b(b):
                for t in range(NT):
                    dve.wait_ge(logit_done, at(logit_done, b, t + 1))
                    lg = bank(4 + t % 2, HEADS * M_LSH).rearrange("p (h m) -> p h m", m=M_LSH)
                    vv.tensor_reduce(lmx[:, 0, :], lg, AX.X, ALU.max).then_inc(vec_c, vc.up())
                    dve.wait_ge(vec_c, vc.now())
                    if t >= 1:
                        dve.wait_ge(lp_turned, at(lp_turned, b, t))
                    TT(lp, lg, lmx[:, 0, :].unsqueeze(2).to_broadcast([P, HEADS, M_LSH]), ALU.subtract
                       ).then_inc(lmax_ready, 1)
                    dve.wait_ge(lexp_ready, at(lexp_ready, b, t + 1))
                    vv.tensor_reduce(lmx[:, 1, :], lp, AX.X, ALU.add).then_inc(vec_c, vc.up())
                    dve.wait_ge(vec_c, vc.now())
                    vv.reciprocal(lmx[:, 2, :], lmx[:, 1, :]).then_inc(vec_c, vc.up())
                    dve.wait_ge(vec_c, vc.now())
                    dve.wait_ge(lo_done, at(lo_done, b, t + 1))
                    TT(tmp[:, t, :].rearrange("p (h d) -> p h d", d=DH_LSH),
                               bank(6, C, P, t * C).rearrange("p (h d) -> p h d", d=DH_LSH),
                               lmx[:, 2, :].unsqueeze(2).to_broadcast([P, HEADS, DH_LSH]), ALU.mult).then_inc(vec_c, vc.up())

            def mlp(b):
                dve.wait_ge(vec_c, vc.now())
                TT(n2[:, :, :], n2[:, :, :], tmp[:, :, :], ALU.add).then_inc(vec_c, vc.up())
                dve.wait_ge(vec_c, vc.now())
                norm(vc, n2[:, :, :], tmp[:, :, :], sq2[:, :, :], ln2, 2, 3, b).then_inc(vec_c, vc.up())
                dve.wait_ge(vec_c, vc.now())
                TT(tmp[:, :, :], tmp[:, :, :], n2gb[:, 0:1, :].to_broadcast([P, NT, C]), ALU.mult).then_inc(vec_c, vc.up())
                dve.wait_ge(vec_c, vc.now())
                TT(tmp[:, :, :], tmp[:, :, :], n2gb[:, 1:2, :].to_broadcast([P, NT, C]), ALU.add
                   ).then_inc(y2_ready, 1)
                TT(h1c[:, :, :], h1c[:, :, :], n2[:, :, :], ALU.add).then_inc(vec_c, vc.up())
                dve.wait_ge(vec_c, vc.now())
                dve.wait_ge(fc2_done, after(fc2_done, b))
                TT(h1c[:, :, :], h1c[:, :, :], tiles(bank(6, NT * C)), ALU.add).then_inc(vec_c, vc.up())
                dve.wait_ge(vec_c, vc.now())
                norm(vc, h1c[:, :, :], n2[:, :, :], sq2[:, :, :], ln2, 2, 4, b).then_inc(n3_ready, 1)

            def moe_a(b):
                dve.wait_ge(gate_done, after(gate_done, b))
                vv.tensor_copy(gl[:, :, :], bank(7, NT * EXPERTS).rearrange("p (t e) -> p t e", t=NT)).then_inc(vec_c, vc.up())
                dve.wait_ge(vec_c, vc.now())
                apart(dve, gate_vec, b)
                for t in range(NT):
                    vv.max(gtop[:, t, :], gl[:, t, :]).then_inc(vec_c, vc.up())
                dve.wait_ge(vec_c, vc.now())
                apart(dve, gate_vec, b)
                for t in range(NT):
                    vv.max_index(gidx[:, t, :], gtop[:, t, :], gl[:, t, :]).then_inc(vec_c, vc.up())
                TT(gw[:, 0, :], gtop[:, :, 1], gtop[:, :, 0], ALU.subtract).then_inc(gsoft_in, 1)
                dve.wait_ge(gsoft_in, after(gsoft_in, b))
                vv.tensor_copy(gidf[:, :, :], gidx[:, :, :]).then_inc(vec_c, vc.up())
                dve.wait_ge(gsoft_out, after(gsoft_out, b))
                TS(gw[:, 3, :], gw[:, 1, :], 1.0, None, ALU.add).then_inc(vec_c, vc.up())
                dve.wait_ge(vec_c, vc.now())
                vv.reciprocal(gw[:, 2, :], gw[:, 3, :]).then_inc(vec_c, vc.up())
                dve.wait_ge(vec_c, vc.now())
                TT(gw[:, 3, :], gw[:, 2, :], gw[:, 1, :], ALU.mult).then_inc(vec_c, vc.up())
                te = [P, NT, EXPERTS]
                ie = iota_e[:, :].unsqueeze(1).to_broadcast(te)
                TT(coef[:, :, :], gidf[:, :, 0:1].to_broadcast(te), ie, ALU.is_equal).then_inc(vec_c, vc.up())
                TT(coef2[:, :, :], gidf[:, :, 1:2].to_broadcast(te), ie, ALU.is_equal).then_inc(vec_c, vc.up())
                dve.wait_ge(vec_c, vc.now())
                TT(coef[:, :, :], coef[:, :, :], gw[:, 2, :].unsqueeze(2).to_broadcast(te), ALU.mult).then_inc(vec_c, vc.up())
                TT(coef2[:, :, :], coef2[:, :, :], gw[:, 3, :].unsqueeze(2).to_broadcast(te), ALU.mult).then_inc(vec_c, vc.up())
                dve.wait_ge(vec_c, vc.now())
                TT(coef[:, :, :], coef[:, :, :], coef2[:, :, :], ALU.add).then_inc(vec_c, vc.up())
                dve.wait_ge(vec_c, vc.now())

            def moe_b(b):
                for e in range(EXPERTS):
                    dve.wait_ge(e_out, at(e_out, b, e + 1))
                    dst = moe if e == 0 else tmp
                    dve.wait_ge(vec_c, vc.now())
                    TT(dst[:, :, :], tiles(bank(6 + e % 2, NT * C)), coef[:, :, e:e + 1].to_broadcast([P, NT, C]),
                       ALU.mult).then_inc(e_used, 1)
                    dve.wait_ge(e_used, at(e_used, b, e + 1))
                    if e > 0:
                        TT(moe[:, :, :], moe[:, :, :], tmp[:, :, :], ALU.add).then_inc(vec_c, vc.up())
                dve.wait_ge(vec_c, vc.now())
                TT(moe[:, :, :], moe[:, :, :], n2[:, :, :], ALU.add).then_inc(vec_c, vc.up())
                dve.wait_ge(vec_c, vc.now())
                norm(vc, moe[:, :, :], tmp[:, :, :], sq2[:, :, :], ln2, 2, 5, b).then_inc(vec_c, vc.up())
                dve.wait_ge(vec_c, vc.now())
                TT(tmp[:, :, :], tmp[:, :, :], ngb[:, 0:1, :].to_broadcast([P, NT, C]), ALU.mult).then_inc(vec_c, vc.up())
                dve.wait_ge(vec_c, vc.now())
                TT(tmp[:, :, :], tmp[:, :, :], ngb[:, 1:2, :].to_broadcast([P, NT, C]), ALU.add).then_inc(vec_c, vc.up())
                dve.wait_ge(vec_c, vc.now())
                if not is_first(b):
                    dve.wait_ge(out_stored, after(out_stored, b - 1))
                TT(outb[:, :, :], tmp[:, :, :], h1c[:, :, :], ALU.add).then_inc(out_ready, 1)
                dve.wait_ge(out_ready, after(out_ready, b))
                dve.sem_inc(c_used, 1)
                vc.end()

            def rest(b, t):
                if t == 0:
                    attention(b, 0)
                    attention(b, 1)
                    attention(b, 2)
                elif t == 1:
                    attention(b, 3)
                    attention(b, 4)
                elif t == 2:
                    attention(b, 5)
                    lsh_a(b)
                elif t == 3:
                    lsh_b(b)
                elif t == 4:
                    mlp(b)
                    moe_a(b)
                else:
                    moe_b(b)

            pipeline(dve, stage_a, topk, weigh, lambda b: None, rest)


STEPS = dict(vec_a=25, vec_t=870, vec_g=96, vec_c=123)
SET_POOL = 17
SET_ZEROED = 1
SET_ANGLE = 69
SET_VEC = 72


def kernel(x, L0_tok_filt, L0_tok_W_k, L0_tok_b_k, L0_attn_Wi, L0_attn_bi, L0_attn_Wo, L0_attn_bo,
           L0_attn_params_log, L0_ffn_Wq_pk, L0_ffn_pk_keys, L0_ffn_Wq, L0_ffn_keys_table, L0_ffn_values_table,
           L0_ffn_Wo, L1_attn_rotations, L1_attn_norm1_g, L1_attn_norm1_b, L1_attn_q_w, L1_attn_kv_w,
           L1_attn_norm2_g, L1_attn_norm2_b, L1_attn_fc1_w, L1_attn_fc1_b, L1_attn_fc2_w, L1_attn_fc2_b,
           L1_ffn_gate_w, L1_ffn_gate_b, L1_ffn_w1, L1_ffn_b1, L1_ffn_w2, L1_ffn_b2, L1_ffn_gamma, L1_ffn_beta):
    import concourse.bacc as bacc
    from concourse.bass_utils import run_bass_kernel_spmd

    row = lambda a: np.asarray(a).reshape(1, -1)
    arrays = dict(
        x=np.asarray(x), filt=np.asarray(L0_tok_filt).T, w_k=np.asarray(L0_tok_W_k), b_k=row(L0_tok_b_k),
        wi_t=np.asarray(L0_attn_Wi).T, bi=row(L0_attn_bi), wo_t=np.asarray(L0_attn_Wo).T, bo=row(L0_attn_bo),
        lru_log=np.asarray(L0_attn_params_log).T,
        wqpk_t=np.asarray(L0_ffn_Wq_pk).T.reshape(2 * HEADS, C // 2, C),
        keys_t=np.asarray(L0_ffn_pk_keys).transpose(0, 2, 3, 1).reshape(2 * HEADS, C // 2, NKEY),
        wq=np.asarray(L0_ffn_Wq),
        kv_rows=np.concatenate([np.asarray(L0_ffn_keys_table), np.asarray(L0_ffn_values_table)], axis=1),
        wo_pk=np.asarray(L0_ffn_Wo), rot=np.asarray(L1_attn_rotations).reshape(C, -1),
        n1g=row(L1_attn_norm1_g), n1b=row(L1_attn_norm1_b), q_w=np.asarray(L1_attn_q_w),
        kv_w=np.asarray(L1_attn_kv_w), n2g=row(L1_attn_norm2_g), n2b=row(L1_attn_norm2_b),
        fc1_w=np.asarray(L1_attn_fc1_w), fc1_b=np.asarray(L1_attn_fc1_b).reshape(2, P).T, fc2_w=np.asarray(L1_attn_fc2_w),
        fc2_b=row(L1_attn_fc2_b), gate_w=np.asarray(L1_ffn_gate_w), gate_b=row(L1_ffn_gate_b),
        w1=np.asarray(L1_ffn_w1), b1=np.asarray(L1_ffn_b1)[None], w2=np.asarray(L1_ffn_w2),
        b2=np.asarray(L1_ffn_b2)[None], gamma=row(L1_ffn_gamma), beta=row(L1_ffn_beta),
    )
    arrays = {name: np.ascontiguousarray(a) for name, a in arrays.items()}
    nc = bacc.Bacc("TRN2", target_bir_lowering=False, num_devices=1)
    args = {name: nc.dram_tensor(f"in_{name}", a.shape, mybir.dt.from_np(a.dtype), kind="ExternalInput").ap()
            for name, a in arrays.items()}
    B, L, _ = x.shape
    nt = -(-(L - TAPS) // P)
    out = nc.dram_tensor("tokens_out", (B, L - TAPS, C), F32, kind="ExternalOutput").ap()
    h1_dram = nc.dram_tensor("h1_scratch", (B, P, nt, C), F32, kind="Internal").ap()
    n1t_dram = nc.dram_tensor("n1t_scratch", (B, C, nt * P), F32, kind="Internal").ap()
    audio_tower(nc, **args, out=out, h1_dram=h1_dram, n1t_dram=n1t_dram)
    r = run_bass_kernel_spmd(nc, [{f"in_{name}": a for name, a in arrays.items()}], core_ids=[0])
    return r.results[0]["tokens_out"]
```

```python
import math
from contextlib import ExitStack

import numpy as np

import concourse.bass as bass
from concourse import mybir

ALU = mybir.AluOpType
ACT = mybir.ActivationFunctionType
AX = mybir.AxisListType
F32 = mybir.dt.float32
I32 = mybir.dt.int32
U32 = mybir.dt.uint32

P = 128
D_IN = 128
C = 64
TAPS = 8
NST = 128
HEADS = 8
NKEY = 64
TOPK = 16
HASHES, BUCKETS = 4, 8
M_LSH = HASHES * BUCKETS
DH_LSH = C // HEADS
DFF = 4 * C
EXPERTS, FEXP = 16, 128
EPS = 1e-5
NEG = -1e30
LOWEST = -3.0e38
ROUND = 12582912.0
TWO_PI = 2.0 * math.pi

CAND_LEN = [TOPK // (a + 1) for a in range(TOPK)]
CAND_OFF = [sum(CAND_LEN[:a]) for a in range(TOPK)]
NCAND = sum(CAND_LEN)
CAND_RUNS = []
for _a, _n in enumerate(CAND_LEN):
    if CAND_RUNS and CAND_RUNS[-1][2] == _n:
        CAND_RUNS[-1][1] += 1
    else:
        CAND_RUNS.append([_a, 1, _n])

SPREAD = 16384.0
PICKS = 6
RING = 4


class Steps:

    def __init__(self, sem, per):
        self.sem, self.per, self.b, self.n = sem, per, 0, 0

    def begin(self, b, n=0):
        self.b, self.n = b, n

    def up(self):
        self.n += 1
        return 1

    def now(self):
        return self.b * self.per + self.n

    def end(self):
        assert self.n == self.per, (self.n, self.per)


def audio_tower(nc, x, filt, w_k, b_k, wi_t, bi, wo_t, bo, lru_log, wqpk_t, keys_t, wq, kv_rows, wo_pk,
                rot, n1g, n1b, q_w, kv_w, n2g, n2b, fc1_w, fc1_b, fc2_w, fc2_b,
                gate_w, gate_b, w1, b1, w2, b2, gamma, beta, out, h1_dram, n1t_dram):
    B, L, _ = x.shape
    N = L - TAPS
    NT = -(-N // P)
    NP_ = NT * P
    TAIL = N - (NT - 1) * P
    XTAIL = L - (NT - 1) * P
    HALF = NP_ // 2
    USES = NT * HEADS // RING
    assert HALF <= 512 and NCAND == 50

    with ExitStack() as ctx:
        def sb(name, shape, dt=F32):
            return ctx.enter_context(nc.sbuf_tensor(name, shape, dt))

        ps = ctx.enter_context(nc.psum_tensor("ps", [P, 8 * 512], F32))

        def bank(i, n, rows=P, off=0):
            return ps[0:rows, i * 512 + off:i * 512 + off + n]

        ident = sb("ident", [P, P])
        causal = sb("causal", [P, P])
        ones_row = sb("ones_row", [1, P])
        wc = sb("wc", [P, TAPS, C])
        filt_c = sb("filt_c", [P, TAPS])
        bk_row = sb("bk_row", [1, C])
        wi_aug = sb("wi_aug", [C + 1, 2 * NST])
        wo_g = sb("wo_g", [P, 2, C])
        bo_row = sb("bo_row", [1, C])
        logs = sb("logs", [P, 3])
        lam = sb("lam", [P, 4])
        small = sb("small", [P, 12])
        small_i = sb("small_i", [P, 4], I32)
        cos_t = sb("cos_t", [P, NP_])
        sin_t = sb("sin_t", [P, NP_])
        w_sim = sb("w_sim", [C, 2 * HEADS * NKEY])
        wq_s = sb("wq_s", [C, HEADS * C])
        wo_f = sb("wo_f", [P, HEADS * C // P, C])
        n1gb = sb("n1gb", [P, 2, C])
        n2gb = sb("n2gb", [P, 2, C])
        ngb = sb("ngb", [P, 2, C])
        rot_s = sb("rot_s", [C, HASHES * BUCKETS // 2])
        qw_s = sb("qw_s", [C, C])
        kvw_s = sb("kvw_s", [C, 2 * C])
        head_mask = sb("head_mask", [C, HEADS])
        v_mask = sb("v_mask", [P, 2, C])
        fc1_s = sb("fc1_s", [C, DFF])
        fc1b_c = sb("fc1b_c", [P, 2])
        fc2_s = sb("fc2_s", [P, 2, C])
        fc2b_row = sb("fc2b_row", [1, C])
        gate_aug = sb("gate_aug", [C + 1, EXPERTS])
        w1_aug = sb("w1_aug", [C + 1, EXPERTS, FEXP])
        w2_s = sb("w2_s", [P, EXPERTS, C])
        b2_row = sb("b2_row", [EXPERTS, C])
        iota_c = sb("iota_c", [P, NCAND])
        iota_e = sb("iota_e", [P, EXPERTS])
        rank8 = sb("rank8", [P, BUCKETS])
        head_base = sb("head_base", [P, HEADS])
        valid = sb("valid", [P, NT])

        xrow = sb("xrow", [P, NT, D_IN])
        xt = sb("xt", [P, NP_ + TAPS])
        h0 = sb("h0", [P, NT, C])
        z = sb("z", [P, NT, C])
        zt = sb("zt", [C + 1, NP_])
        wide = sb("wide", [P, 6, NP_])
        h1a = sb("h1a", [P, NT, C])
        n1t = sb("n1t", [C, NP_])
        lnv = sb("lnv", [P, 4, NT])

        tv = sb("tv", [P, 2 * HEADS, TOPK])
        ti = sb("ti", [P, 2 * HEADS, TOPK], U32)
        tif = sb("tif", [P, 2 * HEADS, TOPK])
        cs = sb("cs", [P, HEADS, NCAND])
        ci = sb("ci", [P, HEADS, NCAND])
        cs2 = sb("cs2", [P, HEADS, NCAND])
        fs = sb("fs", [P, HEADS, TOPK])
        fe = sb("fe", [P, HEADS, TOPK])
        fp = sb("fp", [P, HEADS, TOPK], U32)
        fpf = sb("fpf", [P, HEADS, TOPK])
        fsum = sb("fsum", [P, 2, HEADS])
        row_i = sb("row_i", [P, NT, HEADS * TOPK], U32)
        row_w = sb("row_w", [P, NT, HEADS * TOPK])
        ONEHOT = HEADS // 2 * TOPK * NCAND
        flat = wide[:, :, :].rearrange("p a n -> p (a n)")
        onehot = flat[:, 0:ONEHOT]
        trest = flat[:, ONEHOT:ONEHOT + 2 * HEADS * NKEY].rearrange("p (g k) -> p g k", k=NKEY)

        ring = sb("ring", [P, RING, TOPK, 2 * C])
        kv = sb("kv", [P, NT, 2, HEADS, C])

        kt = sb("kt", [P, HEADS // 2, NP_])
        v = sb("v", [P, NT, HEADS, C])
        h1c = sb("h1c", [P, NT, C])
        lt = sb("lt", [C + 1, NP_])
        n1tc = lt
        qt = sb("qt", [P, HEADS // 2, P])
        prob = sb("prob", [P, 2, NP_])
        probt = sb("probt", [P, 2, NP_])
        nmax = sb("nmax", [P, HEADS])
        rsum = sb("rsum", [P, HEADS])
        rinv = sb("rinv", [P, HEADS])
        on = sb("on", [P, HEADS * C])
        ot = sb("ot", [P, HEADS // 2, P])
        n2 = sb("n2", [P, NT, C])
        xh = sb("xh", [P, NT, C + 1])
        tmp = sb("tmp", [P, NT, C])
        ln2 = sb("ln2", [P, 4, NT])
        rots = sb("rots", [P, NT, HASHES, BUCKETS])
        oneh = sb("oneh", [P, NT, HASHES, BUCKETS])
        rmx = sb("rmx", [P, NT, HASHES])
        pool_s = sb("pool_s", [M_LSH, C + 1])
        pinv = sb("pinv", [M_LSH, 2])
        rpt = sb("rpt", [C + 1, M_LSH])
        rpt4 = sb("rpt4", [C, 4, M_LSH])
        kbd = sb("kbd", [C + 1, HEADS, M_LSH])
        vbd = sb("vbd", [P, 2, C])
        lp = prob[:, 0, 0:HEADS * M_LSH].rearrange("p (h m) -> p h m", m=M_LSH)
        lpt = probt[:, 0, 0:2 * P].rearrange("p (g t) -> p g t", g=2)
        lqt = kt[0:C + 1, 0, :]
        lmx = sb("lmx", [P, 3, HEADS])
        hidden = prob
        hexp = probt
        gl = sb("gl", [P, NT, EXPERTS])
        gtop = sb("gtop", [P, NT, 8])
        gidx = sb("gidx", [P, NT, 8], U32)
        gidf = sb("gidf", [P, NT, 8])
        gw = sb("gw", [P, 4, NT])
        coef = sb("coef", [P, NT, EXPERTS])
        coef2 = sb("coef2", [P, NT, EXPERTS])
        coeft = v[0:EXPERTS, 0:2, :, :].rearrange("p t h c -> p (t h c)")[:, 0:NP_]
        moe = on[:, 0:NT * C].rearrange("p (t c) -> p t c", c=C)
        sq2 = ot[:, :, :].rearrange("p g n -> p (g n)")[:, 0:NT * C].rearrange("p (t c) -> p t c", c=C)
        outb = sb("outb", [P, NT, C])

        rises = {}

        def sem(name, rise=None):
            rises[name] = rise
            return ctx.enter_context(nc.semaphore(name))

        x_loaded = sem("x_loaded", 32)
        x_turned = sem("x_turned", 2)
        xt_ready = sem("xt_ready", 2)
        conv_done = sem("conv_done", 1)
        h0_ready = sem("h0_ready", 1)
        z_ready = sem("z_ready", 1)
        z_turned = sem("z_turned", 2)
        zt_ready = sem("zt_ready", 2)
        u_done = sem("u_done", 1)
        y_ready = sem("y_ready", 1)
        lru_done = sem("lru_done", 1)
        h1_ready = sem("h1_ready", 1)
        n1_ready = sem("n1_ready", 1)
        n1_turned = sem("n1_turned", 2)
        n1t_ready = sem("n1t_ready", 2)
        a_stored = sem("a_stored", 32)
        sims_done = sem("sims_done", NT)
        sims_copied = sem("sims_copied", NT)
        soft_in = sem("soft_in", NT)
        soft_exp = sem("soft_exp", NT)
        rows_ready = sem("rows_ready", NT)
        weighed = sem("weighed", NT * HEADS)
        k_turned = sem("k_turned", NT)
        kt_ready = sem("kt_ready", NT)
        v_ready = sem("v_ready", 1)
        c_loaded = sem("c_loaded", 32)
        c_used = sem("c_used", 1)
        q_done = sem("q_done", NT)
        qt_ready = sem("qt_ready", NT)
        s_done = sem("s_done", NT * HEADS)
        max_ready = sem("max_ready", NT * HEADS)
        p_ready = sem("p_ready", NT * HEADS)
        p_turned = sem("p_turned", NT * HEADS)
        pt_ready = sem("pt_ready", NT * HEADS)
        o_done = sem("o_done", NT * HEADS)
        on_ready = sem("on_ready", NT)
        on_turned = sem("on_turned", NT)
        ot_ready = sem("ot_ready", NT)
        ffn_done = sem("ffn_done", 1)
        xh_ready = sem("xh_ready", 1)
        lt_turned = sem("lt_turned", 6)
        lt_ready = sem("lt_ready", 6)
        rot_done = sem("rot_done", 1)
        oneh_ready = sem("oneh_ready", 1)
        pooled = sem("pooled", 1)
        pool_ready = sem("pool_ready", 1)
        rp_turned = sem("rp_turned", 1)
        rpt_ready = sem("rpt_ready", 2)
        kvl_done = sem("kvl_done", 1)
        kbd_ready = sem("kbd_ready", 1)
        lq_done = sem("lq_done", 1)
        lqt_ready = sem("lqt_ready", 1)
        logit_done = sem("logit_done", NT)
        lmax_ready = sem("lmax_ready", NT)
        lexp_ready = sem("lexp_ready", NT)
        lp_turned = sem("lp_turned", NT)
        lpt_ready = sem("lpt_ready", NT)
        lo_done = sem("lo_done", NT)
        y2_ready = sem("y2_ready", 1)
        fc1_done = sem("fc1_done", 2)
        hid_ready = sem("hid_ready", 2)
        fc2_done = sem("fc2_done", 1)
        n3_ready = sem("n3_ready", 1)
        gate_done = sem("gate_done", 1)
        gsoft_in = sem("gsoft_in", 1)
        gsoft_out = sem("gsoft_out", 1)
        e_hid = sem("e_hid", EXPERTS)
        e_relu = sem("e_relu", EXPERTS)
        e_out = sem("e_out", EXPERTS)
        coef_ready = sem("coef_ready", 1)
        coef_turned = sem("coef_turned", 2)
        coeft_ready = sem("coeft_ready", 2)
        eb_out = sem("eb_out", 1)
        e_used = sem("e_used", EXPERTS)
        out_ready = sem("out_ready", 1)
        out_stored = sem("out_stored", 32)
        std = [sem("std0", 1), sem("std1", 1), sem("std2", 5)]
        root = [sem("root0", 1), sem("root1", 1), sem("root2", 5)]
        vec_a, vec_t = sem("vec_a", STEPS["vec_a"]), sem("vec_t", STEPS["vec_t"])
        vec_c = sem("vec_c", STEPS["vec_c"])
        gathered = [sem(f"gathered{i}") for i in range(RING)]
        ring_free = [sem(f"ring_free{i}") for i in range(RING)]
        w_loaded = sem("w_loaded")
        set_vec, set_act, set_pe, set_pool = sem("set_vec"), sem("set_act"), sem("set_pe"), sem("set_pool")
        gate_pe, gate_pool, gate_vec = sem("gate_pe"), sem("gate_pool"), sem("gate_vec")

        def at(s, b, n):
            return b * rises[s.name] + n

        def after(s, b):
            return at(s, b, rises[s.name])

        def apart(e, count, b):
            if not isinstance(b, int):
                e.sem_inc(count, 1)

        block = ctx.enter_context(nc.Block())

        def is_first(b):
            return isinstance(b, int) and b == 0

        ATT_BEATS = ({0: 0, 4: 1}, {0: 2, 3: 3, 6: 4}, {1: 5, 4: 6, 6: 7},
                     {0: 0, 2: 1, 4: 2, 6: 3}, {0: 4, 2: 5, 4: 6, 6: 7}, {0: 0, 2: 1, 4: 2, 6: 3})

        def beat_at(beat, i, h):
            if h in ATT_BEATS[i]:
                beat(ATT_BEATS[i][h])

        def pipeline(e, stage_a, topk, weigh, kv_final, rest):
            def turn_of(i, ahead=True, gather=True, behind=True):
                for t in range(NT):
                    def pick(k):
                        if gather and k < PICKS:
                            if t < NT - 1:
                                topk(i, t + 1, k)
                            elif ahead:
                                topk(i + 1, 0, k)

                    def total(h):
                        if gather:
                            weigh(i, t, h)

                    def beat(k):
                        pick(k)
                        total(k)

                    if t == NT - 2:
                        pick(0)
                        if behind:
                            rest(i - 1, t, beat)
                        pick(1)
                        total(0)
                        pick(2)
                        total(1)
                        pick(3)
                        pick(4)
                        total(2)
                        pick(5)
                        total(3)
                        if ahead:
                            stage_a(i + 1, total)
                        else:
                            for h in range(4, HEADS):
                                total(h)
                    elif behind:
                        rest(i - 1, t, beat)
                    else:
                        for k in range(HEADS):
                            beat(k)
                if gather:
                    kv_final(i)

            stage_a(0, lambda h: None)
            for k in range(PICKS):
                topk(0, 0, k)
            turn_of(0, ahead=B > 1, behind=False)
            if B > 2:
                with e.Fori(1, B - 1) as i:
                    turn_of(i)
            if B > 1:
                turn_of(B - 1, ahead=False)
            turn_of(B, ahead=False, gather=False)

        weights = [
            (filt_c[:, :], filt),
            (wc[:, :, :], w_k.rearrange("(f d) k -> d f k", d=D_IN)),
            (bk_row[:, :], b_k), (wi_aug[0:C, :], wi_t), (wi_aug[C:C + 1, :], bi),
            (wo_g[:, :, :], wo_t.rearrange("(r n) c -> n r c", n=NST)), (bo_row[:, :], bo),
            (logs[:, :], lru_log), (wq_s[:, :], wq),
            (wo_f[:, :, :], wo_pk.rearrange("(g p) c -> p g c", p=P)),
            (ring[0:32, 0, 0:8, :].rearrange("p a b -> p (a b)"), wqpk_t.rearrange("g d c -> d g c")),
            (ring[0:32, 0, 8:16, :].rearrange("p a b -> p (a b)"), keys_t.rearrange("g d k -> d g k")),
            (n1gb[:, 0, :], n1g.to_broadcast([P, C])), (n1gb[:, 1, :], n1b.to_broadcast([P, C])),
            (n2gb[:, 0, :], n2g.to_broadcast([P, C])), (n2gb[:, 1, :], n2b.to_broadcast([P, C])),
            (ngb[:, 0, :], gamma.to_broadcast([P, C])), (ngb[:, 1, :], beta.to_broadcast([P, C])),
            (rot_s[:, :], rot), (qw_s[:, :], q_w), (kvw_s[:, :], kv_w), (fc1_s[:, :], fc1_w),
            (fc1b_c[:, :], fc1_b),
            (fc2_s[:, :, :], fc2_w.rearrange("(g p) c -> p g c", p=P)), (fc2b_row[:, :], fc2_b),
            (gate_aug[0:C, :], gate_w), (gate_aug[C:C + 1, :], gate_b),
            (w1_aug[0:C, :, :], w1.rearrange("e h f -> h e f")), (w1_aug[C:C + 1, :, :], b1),
            (w2_s[:, :, :], w2.rearrange("e f h -> f e h")), (b2_row[:, :], b2),
        ]
        ALL_W = 16 * len(weights)

        @block.sync
        def _(sp):
            for dst, src in weights:
                sp.dma_start(dst, src).then_inc(w_loaded, 16)
            sp.wait_ge(set_vec, SET_ZEROED)

            def load_x(b):
                sp.dma_start(xrow[:, 0:NT - 1, :], x[bass.ds(b, 1), 0:(NT - 1) * P, :].rearrange(
                    "o (t p) d -> p (o t) d", p=P)).then_inc(x_loaded, 16)
                sp.dma_start(xrow[0:XTAIL, NT - 1, :], x[bass.ds(b, 1), (NT - 1) * P:L, :].rearrange(
                    "o p d -> (o p) d")).then_inc(x_loaded, 16)

            def load_a(b):
                if not is_first(b):
                    sp.wait_ge(x_turned, after(x_turned, b - 1))
                load_x(b)

            def store_a(b):
                sp.wait_ge(h1_ready, after(h1_ready, b))
                sp.dma_start(h1_dram[bass.ds(b, 1), :, :, :].rearrange("o p t c -> (o p) t c"),
                             h1a[:, :, :]).then_inc(a_stored, 16)
                sp.wait_ge(n1t_ready, after(n1t_ready, b))
                sp.dma_start(n1t_dram[bass.ds(b, 1), :, :].rearrange("o c n -> (o c) n"),
                             n1t[:, :]).then_inc(a_stored, 16)

            def load_c(b):
                sp.wait_ge(a_stored, after(a_stored, b))
                if not is_first(b):
                    sp.wait_ge(c_used, after(c_used, b - 1))
                sp.dma_start(h1c[:, :, :], h1_dram[bass.ds(b, 1), :, :, :].rearrange("o p t c -> (o p) t c")
                             ).then_inc(c_loaded, 16)
                sp.dma_start(n1tc[0:C, :], n1t_dram[bass.ds(b, 1), :, :].rearrange("o c n -> (o c) n")
                             ).then_inc(c_loaded, 16)

            def store_out(b):
                sp.wait_ge(out_ready, after(out_ready, b))
                sp.dma_start(out[bass.ds(b, 1), 0:(NT - 1) * P, :].rearrange("o (t p) c -> p (o t) c", p=P),
                             outb[:, 0:NT - 1, :]).then_inc(out_stored, 16)
                sp.dma_start(out[bass.ds(b, 1), (NT - 1) * P:N, :].rearrange("o p c -> (o p) c"),
                             outb[0:TAIL, NT - 1, :]).then_inc(out_stored, 16)

            def turn_of(i, ahead=True, behind=True):
                if ahead:
                    load_a(i + 1)
                if behind:
                    load_c(i - 1)
                if ahead:
                    store_a(i + 1)
                if behind:
                    store_out(i - 1)

            load_a(0)
            store_a(0)
            turn_of(0, ahead=B > 1, behind=False)
            if B > 2:
                with sp.Fori(1, B - 1) as i:
                    turn_of(i)
            if B > 1:
                turn_of(B - 1, ahead=False)
            turn_of(B, ahead=False)
            sp.wait_ge(out_stored, after(out_stored, B - 1))
            sp.wait_ge(a_stored, after(a_stored, B - 1))

        @block.gpsimd
        def _(pool):
            g = nc.gpsimd
            n = [0]

            def one(ins):
                ins.then_inc(set_pool, 1)
                n[0] += 1

            one(g.memset(ident[:, :], 1.0))
            one(g.memset(causal[:, :], 0.0))
            one(g.memset(head_mask[:, :], 1.0))
            one(g.memset(v_mask[:, :, :], 1.0))
            one(g.memset(valid[:, :], 1.0))
            one(g.iota(cos_t[:, :], pattern=[[1, NP_]], base=0, channel_multiplier=0,
                       allow_small_or_imprecise_dtypes=True))
            one(g.iota(iota_c[:, :], pattern=[[int(SPREAD), NCAND]], base=0, channel_multiplier=0,
                       allow_small_or_imprecise_dtypes=True))
            one(g.iota(iota_e[:, :], pattern=[[1, EXPERTS]], base=0, channel_multiplier=0,
                       allow_small_or_imprecise_dtypes=True))
            one(g.iota(rank8[:, :], pattern=[[-1, BUCKETS]], base=BUCKETS, channel_multiplier=0,
                       allow_small_or_imprecise_dtypes=True))
            one(g.iota(head_base[:, :], pattern=[[NKEY * NKEY, HEADS]], base=0, channel_multiplier=0,
                       allow_small_or_imprecise_dtypes=True))
            pool.wait_ge(set_pool, n[0])
            one(g.affine_select(out=ident[:, :], in_=ident[:, :], compare_op=ALU.is_equal, fill=0.0, base=0,
                                pattern=[[-1, P]], channel_multiplier=1))
            one(g.affine_select(out=causal[:, :], in_=causal[:, :], compare_op=ALU.is_ge, fill=NEG, base=0,
                                pattern=[[-1, P]], channel_multiplier=1))
            one(g.affine_select(out=head_mask[:, :], in_=head_mask[:, :], compare_op=ALU.is_ge, fill=0.0, base=0,
                                pattern=[[-DH_LSH, HEADS]], channel_multiplier=1))
            one(g.affine_select(out=v_mask[:, :, :].rearrange("p g (h d) -> p g h d", d=DH_LSH),
                                in_=v_mask[:, :, :].rearrange("p g (h d) -> p g h d", d=DH_LSH),
                                compare_op=ALU.is_ge, fill=0.0, base=0,
                                pattern=[[P, 2], [-M_LSH, HEADS], [0, DH_LSH]], channel_multiplier=1))
            one(g.affine_select(out=valid[:, :], in_=valid[:, :], compare_op=ALU.is_ge, fill=0.0, base=N - 1,
                                pattern=[[-P, NT]], channel_multiplier=-1))
            pool.wait_ge(set_pool, n[0])
            one(g.affine_select(out=head_mask[:, :], in_=head_mask[:, :], compare_op=ALU.is_ge, fill=0.0,
                                base=DH_LSH - 1, pattern=[[DH_LSH, HEADS]], channel_multiplier=-1))
            one(g.affine_select(out=v_mask[:, :, :].rearrange("p g (h d) -> p g h d", d=DH_LSH),
                                in_=v_mask[:, :, :].rearrange("p g (h d) -> p g h d", d=DH_LSH),
                                compare_op=ALU.is_ge, fill=0.0, base=M_LSH - 1,
                                pattern=[[-P, 2], [M_LSH, HEADS], [0, DH_LSH]], channel_multiplier=-1))
            assert n[0] == SET_POOL
            pool.wait_ge(set_pool, SET_POOL)
            pool.wait_ge(set_vec, SET_VEC)

            def body(b):
                for t in range(NT):
                    rows = P if t < NT - 1 else TAIL
                    pool.wait_ge(rows_ready, at(rows_ready, b, t + 1))
                    pool.sem_inc(gate_pool, 1)
                    for h in range(HEADS):
                        use, slot = divmod(t * HEADS + h, RING)
                        pool.wait_ge(ring_free[slot], b * USES + use + 1)
                        pool.sem_inc(gate_pool, 1)
                        for r in range(TOPK):
                            j = h * TOPK + r
                            g.indirect_dma_start(ring[0:rows, slot, r, :], None, kv_rows,
                                                 bass.IndirectOffsetOnAxis(ap=row_i[0:rows, t, j:j + 1], axis=0)
                                                 ).then_inc(gathered[slot], 16)

            body(0)
            if B > 1:
                with pool.Fori(1, B) as b:
                    body(b)

        @block.scalar
        def _(act):
            a = nc.scalar
            act.wait_ge(set_vec, SET_ANGLE)
            a.activation(sin_t[:, :], sin_t[:, :], ACT.Sin, scale=6.2831845).then_inc(set_act, 1)
            a.activation(cos_t[:, :], cos_t[:, :], ACT.Sin, scale=6.2831845).then_inc(set_act, 1)
            act.wait_ge(set_pe, 2)
            a.activation(w_sim[:, :], bank(0, 1024, C), ACT.Copy).then_inc(set_act, 1)

            def copy_turned(turned, copied, dst, rows, b, base=0):
                act.wait_ge(turned, at(turned, b, base + 1))
                a.activation(dst[0:rows, 0:512], bank(0, 512, rows), ACT.Copy).then_inc(copied, 1)
                act.wait_ge(turned, at(turned, b, base + 2))
                a.activation(dst[0:rows, 512:NP_], bank(1, NP_ - 512, rows), ACT.Copy).then_inc(copied, 1)

            def take_root(i, buf, b, n):
                act.wait_ge(std[i], at(std[i], b, n))
                a.activation(buf[:, 2, :], buf[:, 1, :], ACT.Sqrt).then_inc(root[i], 1)

            def stage_a(b, total):
                copy_turned(x_turned, xt_ready, xt, P, b)
                act.wait_ge(conv_done, after(conv_done, b))
                a.activation(h0[:, :, :].rearrange("p t c -> p (t c)"), bank(2, NT * C), ACT.Relu
                             ).then_inc(h0_ready, 1)
                take_root(0, lnv, b, 1)
                copy_turned(z_turned, zt_ready, zt, C, b)
                total(4)
                total(5)
                take_root(1, lnv, b, 1)
                total(6)
                if not is_first(b):
                    act.wait_ge(a_stored, after(a_stored, b - 1))
                copy_turned(n1_turned, n1t_ready, n1t, C, b)
                total(7)

            def topk(b, t, part):
                if part == 0:
                    if t > 0:
                        act.wait_ge(rows_ready, at(rows_ready, b, t))
                    act.wait_ge(sims_done, at(sims_done, b, t + 1))
                    a.activation(trest.rearrange("p g k -> p (g k)"), bank(4, 2 * HEADS * NKEY), ACT.Copy
                                 ).then_inc(sims_copied, 1)
                elif part == 4:
                    act.wait_ge(soft_in, at(soft_in, b, t + 1))
                    a.activation(fe[:, :, :], fe[:, :, :], ACT.Exp).then_inc(soft_exp, 1)

            def weigh(b, t, h):
                act.wait_ge(rows_ready, at(rows_ready, b, t + 1))
                use, slot = divmod(t * HEADS + h, RING)
                act.wait_ge(gathered[slot], (b * USES + use + 1) * 16 * TOPK)
                for k in range(TOPK):
                    last = a.activation(ring[:, slot, k, :], ring[:, slot, k, :], ACT.Copy,
                                        scale=row_w[:, t, h * TOPK + k:h * TOPK + k + 1])
                last.then_inc(weighed, 1)

            def kv_final(b):
                for t in range(NT):
                    act.wait_ge(k_turned, at(k_turned, b, t + 1))
                    a.activation(kt[:, :, t * P:(t + 1) * P],
                                 bank(t % 2, 512).rearrange("p (g n) -> p g n", g=HEADS // 2),
                                 ACT.Copy).then_inc(kt_ready, 1)
                a.activation(v[:, :, :, :].rearrange("p t h c -> p t (h c)"),
                             kv[:, :, 1, :, :].rearrange("p t h c -> p t (h c)"),
                             ACT.Copy).then_inc(v_ready, 1)

            def attention(b, i, beat):
                n = (i + 1) * P
                beat_at(beat, i, 0)
                act.wait_ge(q_done, at(q_done, b, i + 1))
                a.activation(qt[:, :, :].rearrange("p g n -> p (g n)"), bank(0, 512), ACT.Copy,
                             scale=C ** -0.5).then_inc(qt_ready, 1)
                for h in range(HEADS + 1):
                    if h > 0:
                        beat_at(beat, i, h)
                    if h < HEADS:
                        u = i * HEADS + h
                        act.wait_ge(max_ready, at(max_ready, b, u + 1))
                        if u >= 2:
                            act.wait_ge(p_turned, at(p_turned, b, u - 1))
                        a.activation(prob[:, u % 2, 0:n], bank(2 + 2 * (u % 2), n), ACT.Exp,
                                     bias=nmax[:, h:h + 1], accum_out=rsum[:, h:h + 1]
                                     ).then_inc(p_ready, 1)
                    if h > 0:
                        u = i * HEADS + h - 1
                        act.wait_ge(p_turned, at(p_turned, b, u + 1))
                        if u >= 2:
                            act.wait_ge(o_done, at(o_done, b, u - 1))
                        a.activation(probt[:, u % 2, 0:n], bank(0, n), ACT.Copy).then_inc(pt_ready, 1)
                act.wait_ge(on_turned, at(on_turned, b, i + 1))
                a.activation(ot[:, :, :].rearrange("p g n -> p (g n)"), bank(0, 512), ACT.Copy
                             ).then_inc(ot_ready, 1)

            def lsh_a(b, beat):
                beat(4)
                take_root(2, ln2, b, 1)
                take_root(2, ln2, b, 2)
                copy_turned(lt_turned, lt_ready, lt, C, b, 0)
                beat(5)
                beat(6)
                act.wait_ge(rp_turned, after(rp_turned, b))
                a.activation(rpt[:, :], bank(5, M_LSH, C + 1), ACT.Copy).then_inc(rpt_ready, 1)
                a.activation(rpt4[:, :, :], bank(5, M_LSH, C).unsqueeze(1).to_broadcast([C, 4, M_LSH]), ACT.Copy
                             ).then_inc(rpt_ready, 1)
                act.wait_ge(lq_done, after(lq_done, b))
                a.activation(lqt[0:C, :].rearrange("c (g n) -> c g n", g=2),
                             ps[0:C, 1024:2048].rearrange("c (g n) -> c g n", g=2)[:, :, 0:HALF],
                             ACT.Copy, scale=DH_LSH ** -0.5).then_inc(lqt_ready, 1)
                beat(7)

            def lsh_b(b, beat):
                for t in range(NT):
                    beat(t)
                    act.wait_ge(lmax_ready, at(lmax_ready, b, t + 1))
                    a.activation(lp, lp, ACT.Exp).then_inc(lexp_ready, 1)
                    act.wait_ge(lp_turned, at(lp_turned, b, t + 1))
                    a.activation(probt[:, 0, 0:2 * P], bank(0, 2 * P), ACT.Copy).then_inc(lpt_ready, 1)

            def mlp(b, beat):
                take_root(2, ln2, b, 3)
                copy_turned(lt_turned, lt_ready, lt, C, b, 2)
                beat(6)
                for f in range(2):
                    act.wait_ge(fc1_done, at(fc1_done, b, f + 1))
                    a.activation(hidden[:, f, :].rearrange("p (g n) -> p g n", g=2),
                                 ps[:, 1024 * (1 + f):1024 * (2 + f)].rearrange("p (g n) -> p g n", g=2)[:, :, 0:HALF],
                                 ACT.Gelu, bias=fc1b_c[:, f:f + 1]).then_inc(hid_ready, 1)
                beat(7)
                take_root(2, ln2, b, 4)

            def moe_a(b):
                copy_turned(lt_turned, lt_ready, lt, C, b, 4)
                act.wait_ge(gsoft_in, after(gsoft_in, b))
                a.activation(gw[:, 1, :], gw[:, 0, :], ACT.Exp).then_inc(gsoft_out, 1)

            def moe_b(b, beat):
                for e in range(EXPERTS):
                    if e % 2 == 0:
                        beat(e // 2)
                    act.wait_ge(e_hid, at(e_hid, b, e + 1))
                    if e >= 2:
                        act.wait_ge(e_out, at(e_out, b, e - 1))
                    k = 2 + 2 * (e % 2)
                    a.activation(hexp[:, e % 2, :].rearrange("p (g n) -> p g n", g=2),
                                 ps[:, 512 * k:512 * (k + 2)].rearrange("p (g n) -> p g n", g=2)[:, :, 0:HALF],
                                 ACT.Relu).then_inc(e_relu, 1)
                copy_turned(coef_turned, coeft_ready, coeft, EXPERTS, b)
                take_root(2, ln2, b, 5)

            def rest(b, t, beat):
                if t == 0:
                    attention(b, 0, beat)
                    attention(b, 1, beat)
                    attention(b, 2, beat)
                elif t == 1:
                    attention(b, 3, beat)
                    attention(b, 4, beat)
                elif t == 2:
                    attention(b, 5, beat)
                    lsh_a(b, beat)
                elif t == 3:
                    lsh_b(b, beat)
                    mlp(b, beat)
                elif t == 4:
                    moe_a(b)
                elif t == 5:
                    moe_b(b, beat)

            pipeline(act, stage_a, topk, weigh, kv_final, rest)

        @block.tensor
        def _(pe):
            mm = nc.tensor.matmul
            pe.wait_ge(set_pool, SET_POOL)
            pe.wait_ge(w_loaded, ALL_W)
            pe.wait_ge(set_vec, SET_VEC - 1)
            wqb = ring[0:32, 0, 0:8, :].rearrange("p a b -> p (a b)")
            kyb = ring[0:32, 0, 8:16, :].rearrange("p a b -> p (a b)")
            for g in range(2 * HEADS):
                last = mm(ps[0:C, g * C:(g + 1) * C], wqb[:, g * C:(g + 1) * C], kyb[:, g * C:(g + 1) * C],
                          start=True, stop=True)
                if g == HEADS - 1:
                    last.then_inc(set_pe, 1)
            last.then_inc(set_pe, 1)
            pe.wait_ge(set_act, 3)

            def turn(src, rows_out, done):
                for t in range(NT):
                    last = nc.tensor.transpose(bank(t // 4, P, rows_out, (t % 4) * P), src(t), ident[:, :])
                    if t == 3 or t == NT - 1:
                        last.then_inc(done, 1)

            def stage_a(b, total):
                pe.wait_ge(x_loaded, after(x_loaded, b))
                apart(pe, gate_pe, b)
                turn(lambda t: xrow[:, t, :], P, x_turned)
                pe.wait_ge(xt_ready, after(xt_ready, b))
                apart(pe, gate_pe, b)
                for t in range(NT):
                    o = bank(2, C, P, t * C)
                    for f in range(TAPS):
                        mm(o, xt[:, t * P + f:t * P + f + P], wc[:, f, :], start=(f == 0), stop=False)
                    last = mm(o, ones_row[:, :], bk_row[:, :], start=False, stop=True)
                last.then_inc(conv_done, 1)
                pe.wait_ge(z_ready, after(z_ready, b))
                apart(pe, gate_pe, b)
                turn(lambda t: z[:, t, :], C, z_turned)
                pe.wait_ge(zt_ready, after(zt_ready, b))
                apart(pe, gate_pe, b)
                for r in range(2):
                    for c in range(2):
                        last = mm(bank(2 + 2 * r + c, HALF), wi_aug[:, r * NST:(r + 1) * NST],
                                  zt[:, c * HALF:(c + 1) * HALF], start=True, stop=True)
                last.then_inc(u_done, 1)
                pe.wait_ge(y_ready, after(y_ready, b))
                apart(pe, gate_pe, b)
                for t in range(NT):
                    o = bank(2, C, P, t * C)
                    for r in range(2):
                        mm(o, wide[:, r, t * P:(t + 1) * P], wo_g[:, r, :], start=(r == 0), stop=False)
                    last = mm(o, ones_row[:, :], bo_row[:, :], start=False, stop=True)
                last.then_inc(lru_done, 1)
                pe.wait_ge(n1_ready, after(n1_ready, b))
                apart(pe, gate_pe, b)
                turn(lambda t: z[:, t, :], C, n1_turned)
                pe.wait_ge(n1t_ready, after(n1t_ready, b))
                apart(pe, gate_pe, b)

            def topk(b, t, part):
                if part > 0:
                    return
                for p in range(2):
                    last = mm(bank(4 + p, 512), n1t[:, t * P:(t + 1) * P], w_sim[:, p * 512:(p + 1) * 512],
                              start=True, stop=True)
                last.then_inc(sims_done, 1)
                pe.wait_ge(sims_copied, at(sims_copied, b, t + 1))
                apart(pe, gate_pe, b)

            def kv_final(b):
                for t in range(NT):
                    for s in ring_free:
                        pe.wait_ge(s, b * USES + (t + 1) * HEADS // RING + 1)
                    apart(pe, gate_pe, b)
                    if t >= 2:
                        pe.wait_ge(kt_ready, at(kt_ready, b, t - 1))
                        apart(pe, gate_pe, b)
                    for g in range(HEADS // 2):
                        last = nc.tensor.transpose(bank(t % 2, P, P, g * P), kv[:, t, 0, 2 * g:2 * g + 2, :].rearrange("p h c -> p (h c)"),
                                                   ident[:, :])
                    last.then_inc(k_turned, 1)
                pe.wait_ge(kt_ready, after(kt_ready, b))
                apart(pe, gate_pe, b)

            def attention(b, i, beat):
                n = (i + 1) * P
                beat_at(beat, i, 0)
                if i == 0:
                    pe.wait_ge(c_loaded, after(c_loaded, b))
                    apart(pe, gate_pe, b)
                    pe.wait_ge(kt_ready, after(kt_ready, b))
                    apart(pe, gate_pe, b)
                    pe.wait_ge(v_ready, after(v_ready, b))
                    apart(pe, gate_pe, b)
                if i > 0:
                    pe.wait_ge(ot_ready, at(ot_ready, b, i))
                    apart(pe, gate_pe, b)
                for g in range(HEADS // 2):
                    last = mm(bank(0, P, P, g * P), wq_s[:, g * P:(g + 1) * P], n1tc[0:C, i * P:(i + 1) * P],
                              start=True, stop=True)
                last.then_inc(q_done, 1)
                pe.wait_ge(qt_ready, at(qt_ready, b, i + 1))
                apart(pe, gate_pe, b)

                def scores(h):
                    u = i * HEADS + h
                    if u >= 2:
                        pe.wait_ge(p_ready, at(p_ready, b, u - 1))
                        apart(pe, gate_pe, b)
                    r, g, s = C * (h % 2), h // 2, 2 + 2 * (u % 2)
                    for c0 in range(0, n, 512):
                        c1 = min(n, c0 + 512)
                        mm(bank(s, c1 - c0, P, c0), qt[r:r + C, g, :], kt[r:r + C, g, c0:c1],
                           start=True, stop=False, skip_group_check=True)
                    mm(bank(s, P, P, i * P), ident[:, :], causal[:, :], start=False, stop=True,
                       skip_group_check=True).then_inc(s_done, 1)

                def turn_probs(h):
                    u = i * HEADS + h
                    pe.wait_ge(p_ready, at(p_ready, b, u + 1))
                    apart(pe, gate_pe, b)
                    if u >= 1:
                        pe.wait_ge(pt_ready, at(pt_ready, b, u))
                        apart(pe, gate_pe, b)
                    for j in range(i + 1):
                        last = nc.tensor.transpose(bank(0, P, P, j * P), prob[:, u % 2, j * P:(j + 1) * P],
                                                   ident[:, :])
                    last.then_inc(p_turned, 1)

                def values(h):
                    u = i * HEADS + h
                    pe.wait_ge(pt_ready, at(pt_ready, b, u + 1))
                    apart(pe, gate_pe, b)
                    for j in range(i + 1):
                        last = mm(bank(6, C, P, h * C), probt[:, u % 2, j * P:(j + 1) * P], v[:, j, h, :],
                                  start=(j == 0), stop=(j == i))
                    last.then_inc(o_done, 1)

                scores(0)
                if i >= 1:
                    pe.wait_ge(on_ready, at(on_ready, b, i))
                    apart(pe, gate_pe, b)
                for h in range(HEADS):
                    if h + 1 < HEADS:
                        scores(h + 1)
                    turn_probs(h)
                    if h >= 1:
                        values(h - 1)
                values(HEADS - 1)
                pe.wait_ge(on_ready, at(on_ready, b, i + 1))
                apart(pe, gate_pe, b)
                for g in range(HEADS // 2):
                    last = nc.tensor.transpose(bank(0, P, P, g * P), on[:, g * P:(g + 1) * P], ident[:, :])
                last.then_inc(on_turned, 1)
                pe.wait_ge(ot_ready, at(ot_ready, b, i + 1))
                apart(pe, gate_pe, b)
                for g in range(HEADS // 2):
                    last = mm(bank(7, C, P, i * C), ot[:, g, :], wo_f[:, g, :], start=(g == 0),
                              stop=(g == HEADS // 2 - 1))
                if i == NT - 1:
                    last.then_inc(ffn_done, 1)

            def lsh_a(b, beat):
                pe.wait_ge(xh_ready, after(xh_ready, b))
                apart(pe, gate_pe, b)
                turn(lambda t: xh[:, t, 0:C], C, lt_turned)
                pe.wait_ge(lt_ready, at(lt_ready, b, 2))
                apart(pe, gate_pe, b)
                for t in range(NT):
                    last = mm(bank(4, 16, P, t * 16), lt[0:C, t * P:(t + 1) * P], rot_s[:, :], start=True, stop=True)
                last.then_inc(rot_done, 1)
                pe.wait_ge(oneh_ready, after(oneh_ready, b))
                apart(pe, gate_pe, b)
                for t in range(NT):
                    last = mm(bank(5, C + 1, M_LSH), oneh[:, t, :, :].rearrange("p i j -> p (i j)"), xh[:, t, :],
                              start=(t == 0), stop=(t == NT - 1))
                last.then_inc(pooled, 1)
                for c in range(2):
                    last = mm(bank(2 + c, HALF, C), qw_s[:, :], lt[0:C, c * HALF:(c + 1) * HALF],
                              start=True, stop=True)
                last.then_inc(lq_done, 1)
                pe.wait_ge(pool_ready, after(pool_ready, b))
                apart(pe, gate_pe, b)
                nc.tensor.transpose(bank(5, M_LSH, C + 1), pool_s[:, :], ident[0:M_LSH, 0:M_LSH]
                                    ).then_inc(rp_turned, 1)
                pe.wait_ge(rpt_ready, after(rpt_ready, b))
                apart(pe, gate_pe, b)
                mm(bank(5, M_LSH, C), kvw_s[:, 0:C], rpt[0:C, :], start=True, stop=True)
                mm(bank(6, C), rpt4[:, :, :].rearrange("c a m -> c (a m)"), kvw_s[:, C:2 * C],
                   start=True, stop=True).then_inc(kvl_done, 1)
                pe.wait_ge(kbd_ready, after(kbd_ready, b))
                apart(pe, gate_pe, b)
                pe.wait_ge(lqt_ready, after(lqt_ready, b))
                apart(pe, gate_pe, b)

            def lsh_b(b, beat):
                def logits(t):
                    if t >= 2:
                        pe.wait_ge(lmax_ready, at(lmax_ready, b, t - 1))
                        apart(pe, gate_pe, b)
                    mm(bank(4 + t % 2, HEADS * M_LSH), lqt[:, t * P:(t + 1) * P],
                       kbd[:, :, :].rearrange("c h m -> c (h m)"), start=True, stop=True
                       ).then_inc(logit_done, 1)

                beat(0)
                logits(0)
                for t in range(NT):
                    if t + 1 < NT:
                        logits(t + 1)
                    pe.wait_ge(lexp_ready, at(lexp_ready, b, t + 1))
                    apart(pe, gate_pe, b)
                    for g in range(2):
                        last = nc.tensor.transpose(bank(0, P, P, g * P), prob[:, 0, g * P:(g + 1) * P], ident[:, :])
                    last.then_inc(lp_turned, 1)
                    pe.wait_ge(lpt_ready, at(lpt_ready, b, t + 1))
                    apart(pe, gate_pe, b)
                    for g in range(2):
                        last = mm(bank(6, C, P, t * C), lpt[:, g, :], vbd[:, g, :], start=(g == 0), stop=(g == 1))
                    last.then_inc(lo_done, 1)

            def mlp(b, beat):
                pe.wait_ge(y2_ready, after(y2_ready, b))
                apart(pe, gate_pe, b)
                turn(lambda t: tmp[:, t, :], C, lt_turned)
                pe.wait_ge(lt_ready, at(lt_ready, b, 4))
                apart(pe, gate_pe, b)
                for f in range(2):
                    for c in range(2):
                        last = mm(bank(2 + 2 * f + c, HALF), fc1_s[:, f * P:(f + 1) * P],
                                  lt[0:C, c * HALF:(c + 1) * HALF], start=True, stop=True)
                    last.then_inc(fc1_done, 1)
                pe.wait_ge(hid_ready, after(hid_ready, b))
                apart(pe, gate_pe, b)
                for t in range(NT):
                    for f in range(2):
                        mm(bank(6, C, P, t * C), hidden[:, f, t * P:(t + 1) * P], fc2_s[:, f, :],
                           start=(f == 0), stop=False)
                    last = mm(bank(6, C, P, t * C), ones_row[:, :], fc2b_row[:, :], start=False, stop=True)
                last.then_inc(fc2_done, 1)

            def moe_a(b):
                pe.wait_ge(n3_ready, after(n3_ready, b))
                apart(pe, gate_pe, b)
                turn(lambda t: n2[:, t, :], C, lt_turned)
                pe.wait_ge(lt_ready, at(lt_ready, b, 6))
                apart(pe, gate_pe, b)
                for t in range(NT):
                    last = mm(bank(7, EXPERTS, P, t * EXPERTS), lt[:, t * P:(t + 1) * P], gate_aug[:, :],
                              start=True, stop=True)
                last.then_inc(gate_done, 1)

            def moe_b(b, beat):
                def expert_in(e):
                    if e >= 2:
                        pe.wait_ge(e_relu, at(e_relu, b, e - 1))
                        apart(pe, gate_pe, b)
                    for c in range(2):
                        last = mm(bank(2 + 2 * (e % 2) + c, HALF), w1_aug[:, e, :],
                                  lt[:, c * HALF:(c + 1) * HALF], start=True, stop=True)
                    last.then_inc(e_hid, 1)

                beat(0)
                expert_in(0)
                for e in range(EXPERTS):
                    if e + 1 < EXPERTS:
                        expert_in(e + 1)
                    pe.wait_ge(e_relu, at(e_relu, b, e + 1))
                    apart(pe, gate_pe, b)
                    if e == 1:
                        pe.wait_ge(gsoft_in, after(gsoft_in, b))
                        apart(pe, gate_pe, b)
                    if e >= 2:
                        pe.wait_ge(e_used, at(e_used, b, e - 1))
                        apart(pe, gate_pe, b)
                    for t in range(NT):
                        last = mm(bank(6 + e % 2, C, P, t * C), hexp[:, e % 2, t * P:(t + 1) * P], w2_s[:, e, :],
                                  start=True, stop=True)
                    last.then_inc(e_out, 1)
                pe.wait_ge(coef_ready, after(coef_ready, b))
                apart(pe, gate_pe, b)
                for t in range(NT):
                    last = nc.tensor.transpose(bank(t // 4, P, EXPERTS, (t % 4) * P), coef[:, t, :], ident[:, :])
                    if t == 3 or t == NT - 1:
                        last.then_inc(coef_turned, 1)
                pe.wait_ge(coeft_ready, after(coeft_ready, b))
                apart(pe, gate_pe, b)
                pe.wait_ge(e_used, at(e_used, b, EXPERTS - 1))
                apart(pe, gate_pe, b)
                for t in range(NT):
                    last = mm(bank(6, C, P, t * C), coeft[:, t * P:(t + 1) * P], b2_row[:, :], start=True, stop=True)
                last.then_inc(eb_out, 1)

            def rest(b, t, beat):
                if t == 0:
                    attention(b, 0, beat)
                    attention(b, 1, beat)
                    attention(b, 2, beat)
                elif t == 1:
                    attention(b, 3, beat)
                    attention(b, 4, beat)
                elif t == 2:
                    attention(b, 5, beat)
                    lsh_a(b, beat)
                elif t == 3:
                    lsh_b(b, beat)
                    mlp(b, beat)
                elif t == 4:
                    moe_a(b)
                elif t == 5:
                    moe_b(b, beat)

            pipeline(pe, stage_a, topk, lambda i, t, half: None, kv_final, rest)

        @block.vector
        def _(dve):
            vv = nc.vector
            TT, TS, STT = vv.tensor_tensor, vv.tensor_scalar, vv.scalar_tensor_tensor
            zeroed = [0]

            def first(ins):
                ins.then_inc(set_vec, 1)
                zeroed[0] += 1

            first(vv.memset(xrow[:, :, :], 0.0))
            assert zeroed[0] == SET_ZEROED
            first(vv.memset(xt[:, :], 0.0))
            first(vv.memset(ones_row[:, :], 1.0))
            first(vv.memset(zt[C:C + 1, :], 1.0))
            first(vv.memset(lt[C:C + 1, :], 1.0))
            first(vv.memset(xh[:, :, C:C + 1], 1.0))
            first(vv.memset(ring[:, 1:RING, :, :], 0.0))
            dve.wait_ge(w_loaded, ALL_W)
            dve.wait_ge(set_pool, SET_POOL)

            def exact_exp(dst, src, a, n, r, p, whole):
                first(TS(n, src, 1.0 / math.log(2.0), ROUND, ALU.mult, ALU.add))
                dve.wait_ge(set_vec, zeroed[0])
                first(TS(n, n, -ROUND, None, ALU.add))
                dve.wait_ge(set_vec, zeroed[0])
                first(STT(out=r, in0=n, scalar=-0.693359375, in1=src, op0=ALU.mult, op1=ALU.add))
                dve.wait_ge(set_vec, zeroed[0])
                first(STT(out=r, in0=n, scalar=2.12194440e-4, in1=r, op0=ALU.mult, op1=ALU.add))
                dve.wait_ge(set_vec, zeroed[0])
                first(TS(p, r, 1.0 / math.factorial(8), 1.0 / math.factorial(7), ALU.mult, ALU.add))
                for k in range(6, -1, -1):
                    dve.wait_ge(set_vec, zeroed[0])
                    first(TT(p, p, r, ALU.mult))
                    dve.wait_ge(set_vec, zeroed[0])
                    first(TS(p, p, 1.0 / math.factorial(k), None, ALU.add))
                first(TS(n, n, 127.0, 8388608.0, ALU.add, ALU.mult))
                dve.wait_ge(set_vec, zeroed[0])
                first(vv.tensor_copy(whole, n))
                dve.wait_ge(set_vec, zeroed[0])
                first(TT(dst, p, whole.bitcast(F32), ALU.mult))
                dve.wait_ge(set_vec, zeroed[0])

            exact_exp(lam[:, 0:3], logs[:, :], None, small[:, 0:3], small[:, 3:6], small[:, 6:9], small_i[:, 0:3])
            first(TS(small[:, 9:10], lam[:, 0:1], -1.0, None, ALU.mult))
            dve.wait_ge(set_vec, zeroed[0])
            exact_exp(lam[:, 3:4], small[:, 9:10], None, small[:, 0:1], small[:, 3:4], small[:, 6:7],
                      small_i[:, 0:1])
            hi, lo = small[:, 10:11], small[:, 11:12]
            HI_ROUND = 1.5 * 2.0 ** 11
            first(TS(hi, lam[:, 1:2], 1.0 / TWO_PI, HI_ROUND, ALU.mult, ALU.add))
            dve.wait_ge(set_vec, zeroed[0])
            first(TS(hi, hi, -HI_ROUND, None, ALU.add))
            dve.wait_ge(set_vec, zeroed[0])
            first(STT(out=lo, in0=hi, scalar=-6.28125, in1=lam[:, 1:2], op0=ALU.mult, op1=ALU.add))
            dve.wait_ge(set_vec, zeroed[0])
            first(STT(out=lo, in0=hi, scalar=-(TWO_PI - 6.28125), in1=lo, op0=ALU.mult, op1=ALU.add))
            dve.wait_ge(set_vec, zeroed[0])
            first(TS(lo, lo, 1.0 / TWO_PI, None, ALU.mult))
            dve.wait_ge(set_vec, zeroed[0])

            def to_turn(dst, scratch):
                first(TS(scratch, dst, ROUND, None, ALU.add))
                dve.wait_ge(set_vec, zeroed[0])
                first(TS(scratch, scratch, -ROUND, None, ALU.add))
                dve.wait_ge(set_vec, zeroed[0])
                first(TT(dst, dst, scratch, ALU.subtract))
                dve.wait_ge(set_vec, zeroed[0])

            w0, w1_, w2_ = wide[:, 0, :], wide[:, 1, :], wide[:, 2, :]
            first(TS(w0, cos_t[:, :], hi, None, ALU.mult))
            dve.wait_ge(set_vec, zeroed[0])
            to_turn(w0, w2_)
            first(STT(out=sin_t[:, :], in0=cos_t[:, :], scalar=lo, in1=w0, op0=ALU.mult, op1=ALU.add))
            dve.wait_ge(set_vec, zeroed[0])
            to_turn(sin_t[:, :], w2_)
            first(TS(cos_t[:, :], sin_t[:, :], 0.25, None, ALU.add))
            dve.wait_ge(set_vec, zeroed[0])
            to_turn(cos_t[:, :], w2_)
            assert zeroed[0] == SET_ANGLE, zeroed[0]
            first(TT(wc[:, :, :], wc[:, :, :], filt_c[:, :].unsqueeze(2).to_broadcast([P, TAPS, C]), ALU.mult))
            first(TS(wo_g[:, :, :], wo_g[:, :, :], lam[:, 2:3], None, ALU.mult))
            assert zeroed[0] == SET_VEC - 1, zeroed[0]
            dve.wait_ge(set_pe, 2)
            first(vv.memset(ring[:, 0, :, :], 0.0))
            dve.wait_ge(set_act, 2)
            for s in ring_free:
                dve.sem_inc(s, 1)

            va = Steps(vec_a, STEPS["vec_a"])
            vt = Steps(vec_t, STEPS["vec_t"])
            vc = Steps(vec_c, STEPS["vec_c"])

            def norm(st, x_in, xo, sq, buf, i, n, b):
                vv.tensor_reduce(buf[:, 0, :], x_in, AX.X, ALU.add).then_inc(st.sem, st.up())
                dve.wait_ge(st.sem, st.now())
                TS(buf[:, 0, :], buf[:, 0, :], -1.0 / C, None, ALU.mult).then_inc(st.sem, st.up())
                dve.wait_ge(st.sem, st.now())
                TT(xo, x_in, buf[:, 0, :].unsqueeze(2).to_broadcast([P, NT, C]), ALU.add).then_inc(st.sem, st.up())
                dve.wait_ge(st.sem, st.now())
                TT(sq, xo, xo, ALU.mult).then_inc(st.sem, st.up())
                dve.wait_ge(st.sem, st.now())
                vv.tensor_reduce(buf[:, 1, :], sq, AX.X, ALU.add).then_inc(st.sem, st.up())
                dve.wait_ge(st.sem, st.now())
                TS(buf[:, 1, :], buf[:, 1, :], 1.0 / C, EPS, ALU.mult, ALU.add).then_inc(std[i], 1)
                dve.wait_ge(root[i], at(root[i], b, n))
                vv.reciprocal(buf[:, 3, :], buf[:, 2, :]).then_inc(st.sem, st.up())
                dve.wait_ge(st.sem, st.now())
                return TT(xo, xo, buf[:, 3, :].unsqueeze(2).to_broadcast([P, NT, C]), ALU.mult)

            def stage_a(b, total):
                va.begin(b)
                sq = wide[:, 5, 0:NT * C].rearrange("p (t c) -> p t c", c=C)
                dve.wait_ge(h0_ready, after(h0_ready, b))
                norm(va, h0[:, :, :], z[:, :, :], sq, lnv, 0, 1, b).then_inc(z_ready, 1)
                total(4)
                dve.wait_ge(u_done, after(u_done, b))
                halves = lambda x: x.rearrange("p (g n) -> p g n", g=2)
                ur = halves(ps[:, 1024:2048])[:, :, 0:HALF]
                ui = halves(ps[:, 2048:3072])[:, :, 0:HALF]
                cos_h, sin_h = halves(cos_t[:, :]), halves(sin_t[:, :])
                w = [wide[:, k, :] for k in range(6)]
                TT(halves(w[2]), ur, cos_h, ALU.mult).then_inc(vec_a, va.up())
                TT(halves(w[3]), ui, sin_h, ALU.mult).then_inc(vec_a, va.up())
                TT(halves(w[4]), ui, cos_h, ALU.mult).then_inc(vec_a, va.up())
                TT(halves(w[5]), ur, sin_h, ALU.mult).then_inc(vec_a, va.up())
                dve.wait_ge(vec_a, va.now())
                TT(w[2], w[2], w[3], ALU.add).then_inc(vec_a, va.up())
                TT(w[4], w[4], w[5], ALU.subtract).then_inc(vec_a, va.up())
                dve.wait_ge(vec_a, va.now())
                decay = lam[:, 3:4].to_broadcast([P, NP_])
                vv.tensor_tensor_scan(w[3], decay, w[2], 0.0, ALU.mult, ALU.add).then_inc(vec_a, va.up())
                vv.tensor_tensor_scan(w[5], decay, w[4], 0.0, ALU.mult, ALU.add).then_inc(vec_a, va.up())
                dve.wait_ge(vec_a, va.now())
                TT(w[0], w[3], cos_t[:, :], ALU.mult).then_inc(vec_a, va.up())
                TT(w[2], w[5], sin_t[:, :], ALU.mult).then_inc(vec_a, va.up())
                TT(w[1], w[3], sin_t[:, :], ALU.mult).then_inc(vec_a, va.up())
                TT(w[4], w[5], cos_t[:, :], ALU.mult).then_inc(vec_a, va.up())
                dve.wait_ge(vec_a, va.now())
                TT(w[0], w[0], w[2], ALU.subtract).then_inc(vec_a, va.up())
                TT(w[1], w[1], w[4], ALU.add).then_inc(y_ready, 1)
                total(5)
                dve.wait_ge(lru_done, after(lru_done, b))
                if not is_first(b):
                    dve.wait_ge(a_stored, after(a_stored, b - 1))
                TT(h1a[:, :, :], h0[:, :, :], bank(2, NT * C).rearrange("p (t c) -> p t c", c=C),
                   ALU.add).then_inc(h1_ready, 1)
                dve.wait_ge(h1_ready, after(h1_ready, b))
                norm(va, h1a[:, :, :], z[:, :, :], sq, lnv, 1, 1, b).then_inc(n1_ready, 1)
                total(6)
                total(7)
                va.end()

            def top_keys(b, t):
                vt.begin(b, t * (STEPS["vec_t"] // NT))
                dve.wait_ge(sims_copied, at(sims_copied, b, t + 1))
                apart(dve, gate_vec, b)
                sims = [trest[:, g, :] for g in range(2 * HEADS)]
                for g in range(2 * HEADS):
                    vv.max(tv[:, g, 0:8], sims[g]).then_inc(vec_t, vt.up())
                dve.wait_ge(vec_t, vt.now())
                apart(dve, gate_vec, b)
                for g in range(2 * HEADS):
                    vv.max_index(ti[:, g, 0:8], tv[:, g, 0:8], sims[g]).then_inc(vec_t, vt.up())
                dve.wait_ge(vec_t, vt.now())
                apart(dve, gate_vec, b)
                for g in range(2 * HEADS):
                    vv.match_replace(trest[:, g, :], tv[:, g, 0:8], sims[g], LOWEST).then_inc(vec_t, vt.up())

            def next_keys(b, t):
                dve.wait_ge(vec_t, vt.now())
                apart(dve, gate_vec, b)
                for g in range(2 * HEADS):
                    vv.max(tv[:, g, 8:16], trest[:, g, :]).then_inc(vec_t, vt.up())
                dve.wait_ge(vec_t, vt.now())
                apart(dve, gate_vec, b)
                for g in range(2 * HEADS):
                    vv.max_index(ti[:, g, 8:16], tv[:, g, 8:16], trest[:, g, :]).then_inc(vec_t, vt.up())
                dve.wait_ge(vec_t, vt.now())
                vv.tensor_copy(tif[:, :, :], ti[:, :, :]).then_inc(vec_t, vt.up())
                dve.wait_ge(vec_t, vt.now())
                TS(tif[:, HEADS:2 * HEADS, :], tif[:, HEADS:2 * HEADS, :], float(NKEY), None,
                   ALU.mult).then_inc(vec_t, vt.up())
                dve.wait_ge(vec_t, vt.now())
                for dst, src in ((cs, tv), (ci, tif)):
                    for a0, na, ln in CAND_RUNS:
                        off = CAND_OFF[a0]
                        TT(dst[:, :, off:off + na * ln].rearrange("p h (a l) -> p h a l", l=ln),
                                   src[:, 0:HEADS, a0:a0 + na].unsqueeze(3).to_broadcast([P, HEADS, na, ln]),
                                   src[:, HEADS:2 * HEADS, 0:ln].unsqueeze(2).to_broadcast([P, HEADS, na, ln]),
                                   ALU.add).then_inc(vec_t, vt.up())

            def top_pairs(b, t):
                dve.wait_ge(vec_t, vt.now())
                apart(dve, gate_vec, b)
                for h in range(HEADS):
                    vv.max(fs[:, h, 0:8], cs[:, h, :]).then_inc(vec_t, vt.up())
                dve.wait_ge(vec_t, vt.now())
                apart(dve, gate_vec, b)
                for h in range(HEADS):
                    vv.max_index(fp[:, h, 0:8], fs[:, h, 0:8], cs[:, h, :]).then_inc(vec_t, vt.up())
                for h in range(HEADS):
                    vv.match_replace(cs2[:, h, :], fs[:, h, 0:8], cs[:, h, :], LOWEST).then_inc(vec_t, vt.up())
                dve.wait_ge(vec_t, vt.now())
                apart(dve, gate_vec, b)
                for h in range(HEADS):
                    vv.max(fs[:, h, 8:16], cs2[:, h, :]).then_inc(vec_t, vt.up())
                dve.wait_ge(vec_t, vt.now())
                apart(dve, gate_vec, b)
                for h in range(HEADS):
                    vv.max_index(fp[:, h, 8:16], fs[:, h, 8:16], cs2[:, h, :]).then_inc(vec_t, vt.up())
                TT(fe[:, :, :], fs[:, :, :], fs[:, :, 0:1].to_broadcast([P, HEADS, TOPK]),
                   ALU.subtract).then_inc(soft_in, 1)
                dve.wait_ge(soft_in, at(soft_in, b, t + 1))
                vv.tensor_copy(fpf[:, :, :], fp[:, :, :]).then_inc(vec_t, vt.up())
                dve.wait_ge(vec_t, vt.now())
                TS(fpf[:, :, :], fpf[:, :, :], SPREAD, None, ALU.mult).then_inc(vec_t, vt.up())
                TT(ci[:, :, :], ci[:, :, :], iota_c[:, :].unsqueeze(1).to_broadcast([P, HEADS, NCAND]),
                   ALU.add).then_inc(vec_t, vt.up())
                dve.wait_ge(vec_t, vt.now())

            def row_numbers(k):
                HH = HEADS // 2
                oh = onehot.rearrange("p (h r c) -> p h r c", h=HH, c=NCAND)
                hs = slice(k * HH, (k + 1) * HH)
                TT(oh, fpf[:, hs, :].unsqueeze(3).to_broadcast([P, HH, TOPK, NCAND]),
                   ci[:, hs, :].unsqueeze(2).to_broadcast([P, HH, TOPK, NCAND]),
                   ALU.subtract).then_inc(vec_t, vt.up())
                dve.wait_ge(vec_t, vt.now())
                vv.tensor_reduce(fpf[:, hs, :], oh, AX.X, ALU.min, apply_absolute_value=True
                                 ).then_inc(vec_t, vt.up())
                dve.wait_ge(vec_t, vt.now())

            def rows_out(b, t):
                TT(fpf[:, :, :], fpf[:, :, :], head_base[:, :].unsqueeze(2).to_broadcast([P, HEADS, TOPK]),
                   ALU.add).then_inc(vec_t, vt.up())
                dve.wait_ge(vec_t, vt.now())
                dve.wait_ge(soft_exp, at(soft_exp, b, t + 1))
                vv.tensor_reduce(fsum[:, 0, :], fe[:, :, :], AX.X, ALU.add).then_inc(vec_t, vt.up())
                dve.wait_ge(vec_t, vt.now())
                vv.reciprocal(fsum[:, 1, :], fsum[:, 0, :]).then_inc(vec_t, vt.up())
                dve.wait_ge(vec_t, vt.now())
                TT(row_w[:, t, :].rearrange("p (h r) -> p h r", r=TOPK), fe[:, :, :],
                           fsum[:, 1, :].unsqueeze(2).to_broadcast([P, HEADS, TOPK]), ALU.mult).then_inc(vec_t, vt.up())
                vv.tensor_copy(row_i[:, t, :], fpf[:, :, :].rearrange("p h r -> p (h r)")
                               ).then_inc(rows_ready, 1)
                assert vt.n == (t + 1) * (STEPS["vec_t"] // NT)

            def topk(b, t, part):
                if part == 1:
                    top_keys(b, t)
                elif part == 2:
                    next_keys(b, t)
                elif part == 3:
                    top_pairs(b, t)
                elif part == 4:
                    row_numbers(0)
                elif part == 5:
                    row_numbers(1)
                    rows_out(b, t)

            def weigh(b, t, h):
                if t == 0 and h == 0 and not is_first(b):
                    dve.wait_ge(k_turned, after(k_turned, b - 1))
                    dve.wait_ge(v_ready, after(v_ready, b - 1))
                dve.wait_ge(weighed, at(weighed, b, t * HEADS + h + 1))
                slot = (t * HEADS + h) % RING
                vv.tensor_reduce(kv[:, t, :, h, :], ring[:, slot, :, :].rearrange("p r (k c) -> p k c r", k=2),
                                 AX.X, ALU.add).then_inc(ring_free[slot], 1)

            def attention(b, i, beat):
                n = (i + 1) * P
                if i == 0:
                    vc.begin(b)
                for h in range(HEADS):
                    beat_at(beat, i, h)
                    u = i * HEADS + h
                    dve.wait_ge(s_done, at(s_done, b, u + 1))
                    vv.tensor_reduce(nmax[:, h:h + 1], bank(2 + 2 * (u % 2), n), AX.X, ALU.max, negate=True
                                     ).then_inc(max_ready, 1)
                dve.wait_ge(p_ready, at(p_ready, b, (i + 1) * HEADS))
                vv.reciprocal(rinv[:, :], rsum[:, :]).then_inc(vec_c, vc.up())
                dve.wait_ge(vec_c, vc.now())
                dve.wait_ge(o_done, at(o_done, b, (i + 1) * HEADS))
                if i > 0:
                    dve.wait_ge(on_turned, at(on_turned, b, i))
                TT(on[:, :].rearrange("p (h c) -> p h c", c=C), bank(6, 512).rearrange("p (h c) -> p h c", c=C),
                   rinv[:, :].unsqueeze(2).to_broadcast([P, HEADS, C]), ALU.mult).then_inc(on_ready, 1)

            tiles = lambda x: x.rearrange("p (t c) -> p t c", c=C)

            def lsh_a(b, beat):
                beat(4)
                dve.wait_ge(ffn_done, after(ffn_done, b))
                vv.memset(lqt[C:C + 1, :], 1.0).then_inc(vec_c, vc.up())
                TT(h1c[:, :, :], h1c[:, :, :], tiles(bank(7, NT * C)), ALU.add).then_inc(vec_c, vc.up())
                dve.wait_ge(vec_c, vc.now())
                norm(vc, h1c[:, :, :], n2[:, :, :], sq2[:, :, :], ln2, 2, 1, b).then_inc(vec_c, vc.up())
                dve.wait_ge(vec_c, vc.now())
                norm(vc, n2[:, :, :], xh[:, :, 0:C], sq2[:, :, :], ln2, 2, 2, b).then_inc(vec_c, vc.up())
                dve.wait_ge(vec_c, vc.now())
                TT(xh[:, :, 0:C], xh[:, :, 0:C], n1gb[:, 0:1, :].to_broadcast([P, NT, C]), ALU.mult).then_inc(vec_c, vc.up())
                dve.wait_ge(vec_c, vc.now())
                TT(xh[:, :, 0:C], xh[:, :, 0:C], n1gb[:, 1:2, :].to_broadcast([P, NT, C]), ALU.add
                   ).then_inc(xh_ready, 1)
                beat(5)
                dve.wait_ge(rot_done, after(rot_done, b))
                rp = bank(4, NT * 16).rearrange("p (t i j) -> p t i j", t=NT, j=BUCKETS // 2)
                vv.tensor_copy(rots[:, :, :, 0:4], rp).then_inc(vec_c, vc.up())
                TS(rots[:, :, :, 4:8], rp, -1.0, None, ALU.mult).then_inc(vec_c, vc.up())
                dve.wait_ge(vec_c, vc.now())
                vv.tensor_reduce(rmx[:, :, :], rots[:, :, :, :], AX.X, ALU.max).then_inc(vec_c, vc.up())
                dve.wait_ge(vec_c, vc.now())
                full = [P, NT * HASHES, BUCKETS]
                r3 = rots[:, :, :, :].rearrange("p t i j -> p (t i) j")
                o3 = oneh[:, :, :, :].rearrange("p t i j -> p (t i) j")
                m3 = rmx[:, :, :].rearrange("p t i -> p (t i)").unsqueeze(2).to_broadcast(full)
                k3 = rank8[:, :].unsqueeze(1).to_broadcast(full)
                TT(o3, r3, m3, ALU.is_equal).then_inc(vec_c, vc.up())
                dve.wait_ge(vec_c, vc.now())
                TT(r3, o3, k3, ALU.mult).then_inc(vec_c, vc.up())
                dve.wait_ge(vec_c, vc.now())
                vv.tensor_reduce(rmx[:, :, :], rots[:, :, :, :], AX.X, ALU.max).then_inc(vec_c, vc.up())
                dve.wait_ge(vec_c, vc.now())
                TT(o3, r3, m3, ALU.is_equal).then_inc(vec_c, vc.up())
                dve.wait_ge(vec_c, vc.now())
                TT(oneh[:, NT - 1, :, :], oneh[:, NT - 1, :, :],
                   valid[:, NT - 1:NT].unsqueeze(2).to_broadcast([P, HASHES, BUCKETS]), ALU.mult
                   ).then_inc(oneh_ready, 1)
                beat(6)
                dve.wait_ge(pooled, after(pooled, b))
                cnt = bank(5, 1, M_LSH, C)
                TS(pinv[:, 0:1], cnt, 1e-20, None, ALU.add).then_inc(vec_c, vc.up())
                TS(pool_s[:, C:C + 1], cnt, 1.0, NEG, ALU.is_lt, ALU.mult).then_inc(vec_c, vc.up())
                dve.wait_ge(vec_c, vc.now())
                vv.reciprocal(pinv[:, 1:2], pinv[:, 0:1]).then_inc(vec_c, vc.up())
                dve.wait_ge(vec_c, vc.now())
                TS(pool_s[:, 0:C], bank(5, C, M_LSH), pinv[:, 1:2], None, ALU.mult).then_inc(pool_ready, 1)
                dve.wait_ge(rpt_ready, after(rpt_ready, b))
                vv.tensor_copy(kbd[C:C + 1, :, :],
                                       rpt[C:C + 1, :].unsqueeze(1).to_broadcast([1, HEADS, M_LSH])).then_inc(vec_c, vc.up())
                dve.wait_ge(kvl_done, after(kvl_done, b))
                TT(kbd[0:C, :, :], bank(5, M_LSH, C).unsqueeze(1).to_broadcast([C, HEADS, M_LSH]),
                           head_mask[:, :].unsqueeze(2).to_broadcast([C, HEADS, M_LSH]), ALU.mult).then_inc(vec_c, vc.up())
                TT(vbd[:, :, :], bank(6, C).unsqueeze(1).to_broadcast([P, 2, C]), v_mask[:, :, :], ALU.mult
                   ).then_inc(kbd_ready, 1)
                beat(7)

            def lsh_b(b, beat):
                for t in range(NT):
                    beat(t)
                    dve.wait_ge(logit_done, at(logit_done, b, t + 1))
                    lg = bank(4 + t % 2, HEADS * M_LSH).rearrange("p (h m) -> p h m", m=M_LSH)
                    vv.tensor_reduce(lmx[:, 0, :], lg, AX.X, ALU.max).then_inc(vec_c, vc.up())
                    dve.wait_ge(vec_c, vc.now())
                    if t >= 1:
                        dve.wait_ge(lp_turned, at(lp_turned, b, t))
                    TT(lp, lg, lmx[:, 0, :].unsqueeze(2).to_broadcast([P, HEADS, M_LSH]), ALU.subtract
                       ).then_inc(lmax_ready, 1)
                    dve.wait_ge(lexp_ready, at(lexp_ready, b, t + 1))
                    vv.tensor_reduce(lmx[:, 1, :], lp, AX.X, ALU.add).then_inc(vec_c, vc.up())
                    dve.wait_ge(vec_c, vc.now())
                    vv.reciprocal(lmx[:, 2, :], lmx[:, 1, :]).then_inc(vec_c, vc.up())
                    dve.wait_ge(vec_c, vc.now())
                    dve.wait_ge(lo_done, at(lo_done, b, t + 1))
                    TT(tmp[:, t, :].rearrange("p (h d) -> p h d", d=DH_LSH),
                               bank(6, C, P, t * C).rearrange("p (h d) -> p h d", d=DH_LSH),
                               lmx[:, 2, :].unsqueeze(2).to_broadcast([P, HEADS, DH_LSH]), ALU.mult).then_inc(vec_c, vc.up())

            def mlp(b, beat):
                dve.wait_ge(vec_c, vc.now())
                TT(n2[:, :, :], n2[:, :, :], tmp[:, :, :], ALU.add).then_inc(vec_c, vc.up())
                dve.wait_ge(vec_c, vc.now())
                norm(vc, n2[:, :, :], tmp[:, :, :], sq2[:, :, :], ln2, 2, 3, b).then_inc(vec_c, vc.up())
                dve.wait_ge(vec_c, vc.now())
                TT(tmp[:, :, :], tmp[:, :, :], n2gb[:, 0:1, :].to_broadcast([P, NT, C]), ALU.mult).then_inc(vec_c, vc.up())
                dve.wait_ge(vec_c, vc.now())
                TT(tmp[:, :, :], tmp[:, :, :], n2gb[:, 1:2, :].to_broadcast([P, NT, C]), ALU.add
                   ).then_inc(y2_ready, 1)
                beat(6)
                TT(h1c[:, :, :], h1c[:, :, :], n2[:, :, :], ALU.add).then_inc(vec_c, vc.up())
                dve.wait_ge(vec_c, vc.now())
                dve.wait_ge(fc2_done, after(fc2_done, b))
                beat(7)
                TT(h1c[:, :, :], h1c[:, :, :], tiles(bank(6, NT * C)), ALU.add).then_inc(vec_c, vc.up())
                dve.wait_ge(vec_c, vc.now())
                norm(vc, h1c[:, :, :], n2[:, :, :], sq2[:, :, :], ln2, 2, 4, b).then_inc(n3_ready, 1)

            def moe_a(b):
                dve.wait_ge(gate_done, after(gate_done, b))
                vv.tensor_copy(gl[:, :, :], bank(7, NT * EXPERTS).rearrange("p (t e) -> p t e", t=NT)).then_inc(vec_c, vc.up())
                dve.wait_ge(vec_c, vc.now())
                apart(dve, gate_vec, b)
                for t in range(NT):
                    vv.max(gtop[:, t, :], gl[:, t, :]).then_inc(vec_c, vc.up())
                dve.wait_ge(vec_c, vc.now())
                apart(dve, gate_vec, b)
                for t in range(NT):
                    vv.max_index(gidx[:, t, :], gtop[:, t, :], gl[:, t, :]).then_inc(vec_c, vc.up())
                TT(gw[:, 0, :], gtop[:, :, 1], gtop[:, :, 0], ALU.subtract).then_inc(gsoft_in, 1)
                dve.wait_ge(gsoft_in, after(gsoft_in, b))
                vv.tensor_copy(gidf[:, :, :], gidx[:, :, :]).then_inc(vec_c, vc.up())
                dve.wait_ge(gsoft_out, after(gsoft_out, b))
                TS(gw[:, 3, :], gw[:, 1, :], 1.0, None, ALU.add).then_inc(vec_c, vc.up())
                dve.wait_ge(vec_c, vc.now())
                vv.reciprocal(gw[:, 2, :], gw[:, 3, :]).then_inc(vec_c, vc.up())
                dve.wait_ge(vec_c, vc.now())
                TT(gw[:, 3, :], gw[:, 2, :], gw[:, 1, :], ALU.mult).then_inc(vec_c, vc.up())
                te = [P, NT, EXPERTS]
                ie = iota_e[:, :].unsqueeze(1).to_broadcast(te)
                TT(coef[:, :, :], gidf[:, :, 0:1].to_broadcast(te), ie, ALU.is_equal).then_inc(vec_c, vc.up())
                TT(coef2[:, :, :], gidf[:, :, 1:2].to_broadcast(te), ie, ALU.is_equal).then_inc(vec_c, vc.up())
                dve.wait_ge(vec_c, vc.now())
                TT(coef[:, :, :], coef[:, :, :], gw[:, 2, :].unsqueeze(2).to_broadcast(te), ALU.mult).then_inc(vec_c, vc.up())
                TT(coef2[:, :, :], coef2[:, :, :], gw[:, 3, :].unsqueeze(2).to_broadcast(te), ALU.mult).then_inc(vec_c, vc.up())
                dve.wait_ge(vec_c, vc.now())
                TT(coef[:, :, :], coef[:, :, :], coef2[:, :, :], ALU.add).then_inc(coef_ready, 1)
                dve.wait_ge(coef_ready, after(coef_ready, b))

            def moe_b(b, beat):
                for e in range(EXPERTS):
                    if e % 2 == 0:
                        beat(e // 2)
                    dve.wait_ge(e_out, at(e_out, b, e + 1))
                    dst = moe if e == 0 else tmp
                    dve.wait_ge(vec_c, vc.now())
                    TT(dst[:, :, :], tiles(bank(6 + e % 2, NT * C)), coef[:, :, e:e + 1].to_broadcast([P, NT, C]),
                       ALU.mult).then_inc(e_used, 1)
                    dve.wait_ge(e_used, at(e_used, b, e + 1))
                    if e > 0:
                        TT(moe[:, :, :], moe[:, :, :], tmp[:, :, :], ALU.add).then_inc(vec_c, vc.up())
                dve.wait_ge(vec_c, vc.now())
                TT(moe[:, :, :], moe[:, :, :], n2[:, :, :], ALU.add).then_inc(vec_c, vc.up())
                dve.wait_ge(vec_c, vc.now())
                dve.wait_ge(eb_out, after(eb_out, b))
                TT(moe[:, :, :], moe[:, :, :], tiles(bank(6, NT * C)), ALU.add).then_inc(vec_c, vc.up())
                dve.wait_ge(vec_c, vc.now())
                norm(vc, moe[:, :, :], tmp[:, :, :], sq2[:, :, :], ln2, 2, 5, b).then_inc(vec_c, vc.up())
                dve.wait_ge(vec_c, vc.now())
                TT(tmp[:, :, :], tmp[:, :, :], ngb[:, 0:1, :].to_broadcast([P, NT, C]), ALU.mult).then_inc(vec_c, vc.up())
                dve.wait_ge(vec_c, vc.now())
                TT(tmp[:, :, :], tmp[:, :, :], ngb[:, 1:2, :].to_broadcast([P, NT, C]), ALU.add).then_inc(vec_c, vc.up())
                dve.wait_ge(vec_c, vc.now())
                if not is_first(b):
                    dve.wait_ge(out_stored, after(out_stored, b - 1))
                TT(outb[:, :, :], tmp[:, :, :], h1c[:, :, :], ALU.add).then_inc(out_ready, 1)
                dve.wait_ge(out_ready, after(out_ready, b))
                dve.sem_inc(c_used, 1)
                vc.end()

            def rest(b, t, beat):
                if t == 0:
                    attention(b, 0, beat)
                    attention(b, 1, beat)
                    attention(b, 2, beat)
                elif t == 1:
                    attention(b, 3, beat)
                    attention(b, 4, beat)
                elif t == 2:
                    attention(b, 5, beat)
                    lsh_a(b, beat)
                elif t == 3:
                    lsh_b(b, beat)
                    mlp(b, beat)
                elif t == 4:
                    moe_a(b)
                elif t == 5:
                    moe_b(b, beat)

            pipeline(dve, stage_a, topk, weigh, lambda b: None, rest)


STEPS = dict(vec_a=25, vec_t=882, vec_c=123)
SET_POOL = 17
SET_ZEROED = 1
SET_ANGLE = 69
SET_VEC = 72


def kernel(x, L0_tok_filt, L0_tok_W_k, L0_tok_b_k, L0_attn_Wi, L0_attn_bi, L0_attn_Wo, L0_attn_bo,
           L0_attn_params_log, L0_ffn_Wq_pk, L0_ffn_pk_keys, L0_ffn_Wq, L0_ffn_keys_table, L0_ffn_values_table,
           L0_ffn_Wo, L1_attn_rotations, L1_attn_norm1_g, L1_attn_norm1_b, L1_attn_q_w, L1_attn_kv_w,
           L1_attn_norm2_g, L1_attn_norm2_b, L1_attn_fc1_w, L1_attn_fc1_b, L1_attn_fc2_w, L1_attn_fc2_b,
           L1_ffn_gate_w, L1_ffn_gate_b, L1_ffn_w1, L1_ffn_b1, L1_ffn_w2, L1_ffn_b2, L1_ffn_gamma, L1_ffn_beta):
    import concourse.bacc as bacc
    from concourse.bass_utils import run_bass_kernel_spmd

    row = lambda a: np.asarray(a).reshape(1, -1)
    arrays = dict(
        x=np.asarray(x), filt=np.asarray(L0_tok_filt).T, w_k=np.asarray(L0_tok_W_k), b_k=row(L0_tok_b_k),
        wi_t=np.asarray(L0_attn_Wi).T, bi=row(L0_attn_bi), wo_t=np.asarray(L0_attn_Wo).T, bo=row(L0_attn_bo),
        lru_log=np.asarray(L0_attn_params_log).T,
        wqpk_t=np.asarray(L0_ffn_Wq_pk).T.reshape(2 * HEADS, C // 2, C),
        keys_t=np.asarray(L0_ffn_pk_keys).transpose(0, 2, 3, 1).reshape(2 * HEADS, C // 2, NKEY),
        wq=np.asarray(L0_ffn_Wq),
        kv_rows=np.concatenate([np.asarray(L0_ffn_keys_table), np.asarray(L0_ffn_values_table)], axis=1),
        wo_pk=np.asarray(L0_ffn_Wo), rot=np.asarray(L1_attn_rotations).reshape(C, -1),
        n1g=row(L1_attn_norm1_g), n1b=row(L1_attn_norm1_b), q_w=np.asarray(L1_attn_q_w),
        kv_w=np.asarray(L1_attn_kv_w), n2g=row(L1_attn_norm2_g), n2b=row(L1_attn_norm2_b),
        fc1_w=np.asarray(L1_attn_fc1_w), fc1_b=np.asarray(L1_attn_fc1_b).reshape(2, P).T, fc2_w=np.asarray(L1_attn_fc2_w),
        fc2_b=row(L1_attn_fc2_b), gate_w=np.asarray(L1_ffn_gate_w), gate_b=row(L1_ffn_gate_b),
        w1=np.asarray(L1_ffn_w1), b1=np.asarray(L1_ffn_b1)[None], w2=np.asarray(L1_ffn_w2),
        b2=np.asarray(L1_ffn_b2), gamma=row(L1_ffn_gamma), beta=row(L1_ffn_beta),
    )
    arrays = {name: np.ascontiguousarray(a) for name, a in arrays.items()}
    nc = bacc.Bacc("TRN2", target_bir_lowering=False, num_devices=1)
    args = {name: nc.dram_tensor(f"in_{name}", a.shape, mybir.dt.from_np(a.dtype), kind="ExternalInput").ap()
            for name, a in arrays.items()}
    B, L, _ = x.shape
    nt = -(-(L - TAPS) // P)
    out = nc.dram_tensor("tokens_out", (B, L - TAPS, C), F32, kind="ExternalOutput").ap()
    h1_dram = nc.dram_tensor("h1_scratch", (B, P, nt, C), F32, kind="Internal").ap()
    n1t_dram = nc.dram_tensor("n1t_scratch", (B, C, nt * P), F32, kind="Internal").ap()
    audio_tower(nc, **args, out=out, h1_dram=h1_dram, n1t_dram=n1t_dram)
    r = run_bass_kernel_spmd(nc, [{f"in_{name}": a for name, a in arrays.items()}], core_ids=[0])
    return r.results[0]["tokens_out"]
```

```python
import math
from contextlib import ExitStack

import numpy as np

import concourse.bass as bass
from concourse import mybir

ALU = mybir.AluOpType
ACT = mybir.ActivationFunctionType
AX = mybir.AxisListType
F32 = mybir.dt.float32
I32 = mybir.dt.int32
U32 = mybir.dt.uint32

P = 128
D_IN = 128
C = 64
TAPS = 8
NST = 128
HEADS = 8
NKEY = 64
TOPK = 16
HASHES, BUCKETS = 4, 8
M_LSH = HASHES * BUCKETS
DH_LSH = C // HEADS
DFF = 4 * C
EXPERTS, FEXP = 16, 128
EPS = 1e-5
NEG = -1e30
LOWEST = -3.0e38
ROUND = 12582912.0
TWO_PI = 2.0 * math.pi

CAND_LEN = [TOPK // (a + 1) for a in range(TOPK)]
CAND_OFF = [sum(CAND_LEN[:a]) for a in range(TOPK)]
NCAND = sum(CAND_LEN)
CAND_RUNS = []
for _a, _n in enumerate(CAND_LEN):
    if CAND_RUNS and CAND_RUNS[-1][2] == _n:
        CAND_RUNS[-1][1] += 1
    else:
        CAND_RUNS.append([_a, 1, _n])

SPREAD = 16384.0
PICKS = 6
RING = 4


class Steps:

    def __init__(self, sem, per):
        self.sem, self.per, self.b, self.n = sem, per, 0, 0

    def begin(self, b, n=0):
        self.b, self.n = b, n

    def up(self):
        self.n += 1
        return 1

    def now(self):
        return self.b * self.per + self.n

    def end(self):
        assert self.n == self.per, (self.n, self.per)


def audio_tower(nc, x, filt, w_k, b_k, wi_t, bi, wo_t, bo, lru_log, wqpk_t, keys_t, wq, kv_rows, wo_pk,
                rot, n1g, n1b, q_w, kv_w, n2g, n2b, fc1_w, fc1_b, fc2_w, fc2_b,
                gate_w, gate_b, w1, b1, w2, b2, gamma, beta, out, h1_dram, n1t_dram):
    B, L, _ = x.shape
    N = L - TAPS
    NT = -(-N // P)
    NP_ = NT * P
    TAIL = N - (NT - 1) * P
    XTAIL = L - (NT - 1) * P
    HALF = NP_ // 2
    DIRECT = TAIL // TOPK
    SPARE_HEADS = HEADS - DIRECT
    SPARE0 = TAIL // 32 * 32
    assert HEADS * TOPK == P and SPARE0 + 32 == P

    def ranks(t, h):
        return TOPK if t < NT - 1 else max(0, min(TOPK, TAIL - h * TOPK))

    def uses(slot, t, h=-1):
        return sum(1 for k in range(slot, t * HEADS + max(h, 0), RING) if ranks(*divmod(k, HEADS)))

    def landed(slot, t, h=-1):
        return sum(ranks(*divmod(k, HEADS)) for k in range(slot, t * HEADS + max(h, 0), RING))

    assert B > 2 and HALF <= 512 and NCAND == 50

    with ExitStack() as ctx:
        def sb(name, shape, dt=F32):
            return ctx.enter_context(nc.sbuf_tensor(name, shape, dt))

        ps = ctx.enter_context(nc.psum_tensor("ps", [P, 8 * 512], F32))

        def bank(i, n, rows=P, off=0):
            return ps[0:rows, i * 512 + off:i * 512 + off + n]

        ident = sb("ident", [P, P])
        causal = sb("causal", [P, P])
        ones_row = sb("ones_row", [1, P])
        wc = sb("wc", [P, TAPS, C])
        filt_c = sb("filt_c", [P, TAPS])
        bk_row = sb("bk_row", [1, C])
        wi_aug = sb("wi_aug", [C + 1, 2 * NST])
        wo_g = sb("wo_g", [P, 2, C])
        bo_row = sb("bo_row", [1, C])
        logs = sb("logs", [P, 3])
        lam = sb("lam", [P, 4])
        small = sb("small", [P, 12])
        small_i = sb("small_i", [P, 4], I32)
        cos_t = sb("cos_t", [P, NP_])
        sin_t = sb("sin_t", [P, NP_])
        w_sim = sb("w_sim", [C, 2 * HEADS * NKEY])
        wq_s = sb("wq_s", [C, HEADS * C])
        wo_f = sb("wo_f", [P, HEADS * C // P, C])
        n1gb = sb("n1gb", [P, 2, C])
        n2gb = sb("n2gb", [P, 2, C])
        ngb = sb("ngb", [P, 2, C])
        rot_s = sb("rot_s", [C, HASHES * BUCKETS // 2])
        qw_s = sb("qw_s", [C, C])
        kvw_s = sb("kvw_s", [C, 2 * C])
        head_mask = sb("head_mask", [C, HEADS])
        v_mask = sb("v_mask", [P, 2, C])
        fc1_s = sb("fc1_s", [C, DFF])
        fc1b_c = sb("fc1b_c", [P, 2])
        fc2_s = sb("fc2_s", [P, 2, C])
        fc2b_row = sb("fc2b_row", [1, C])
        gate_aug = sb("gate_aug", [C + 1, EXPERTS])
        w1_aug = sb("w1_aug", [C + 1, EXPERTS, FEXP])
        w2_s = sb("w2_s", [P, EXPERTS, C])
        b2_row = sb("b2_row", [EXPERTS, C])
        iota_c = sb("iota_c", [P, NCAND])
        iota_e = sb("iota_e", [P, EXPERTS])
        rank8 = sb("rank8", [P, BUCKETS])
        head_base = sb("head_base", [P, HEADS])
        valid = sb("valid", [P, NT])
        spare_of = sb("spare_of", [P, SPARE_HEADS])

        xrow = sb("xrow", [P, NT, D_IN])
        xt = sb("xt", [P, NP_ + TAPS])
        h0 = sb("h0", [P, NT, C])
        z = sb("z", [P, NT, C])
        zt = sb("zt", [C + 1, NP_])
        wide = sb("wide", [P, 6, NP_])
        h1a = sb("h1a", [P, NT, C])
        n1t = sb("n1t", [C, NP_])
        lnv = sb("lnv", [P, 4, NT])

        tv = sb("tv", [P, 2 * HEADS, TOPK])
        ti = sb("ti", [P, 2 * HEADS, TOPK], U32)
        tif = sb("tif", [P, 2 * HEADS, TOPK])
        cs = sb("cs", [P, HEADS, NCAND])
        ci = sb("ci", [P, HEADS, NCAND])
        fs = sb("fs", [P, HEADS, TOPK])
        fe = sb("fe", [P, HEADS, TOPK])
        fp = sb("fp", [P, HEADS, TOPK], U32)
        fpf = sb("fpf", [P, HEADS, TOPK])
        fsum = sb("fsum", [P, 2, HEADS])
        row_i = sb("row_i", [P, NT, HEADS * TOPK], U32)
        row_w = sb("row_w", [P, NT, HEADS * TOPK])
        ONEHOT = HEADS // 2 * TOPK * NCAND
        flat = wide[:, :, :].rearrange("p a n -> p (a n)")
        onehot = flat[:, 0:ONEHOT]
        trest = flat[:, ONEHOT:ONEHOT + 2 * HEADS * NKEY].rearrange("p (g k) -> p g k", k=NKEY)

        ring = sb("ring", [P, RING, TOPK, 2 * C])
        kv = sb("kv", [P, NT, 2, HEADS, C])

        spare_t = sb("spare_t", [P, SPARE_HEADS, TAIL])

        kt = sb("kt", [P, HEADS // 2, NP_])
        v = sb("v", [P, NT, HEADS, C])
        h1c = sb("h1c", [P, NT, C])
        lt = sb("lt", [C + 1, NP_])
        n1tc = lt
        qt = sb("qt", [P, HEADS // 2, P])
        prob = sb("prob", [P, 2, NP_])
        probt = sb("probt", [P, 2, NP_])
        nmax = sb("nmax", [P, HEADS])
        rsum = sb("rsum", [P, HEADS])
        rinv = sb("rinv", [P, HEADS])
        on = sb("on", [P, HEADS * C])
        ot = sb("ot", [P, HEADS // 2, P])
        n2 = sb("n2", [P, NT, C])
        xh = sb("xh", [P, NT, C + 1])
        tmp = sb("tmp", [P, NT, C])
        ln2 = sb("ln2", [P, 4, NT])
        rots = sb("rots", [P, NT, HASHES, BUCKETS])
        oneh = sb("oneh", [P, NT, HASHES, BUCKETS])
        rmx = sb("rmx", [P, NT, HASHES])
        pool_s = sb("pool_s", [M_LSH, C + 1])
        pinv = sb("pinv", [M_LSH, 2])
        rpt = sb("rpt", [C + 1, M_LSH])
        rpt4 = sb("rpt4", [C, 4, M_LSH])
        kbd = sb("kbd", [C + 1, HEADS, M_LSH])
        vbd = sb("vbd", [P, 2, C])
        lp = prob[:, 0, 0:HEADS * M_LSH].rearrange("p (h m) -> p h m", m=M_LSH)
        lpt = probt[:, 0, 0:2 * P].rearrange("p (g t) -> p g t", g=2)
        lqt = kt[0:C + 1, 0, :]
        lmx = sb("lmx", [P, 3, HEADS])
        hidden = prob
        hexp = probt
        gl = sb("gl", [P, NT, EXPERTS])
        gtop = sb("gtop", [P, NT, 8])
        gidx = sb("gidx", [P, NT, 8], U32)
        gidf = sb("gidf", [P, NT, 8])
        gw = sb("gw", [P, 4, NT])
        coef = sb("coef", [P, NT, EXPERTS])
        coef2 = sb("coef2", [P, NT, EXPERTS])
        coeft = v[0:EXPERTS, 0:2, :, :].rearrange("p t h c -> p (t h c)")[:, 0:NP_]
        moe = on[:, 0:NT * C].rearrange("p (t c) -> p t c", c=C)
        sq2 = ot[:, :, :].rearrange("p g n -> p (g n)")[:, 0:NT * C].rearrange("p (t c) -> p t c", c=C)
        outb = sb("outb", [P, NT, C])

        rises = {}

        def sem(name, rise=None):
            rises[name] = rise
            return ctx.enter_context(nc.semaphore(name))

        x_loaded = sem("x_loaded", 32)
        x_turned = sem("x_turned", 2)
        xt_ready = sem("xt_ready", 2)
        conv_done = sem("conv_done", 1)
        h0_ready = sem("h0_ready", 1)
        z_ready = sem("z_ready", 1)
        z_turned = sem("z_turned", 2)
        zt_ready = sem("zt_ready", 2)
        u_done = sem("u_done", 1)
        y_ready = sem("y_ready", 1)
        lru_done = sem("lru_done", 1)
        h1_ready = sem("h1_ready", 1)
        n1_ready = sem("n1_ready", 1)
        n1_turned = sem("n1_turned", 2)
        n1t_ready = sem("n1t_ready", 2)
        a_stored = sem("a_stored", 32)
        sims_done = sem("sims_done", NT)
        sims_copied = sem("sims_copied", NT)
        soft_in = sem("soft_in", NT)
        soft_exp = sem("soft_exp", NT)
        rows_ready = sem("rows_ready", NT)
        tail_chosen = sem("tail_chosen", 1)
        tail_turned = sem("tail_turned", 1)
        spare_summed = sem("spare_summed", sum(1 for h in range(HEADS) if ranks(NT - 1, h)))
        spare_copied = sem("spare_copied", 1)
        spare_turned = sem("spare_turned", 1)
        spare_in = sem("spare_in", 1)
        weighed = sem("weighed", sum(uses(s, NT) for s in range(RING)))
        k_turned = sem("k_turned", NT)
        kt_ready = sem("kt_ready", NT)
        v_ready = sem("v_ready", NT)
        c_loaded = sem("c_loaded", 32)
        c_used = sem("c_used", 1)
        q_done = sem("q_done", NT)
        qt_ready = sem("qt_ready", NT)
        s_done = sem("s_done", NT * HEADS)
        max_ready = sem("max_ready", NT * HEADS)
        p_ready = sem("p_ready", NT * HEADS)
        p_turned = sem("p_turned", NT * HEADS)
        pt_ready = sem("pt_ready", NT * HEADS)
        o_done = sem("o_done", NT * HEADS)
        on_ready = sem("on_ready", NT)
        on_turned = sem("on_turned", NT)
        ot_ready = sem("ot_ready", NT)
        ffn_done = sem("ffn_done", 1)
        xh_ready = sem("xh_ready", 1)
        lt_turned = sem("lt_turned", 6)
        lt_ready = sem("lt_ready", 6)
        rot_done = sem("rot_done", 1)
        oneh_ready = sem("oneh_ready", 1)
        pooled = sem("pooled", 1)
        pool_ready = sem("pool_ready", 1)
        rp_turned = sem("rp_turned", 1)
        rpt_ready = sem("rpt_ready", 2)
        kvl_done = sem("kvl_done", 1)
        kbd_ready = sem("kbd_ready", 1)
        lq_done = sem("lq_done", 1)
        lqt_ready = sem("lqt_ready", 1)
        logit_done = sem("logit_done", NT)
        lmax_ready = sem("lmax_ready", NT)
        lexp_ready = sem("lexp_ready", NT)
        lp_turned = sem("lp_turned", NT)
        lpt_ready = sem("lpt_ready", NT)
        lo_done = sem("lo_done", NT)
        y2_ready = sem("y2_ready", 1)
        fc1_done = sem("fc1_done", 2)
        hid_ready = sem("hid_ready", 2)
        fc2_done = sem("fc2_done", 1)
        n3_ready = sem("n3_ready", 1)
        gate_done = sem("gate_done", 1)
        gsoft_in = sem("gsoft_in", 1)
        gsoft_out = sem("gsoft_out", 1)
        e_hid = sem("e_hid", EXPERTS)
        e_relu = sem("e_relu", EXPERTS)
        e_out = sem("e_out", EXPERTS)
        coef_ready = sem("coef_ready", 1)
        coef_turned = sem("coef_turned", 2)
        coeft_ready = sem("coeft_ready", 2)
        eb_out = sem("eb_out", 1)
        e_used = sem("e_used", EXPERTS)
        out_ready = sem("out_ready", 1)
        out_stored = sem("out_stored", 32)
        std = [sem("std0", 1), sem("std1", 1), sem("std2", 5)]
        root = [sem("root0", 1), sem("root1", 1), sem("root2", 5)]
        vec_s = sem("vec_s", 1)
        vec_a, vec_t = sem("vec_a", STEPS["vec_a"]), sem("vec_t", STEPS["vec_t"])
        vec_c = sem("vec_c", STEPS["vec_c"])
        gathered = [sem(f"gathered{i}") for i in range(RING)]
        ring_free = [sem(f"ring_free{i}") for i in range(RING)]
        w_loaded = sem("w_loaded")
        set_vec, set_act, set_pe, set_pool = sem("set_vec"), sem("set_act"), sem("set_pe"), sem("set_pool")
        gate_pe, gate_pool, gate_vec = sem("gate_pe"), sem("gate_pool"), sem("gate_vec")

        def at(s, b, n):
            return b * rises[s.name] + n

        def after(s, b):
            return at(s, b, rises[s.name])

        def apart(e, count, b):
            if not isinstance(b, int):
                e.sem_inc(count, 1)

        block = ctx.enter_context(nc.Block())

        def is_first(b):
            return isinstance(b, int) and b == 0

        ATT_BEATS = ({0: 0, 4: 1}, {0: 2, 3: 3, 6: 4}, {1: 5, 4: 6, 6: 7},
                     {0: 0, 2: 1, 4: 2, 6: 3}, {0: 4, 2: 5, 4: 6, 6: 7}, {0: 0, 2: 1, 4: 2, 6: 3})

        MID, LATE = 4, 10
        LEAD = 2
        LATE_STEPS = {10: (0, 1), 11: (2, 3), 12: (4,), 13: (5, 6), 14: (7,), 15: (8, 9)}

        def beat_at(beat, i, h):
            if h in ATT_BEATS[i]:
                beat(ATT_BEATS[i][h])

        def pipeline(e, stage_a, topk, weigh, kv_final, rest):
            def turn_of(i, ahead=True, gather=True, behind=True, first=0):
                last = gather and not ahead
                for t in range(first, NT):
                    def pick(k):
                        if gather and k < PICKS:
                            if t < NT - 1:
                                topk(i, t + 1, k)
                            elif ahead:
                                topk(i + 1, 0, k)

                    def total(h):
                        if gather:
                            weigh(i, t, h)

                    def beat(k):
                        pick(k)
                        total(k)

                    def early(e):
                        if e - MID < PICKS - 1:
                            pick(e - MID + 1)
                            if e > MID:
                                total(e - MID - 1)

                    def late(e):
                        for k in LATE_STEPS[e]:
                            pick(k)
                            if k >= LEAD:
                                total(k - LEAD)

                    def late_sums(e):
                        for k in LATE_STEPS[e]:
                            if k - LEAD >= PICKS - 2:
                                total(k - LEAD)

                    if t == NT - 2:
                        pick(0)
                        if behind:
                            rest(i - 1, t, early)
                        else:
                            for e in range(MID, LATE):
                                early(e)
                        if ahead:
                            stage_a(i + 1, total)
                        else:
                            rest(i - 1, t + 1, late_sums)
                    elif t == NT - 1 and last:
                        kv_final(i, 0, t)
                        rest(i, 0, beat)
                    elif t == NT - 1 and not ahead:
                        pass
                    elif t == NT - 1:
                        if behind:
                            rest(i - 1, t, late)
                        else:
                            for e in range(LATE, EXPERTS):
                                late(e)
                    elif behind:
                        rest(i - 1, t, beat)
                    else:
                        for k in range(HEADS):
                            beat(k)
                if gather:
                    kv_final(i, NT - 1 if last else 0, NT)

            stage_a(0, lambda h: None)
            for k in range(PICKS):
                topk(0, 0, k)
            turn_of(0, behind=False)
            with e.Fori(1, B - 1) as i:
                turn_of(i)
            turn_of(B - 1, ahead=False)
            turn_of(B, ahead=False, gather=False, first=1)

        weights = [
            (filt_c[:, :], filt),
            (wc[:, :, :], w_k.rearrange("(f d) k -> d f k", d=D_IN)),
            (bk_row[:, :], b_k), (wi_aug[0:C, :], wi_t), (wi_aug[C:C + 1, :], bi),
            (wo_g[:, :, :], wo_t.rearrange("(r n) c -> n r c", n=NST)), (bo_row[:, :], bo),
            (logs[:, :], lru_log), (wq_s[:, :], wq),
            (wo_f[:, :, :], wo_pk.rearrange("(g p) c -> p g c", p=P)),
            (ring[0:32, 0, 0:8, :].rearrange("p a b -> p (a b)"), wqpk_t.rearrange("g d c -> d g c")),
            (ring[0:32, 0, 8:16, :].rearrange("p a b -> p (a b)"), keys_t.rearrange("g d k -> d g k")),
            (n1gb[:, 0, :], n1g.to_broadcast([P, C])), (n1gb[:, 1, :], n1b.to_broadcast([P, C])),
            (n2gb[:, 0, :], n2g.to_broadcast([P, C])), (n2gb[:, 1, :], n2b.to_broadcast([P, C])),
            (ngb[:, 0, :], gamma.to_broadcast([P, C])), (ngb[:, 1, :], beta.to_broadcast([P, C])),
            (rot_s[:, :], rot), (qw_s[:, :], q_w), (kvw_s[:, :], kv_w), (fc1_s[:, :], fc1_w),
            (fc1b_c[:, :], fc1_b),
            (fc2_s[:, :, :], fc2_w.rearrange("(g p) c -> p g c", p=P)), (fc2b_row[:, :], fc2_b),
            (gate_aug[0:C, :], gate_w), (gate_aug[C:C + 1, :], gate_b),
            (w1_aug[0:C, :, :], w1.rearrange("e h f -> h e f")), (w1_aug[C:C + 1, :, :], b1),
            (w2_s[:, :, :], w2.rearrange("e f h -> f e h")), (b2_row[:, :], b2),
        ]
        ALL_W = 16 * len(weights)

        @block.sync
        def _(sp):
            for dst, src in weights:
                sp.dma_start(dst, src).then_inc(w_loaded, 16)
            sp.wait_ge(set_vec, SET_ZEROED)

            def load_x(b):
                sp.dma_start(xrow[:, 0:NT - 1, :], x[bass.ds(b, 1), 0:(NT - 1) * P, :].rearrange(
                    "o (t p) d -> p (o t) d", p=P)).then_inc(x_loaded, 16)
                sp.dma_start(xrow[0:XTAIL, NT - 1, :], x[bass.ds(b, 1), (NT - 1) * P:L, :].rearrange(
                    "o p d -> (o p) d")).then_inc(x_loaded, 16)

            def load_a(b):
                if not is_first(b):
                    sp.wait_ge(x_turned, after(x_turned, b - 1))
                load_x(b)

            def store_a(b):
                sp.wait_ge(h1_ready, after(h1_ready, b))
                sp.dma_start(h1_dram[bass.ds(b, 1), :, :, :].rearrange("o p t c -> (o p) t c"),
                             h1a[:, :, :]).then_inc(a_stored, 16)
                sp.wait_ge(n1t_ready, after(n1t_ready, b))
                sp.dma_start(n1t_dram[bass.ds(b, 1), :, :].rearrange("o c n -> (o c) n"),
                             n1t[:, :]).then_inc(a_stored, 16)

            def load_c(b):
                sp.wait_ge(a_stored, after(a_stored, b))
                if not is_first(b):
                    sp.wait_ge(c_used, after(c_used, b - 1))
                sp.dma_start(h1c[:, :, :], h1_dram[bass.ds(b, 1), :, :, :].rearrange("o p t c -> (o p) t c")
                             ).then_inc(c_loaded, 16)
                sp.dma_start(n1tc[0:C, :], n1t_dram[bass.ds(b, 1), :, :].rearrange("o c n -> (o c) n")
                             ).then_inc(c_loaded, 16)

            def store_out(b):
                sp.wait_ge(out_ready, after(out_ready, b))
                sp.dma_start(out[bass.ds(b, 1), 0:(NT - 1) * P, :].rearrange("o (t p) c -> p (o t) c", p=P),
                             outb[:, 0:NT - 1, :]).then_inc(out_stored, 16)
                sp.dma_start(out[bass.ds(b, 1), (NT - 1) * P:N, :].rearrange("o p c -> (o p) c"),
                             outb[0:TAIL, NT - 1, :]).then_inc(out_stored, 16)

            def turn_of(i, ahead=True, behind=True):
                if ahead:
                    load_a(i + 1)
                if behind:
                    load_c(i - 1)
                if ahead:
                    store_a(i + 1)
                if behind:
                    store_out(i - 1)

            load_a(0)
            store_a(0)
            turn_of(0, ahead=B > 1, behind=False)
            if B > 2:
                with sp.Fori(1, B - 1) as i:
                    turn_of(i)
            if B > 1:
                turn_of(B - 1, ahead=False)
            turn_of(B, ahead=False)
            sp.wait_ge(out_stored, after(out_stored, B - 1))
            sp.wait_ge(a_stored, after(a_stored, B - 1))

        @block.gpsimd
        def _(pool):
            g = nc.gpsimd
            n = [0]

            def one(ins):
                ins.then_inc(set_pool, 1)
                n[0] += 1

            one(g.memset(ident[:, :], 1.0))
            one(g.memset(causal[:, :], 0.0))
            one(g.memset(head_mask[:, :], 1.0))
            one(g.memset(v_mask[:, :, :], 1.0))
            one(g.memset(valid[:, :], 1.0))
            one(g.memset(spare_of[:, :], 1.0))
            one(g.iota(cos_t[:, :], pattern=[[1, NP_]], base=0, channel_multiplier=0,
                       allow_small_or_imprecise_dtypes=True))
            one(g.iota(iota_c[:, :], pattern=[[int(SPREAD), NCAND]], base=0, channel_multiplier=0,
                       allow_small_or_imprecise_dtypes=True))
            one(g.iota(iota_e[:, :], pattern=[[1, EXPERTS]], base=0, channel_multiplier=0,
                       allow_small_or_imprecise_dtypes=True))
            one(g.iota(rank8[:, :], pattern=[[-1, BUCKETS]], base=BUCKETS, channel_multiplier=0,
                       allow_small_or_imprecise_dtypes=True))
            one(g.iota(head_base[:, :], pattern=[[NKEY * NKEY, HEADS]], base=0, channel_multiplier=0,
                       allow_small_or_imprecise_dtypes=True))
            pool.wait_ge(set_pool, n[0])
            one(g.affine_select(out=ident[:, :], in_=ident[:, :], compare_op=ALU.is_equal, fill=0.0, base=0,
                                pattern=[[-1, P]], channel_multiplier=1))
            one(g.affine_select(out=causal[:, :], in_=causal[:, :], compare_op=ALU.is_ge, fill=NEG, base=0,
                                pattern=[[-1, P]], channel_multiplier=1))
            one(g.affine_select(out=head_mask[:, :], in_=head_mask[:, :], compare_op=ALU.is_ge, fill=0.0, base=0,
                                pattern=[[-DH_LSH, HEADS]], channel_multiplier=1))
            one(g.affine_select(out=v_mask[:, :, :].rearrange("p g (h d) -> p g h d", d=DH_LSH),
                                in_=v_mask[:, :, :].rearrange("p g (h d) -> p g h d", d=DH_LSH),
                                compare_op=ALU.is_ge, fill=0.0, base=0,
                                pattern=[[P, 2], [-M_LSH, HEADS], [0, DH_LSH]], channel_multiplier=1))
            one(g.affine_select(out=valid[:, :], in_=valid[:, :], compare_op=ALU.is_ge, fill=0.0, base=N - 1,
                                pattern=[[-P, NT]], channel_multiplier=-1))
            one(g.affine_select(out=spare_of[:, :], in_=spare_of[:, :], compare_op=ALU.is_ge, fill=0.0,
                                base=-DIRECT * TOPK, pattern=[[-TOPK, SPARE_HEADS]], channel_multiplier=1))
            pool.wait_ge(set_pool, n[0])
            one(g.affine_select(out=spare_of[:, :], in_=spare_of[:, :], compare_op=ALU.is_ge, fill=0.0,
                                base=DIRECT * TOPK + TOPK - 1, pattern=[[TOPK, SPARE_HEADS]],
                                channel_multiplier=-1))
            one(g.affine_select(out=head_mask[:, :], in_=head_mask[:, :], compare_op=ALU.is_ge, fill=0.0,
                                base=DH_LSH - 1, pattern=[[DH_LSH, HEADS]], channel_multiplier=-1))
            one(g.affine_select(out=v_mask[:, :, :].rearrange("p g (h d) -> p g h d", d=DH_LSH),
                                in_=v_mask[:, :, :].rearrange("p g (h d) -> p g h d", d=DH_LSH),
                                compare_op=ALU.is_ge, fill=0.0, base=M_LSH - 1,
                                pattern=[[-P, 2], [M_LSH, HEADS], [0, DH_LSH]], channel_multiplier=-1))
            pool.wait_ge(set_pool, n[0])
            one(g.affine_select(out=spare_of[:, :], in_=spare_of[:, :], compare_op=ALU.is_ge, fill=0.0,
                                base=-TAIL, pattern=[[0, SPARE_HEADS]], channel_multiplier=1))
            assert n[0] == SET_POOL
            pool.wait_ge(set_pool, SET_POOL)
            pool.wait_ge(set_pe, 2)

            def body(b):
                for t in range(NT):
                    pool.wait_ge(rows_ready, at(rows_ready, b, t + 1))
                    pool.sem_inc(gate_pool, 1)
                    for h in range(HEADS):
                        slot = (t * HEADS + h) % RING
                        if ranks(t, h):
                            pool.wait_ge(ring_free[slot], b * uses(slot, NT) + uses(slot, t, h) + 1)
                            pool.sem_inc(gate_pool, 1)
                        for r in range(ranks(t, h)):
                            j = h * TOPK + r
                            g.indirect_dma_start(ring[:, slot, r, :], None, kv_rows,
                                                 bass.IndirectOffsetOnAxis(ap=row_i[:, t, j:j + 1], axis=0)
                                                 ).then_inc(gathered[slot], 16)

            body(0)
            if B > 1:
                with pool.Fori(1, B) as b:
                    body(b)

        @block.scalar
        def _(act):
            a = nc.scalar
            act.wait_ge(set_pe, 2)
            a.activation(w_sim[:, :], bank(0, 1024, C), ACT.Copy).then_inc(set_act, 1)

            def copy_turned(turned, copied, dst, rows, b, base=0):
                act.wait_ge(turned, at(turned, b, base + 1))
                a.activation(dst[0:rows, 0:512], bank(0, 512, rows), ACT.Copy).then_inc(copied, 1)
                act.wait_ge(turned, at(turned, b, base + 2))
                a.activation(dst[0:rows, 512:NP_], bank(1, NP_ - 512, rows), ACT.Copy).then_inc(copied, 1)

            def take_root(i, buf, b, n):
                act.wait_ge(std[i], at(std[i], b, n))
                a.activation(buf[:, 2, :], buf[:, 1, :], ACT.Sqrt).then_inc(root[i], 1)

            def stage_a(b, total):
                copy_turned(x_turned, xt_ready, xt, P, b)
                act.wait_ge(conv_done, after(conv_done, b))
                a.activation(h0[:, :, :].rearrange("p t c -> p (t c)"), bank(2, NT * C), ACT.Relu
                             ).then_inc(h0_ready, 1)
                if is_first(b):
                    act.wait_ge(set_vec, SET_VEC)
                    a.activation(sin_t[:, :], sin_t[:, :], ACT.Sin, scale=6.2831845).then_inc(set_act, 1)
                    a.activation(cos_t[:, :], cos_t[:, :], ACT.Sin, scale=6.2831845).then_inc(set_act, 1)
                take_root(0, lnv, b, 1)
                copy_turned(z_turned, zt_ready, zt, C, b)
                total(4)
                total(5)
                take_root(1, lnv, b, 1)
                total(6)
                if not is_first(b):
                    act.wait_ge(a_stored, after(a_stored, b - 1))
                copy_turned(n1_turned, n1t_ready, n1t, C, b)
                total(7)

            def topk(b, t, part):
                if part == 0:
                    if t > 0:
                        act.wait_ge(rows_ready, at(rows_ready, b, t))
                    act.wait_ge(sims_done, at(sims_done, b, t + 1))
                    a.activation(trest.rearrange("p g k -> p (g k)"), bank(4, 2 * HEADS * NKEY), ACT.Copy
                                 ).then_inc(sims_copied, 1)
                elif part == 4:
                    act.wait_ge(soft_in, at(soft_in, b, t + 1))
                    a.activation(fe[:, :, :], fe[:, :, :], ACT.Exp).then_inc(soft_exp, 1)

            def weigh(b, t, h):
                if not ranks(t, h):
                    act.wait_ge(spare_summed, after(spare_summed, b))
                    a.activation(spare_t[:, :, :].rearrange("p k t -> p t k"),
                                 bank(1, TAIL * SPARE_HEADS).rearrange("p (t k) -> p t k", k=SPARE_HEADS),
                                 ACT.Copy).then_inc(spare_copied, 1)
                    return
                act.wait_ge(rows_ready, at(rows_ready, b, t + 1))
                slot = (t * HEADS + h) % RING
                act.wait_ge(gathered[slot], (b * landed(slot, NT) + landed(slot, t, h) + ranks(t, h)) * 16)
                for k in range(ranks(t, h)):
                    last = a.activation(ring[:, slot, k, :], ring[:, slot, k, :], ACT.Copy,
                                        scale=row_w[:, t, h * TOPK + k:h * TOPK + k + 1])
                last.then_inc(weighed, 1)

            def kv_final(b, t0, t1):
                for t in range(t0, t1):
                    act.wait_ge(k_turned, at(k_turned, b, t + 1))
                    a.activation(kt[:, :, t * P:(t + 1) * P],
                                 bank(t % 2, 512).rearrange("p (g n) -> p g n", g=HEADS // 2),
                                 ACT.Copy).then_inc(kt_ready, 1)
                    a.activation(v[:, t, :, :].rearrange("p h c -> p (h c)"),
                                 kv[:, t, 1, :, :].rearrange("p h c -> p (h c)"),
                                 ACT.Copy).then_inc(v_ready, 1)

            def attention(b, i, beat):
                n = (i + 1) * P
                beat_at(beat, i, 0)
                act.wait_ge(q_done, at(q_done, b, i + 1))
                a.activation(qt[:, :, :].rearrange("p g n -> p (g n)"), bank(0, 512), ACT.Copy,
                             scale=C ** -0.5).then_inc(qt_ready, 1)
                for h in range(HEADS + 1):
                    if h > 0:
                        beat_at(beat, i, h)
                    if h < HEADS:
                        u = i * HEADS + h
                        act.wait_ge(max_ready, at(max_ready, b, u + 1))
                        if u >= 2:
                            act.wait_ge(p_turned, at(p_turned, b, u - 1))
                        a.activation(prob[:, u % 2, 0:n], bank(2 + 2 * (u % 2), n), ACT.Exp,
                                     bias=nmax[:, h:h + 1], accum_out=rsum[:, h:h + 1]
                                     ).then_inc(p_ready, 1)
                    if h > 0:
                        u = i * HEADS + h - 1
                        act.wait_ge(p_turned, at(p_turned, b, u + 1))
                        if u >= 2:
                            act.wait_ge(o_done, at(o_done, b, u - 1))
                        a.activation(probt[:, u % 2, 0:n], bank(0, n), ACT.Copy).then_inc(pt_ready, 1)
                act.wait_ge(on_turned, at(on_turned, b, i + 1))
                a.activation(ot[:, :, :].rearrange("p g n -> p (g n)"), bank(0, 512), ACT.Copy
                             ).then_inc(ot_ready, 1)

            def lsh_a(b, beat):
                beat(4)
                take_root(2, ln2, b, 1)
                take_root(2, ln2, b, 2)
                copy_turned(lt_turned, lt_ready, lt, C, b, 0)
                beat(5)
                beat(6)
                act.wait_ge(rp_turned, after(rp_turned, b))
                a.activation(rpt[:, :], bank(5, M_LSH, C + 1), ACT.Copy).then_inc(rpt_ready, 1)
                a.activation(rpt4[:, :, :], bank(5, M_LSH, C).unsqueeze(1).to_broadcast([C, 4, M_LSH]), ACT.Copy
                             ).then_inc(rpt_ready, 1)
                act.wait_ge(lq_done, after(lq_done, b))
                a.activation(lqt[0:C, :].rearrange("c (g n) -> c g n", g=2),
                             ps[0:C, 1024:2048].rearrange("c (g n) -> c g n", g=2)[:, :, 0:HALF],
                             ACT.Copy, scale=DH_LSH ** -0.5).then_inc(lqt_ready, 1)
                beat(7)

            def lsh_b(b, beat):
                for t in range(NT):
                    if t % 2 == 0:
                        beat(t // 2)
                    act.wait_ge(lmax_ready, at(lmax_ready, b, t + 1))
                    a.activation(lp, lp, ACT.Exp).then_inc(lexp_ready, 1)
                    act.wait_ge(lp_turned, at(lp_turned, b, t + 1))
                    a.activation(probt[:, 0, 0:2 * P], bank(0, 2 * P), ACT.Copy).then_inc(lpt_ready, 1)

            def mlp(b, beat):
                take_root(2, ln2, b, 3)
                copy_turned(lt_turned, lt_ready, lt, C, b, 2)
                beat(3)
                for f in range(2):
                    act.wait_ge(fc1_done, at(fc1_done, b, f + 1))
                    a.activation(hidden[:, f, :].rearrange("p (g n) -> p g n", g=2),
                                 ps[:, 1024 * (1 + f):1024 * (2 + f)].rearrange("p (g n) -> p g n", g=2)[:, :, 0:HALF],
                                 ACT.Gelu, bias=fc1b_c[:, f:f + 1]).then_inc(hid_ready, 1)
                beat(4)
                take_root(2, ln2, b, 4)

            def moe_a(b, beat):
                copy_turned(lt_turned, lt_ready, lt, C, b, 4)
                beat(5)
                act.wait_ge(gsoft_in, after(gsoft_in, b))
                a.activation(gw[:, 1, :], gw[:, 0, :], ACT.Exp).then_inc(gsoft_out, 1)

            def experts(b, e0, e1, beats, beat):
                for e in range(e0, e1):
                    if e in beats:
                        beat(beats[e])
                    act.wait_ge(e_hid, at(e_hid, b, e + 1))
                    if e >= 2:
                        act.wait_ge(e_out, at(e_out, b, e - 1))
                    k = 2 + 2 * (e % 2)
                    a.activation(hexp[:, e % 2, :].rearrange("p (g n) -> p g n", g=2),
                                 ps[:, 512 * k:512 * (k + 2)].rearrange("p (g n) -> p g n", g=2)[:, :, 0:HALF],
                                 ACT.Relu).then_inc(e_relu, 1)

            def moe_b(b):
                copy_turned(coef_turned, coeft_ready, coeft, EXPERTS, b)
                take_root(2, ln2, b, 5)

            def rest(b, t, beat):
                if t == 0:
                    attention(b, 0, beat)
                    attention(b, 1, beat)
                    attention(b, 2, beat)
                elif t == 1:
                    attention(b, 3, beat)
                    attention(b, 4, beat)
                elif t == 2:
                    attention(b, 5, beat)
                    lsh_a(b, beat)
                elif t == 3:
                    lsh_b(b, beat)
                    mlp(b, beat)
                    moe_a(b, beat)
                    experts(b, 0, MID, {1: 6, 3: 7}, beat)
                elif t == 4:
                    experts(b, MID, LATE, {e: e for e in range(MID, LATE)}, beat)
                elif t == 5:
                    experts(b, LATE, EXPERTS, {e: e for e in range(LATE, EXPERTS)}, beat)
                    moe_b(b)

            pipeline(act, stage_a, topk, weigh, kv_final, rest)

        @block.tensor
        def _(pe):
            mm = nc.tensor.matmul
            pe.wait_ge(set_pool, SET_POOL)
            pe.wait_ge(w_loaded, ALL_W)
            pe.wait_ge(set_vec, SET_CONV)
            wqb = ring[0:32, 0, 0:8, :].rearrange("p a b -> p (a b)")
            kyb = ring[0:32, 0, 8:16, :].rearrange("p a b -> p (a b)")
            for g in range(2 * HEADS):
                last = mm(ps[0:C, g * C:(g + 1) * C], wqb[:, g * C:(g + 1) * C], kyb[:, g * C:(g + 1) * C],
                          start=True, stop=True)
                if g == HEADS - 1:
                    last.then_inc(set_pe, 1)
            last.then_inc(set_pe, 1)
            pe.wait_ge(set_act, 1)

            def turn(src, rows_out, done):
                for t in range(NT):
                    last = nc.tensor.transpose(bank(t // 4, P, rows_out, (t % 4) * P), src(t), ident[:, :])
                    if t == 3 or t == NT - 1:
                        last.then_inc(done, 1)

            def stage_a(b, total):
                pe.wait_ge(x_loaded, after(x_loaded, b))
                apart(pe, gate_pe, b)
                turn(lambda t: xrow[:, t, :], P, x_turned)
                pe.wait_ge(xt_ready, after(xt_ready, b))
                apart(pe, gate_pe, b)
                for t in range(NT):
                    o = bank(2, C, P, t * C)
                    for f in range(TAPS):
                        mm(o, xt[:, t * P + f:t * P + f + P], wc[:, f, :], start=(f == 0), stop=False)
                    last = mm(o, ones_row[:, :], bk_row[:, :], start=False, stop=True)
                last.then_inc(conv_done, 1)
                pe.wait_ge(z_ready, after(z_ready, b))
                apart(pe, gate_pe, b)
                turn(lambda t: z[:, t, :], C, z_turned)
                pe.wait_ge(zt_ready, after(zt_ready, b))
                apart(pe, gate_pe, b)
                for r in range(2):
                    for c in range(2):
                        last = mm(bank(2 + 2 * r + c, HALF), wi_aug[:, r * NST:(r + 1) * NST],
                                  zt[:, c * HALF:(c + 1) * HALF], start=True, stop=True)
                last.then_inc(u_done, 1)
                pe.wait_ge(y_ready, after(y_ready, b))
                apart(pe, gate_pe, b)
                for t in range(NT):
                    o = bank(2, C, P, t * C)
                    for r in range(2):
                        mm(o, wide[:, r, t * P:(t + 1) * P], wo_g[:, r, :], start=(r == 0), stop=False)
                    last = mm(o, ones_row[:, :], bo_row[:, :], start=False, stop=True)
                last.then_inc(lru_done, 1)
                pe.wait_ge(n1_ready, after(n1_ready, b))
                apart(pe, gate_pe, b)
                turn(lambda t: z[:, t, :], C, n1_turned)
                pe.wait_ge(n1t_ready, after(n1t_ready, b))
                apart(pe, gate_pe, b)

            def topk(b, t, part):
                if t == NT - 1 and part == 5:
                    pe.wait_ge(tail_chosen, after(tail_chosen, b))
                    apart(pe, gate_pe, b)
                    nc.tensor.transpose(bank(0, P), fpf[:, :, :].rearrange("p h r -> p (h r)"), ident[:, :])
                    nc.tensor.transpose(bank(0, P, P, P), fe[:, :, :].rearrange("p h r -> p (h r)"),
                                        ident[:, :]).then_inc(tail_turned, 1)
                    pe.wait_ge(rows_ready, after(rows_ready, b))
                    apart(pe, gate_pe, b)
                if part > 0:
                    return
                for p in range(2):
                    last = mm(bank(4 + p, 512), n1t[:, t * P:(t + 1) * P], w_sim[:, p * 512:(p + 1) * 512],
                              start=True, stop=True)
                last.then_inc(sims_done, 1)
                pe.wait_ge(sims_copied, at(sims_copied, b, t + 1))
                apart(pe, gate_pe, b)

            def weigh(b, t, h):
                if t < NT - 1:
                    return
                if ranks(t, h):
                    pe.wait_ge(weighed, at(weighed, b, t * HEADS + h + 1))
                    apart(pe, gate_pe, b)
                    for r in range(ranks(t, h)):
                        last = mm(bank(1, SPARE_HEADS, P, (h * TOPK + r) * SPARE_HEADS),
                                  ring[SPARE0:P, (t * HEADS + h) % RING, r, :], spare_of[SPARE0:P, :],
                                  start=True, stop=True)
                    last.then_inc(spare_summed, 1)
                else:
                    pe.wait_ge(spare_copied, after(spare_copied, b))
                    apart(pe, gate_pe, b)
                    for k in range(SPARE_HEADS):
                        last = nc.tensor.transpose(bank(1, P, TAIL, k * P), spare_t[:, k, :], ident[:, :])
                    last.then_inc(spare_turned, 1)
                    pe.wait_ge(spare_in, after(spare_in, b))
                    apart(pe, gate_pe, b)

            def kv_final(b, t0, t1):
                for t in range(t0, t1):
                    for slot in range(RING):
                        pe.wait_ge(ring_free[slot], b * uses(slot, NT) + uses(slot, t + 1) + 1)
                    apart(pe, gate_pe, b)
                    if t >= 2:
                        pe.wait_ge(kt_ready, at(kt_ready, b, t - 1))
                        apart(pe, gate_pe, b)
                    for g in range(HEADS // 2):
                        last = nc.tensor.transpose(bank(t % 2, P, P, g * P), kv[:, t, 0, 2 * g:2 * g + 2, :].rearrange("p h c -> p (h c)"),
                                                   ident[:, :])
                    last.then_inc(k_turned, 1)
                pe.wait_ge(kt_ready, at(kt_ready, b, t1))
                apart(pe, gate_pe, b)

            def attention(b, i, beat):
                n = (i + 1) * P
                beat_at(beat, i, 0)
                if i == 0:
                    pe.wait_ge(c_loaded, after(c_loaded, b))
                    apart(pe, gate_pe, b)
                pe.wait_ge(kt_ready, at(kt_ready, b, i + 1))
                apart(pe, gate_pe, b)
                pe.wait_ge(v_ready, at(v_ready, b, i + 1))
                apart(pe, gate_pe, b)
                if i > 0:
                    pe.wait_ge(ot_ready, at(ot_ready, b, i))
                    apart(pe, gate_pe, b)
                for g in range(HEADS // 2):
                    last = mm(bank(0, P, P, g * P), wq_s[:, g * P:(g + 1) * P], n1tc[0:C, i * P:(i + 1) * P],
                              start=True, stop=True)
                last.then_inc(q_done, 1)
                pe.wait_ge(qt_ready, at(qt_ready, b, i + 1))
                apart(pe, gate_pe, b)

                def scores(h):
                    u = i * HEADS + h
                    if u >= 2:
                        pe.wait_ge(p_ready, at(p_ready, b, u - 1))
                        apart(pe, gate_pe, b)
                    r, g, s = C * (h % 2), h // 2, 2 + 2 * (u % 2)
                    for c0 in range(0, n, 512):
                        c1 = min(n, c0 + 512)
                        mm(bank(s, c1 - c0, P, c0), qt[r:r + C, g, :], kt[r:r + C, g, c0:c1],
                           start=True, stop=False, skip_group_check=True)
                    mm(bank(s, P, P, i * P), ident[:, :], causal[:, :], start=False, stop=True,
                       skip_group_check=True).then_inc(s_done, 1)

                def turn_probs(h):
                    u = i * HEADS + h
                    pe.wait_ge(p_ready, at(p_ready, b, u + 1))
                    apart(pe, gate_pe, b)
                    if u >= 1:
                        pe.wait_ge(pt_ready, at(pt_ready, b, u))
                        apart(pe, gate_pe, b)
                    for j in range(i + 1):
                        last = nc.tensor.transpose(bank(0, P, P, j * P), prob[:, u % 2, j * P:(j + 1) * P],
                                                   ident[:, :])
                    last.then_inc(p_turned, 1)

                def values(h):
                    u = i * HEADS + h
                    pe.wait_ge(pt_ready, at(pt_ready, b, u + 1))
                    apart(pe, gate_pe, b)
                    for j in range(i + 1):
                        last = mm(bank(6, C, P, h * C), probt[:, u % 2, j * P:(j + 1) * P], v[:, j, h, :],
                                  start=(j == 0), stop=(j == i))
                    last.then_inc(o_done, 1)

                scores(0)
                if i >= 1:
                    pe.wait_ge(on_ready, at(on_ready, b, i))
                    apart(pe, gate_pe, b)
                for h in range(HEADS):
                    if h > 0:
                        beat_at(beat, i, h)
                    if h + 1 < HEADS:
                        scores(h + 1)
                    turn_probs(h)
                    if h >= 1:
                        values(h - 1)
                values(HEADS - 1)
                pe.wait_ge(on_ready, at(on_ready, b, i + 1))
                apart(pe, gate_pe, b)
                for g in range(HEADS // 2):
                    last = nc.tensor.transpose(bank(0, P, P, g * P), on[:, g * P:(g + 1) * P], ident[:, :])
                last.then_inc(on_turned, 1)
                pe.wait_ge(ot_ready, at(ot_ready, b, i + 1))
                apart(pe, gate_pe, b)
                for g in range(HEADS // 2):
                    last = mm(bank(7, C, P, i * C), ot[:, g, :], wo_f[:, g, :], start=(g == 0),
                              stop=(g == HEADS // 2 - 1))
                if i == NT - 1:
                    last.then_inc(ffn_done, 1)

            def lsh_a(b, beat):
                pe.wait_ge(xh_ready, after(xh_ready, b))
                apart(pe, gate_pe, b)
                turn(lambda t: xh[:, t, 0:C], C, lt_turned)
                pe.wait_ge(lt_ready, at(lt_ready, b, 2))
                apart(pe, gate_pe, b)
                for t in range(NT):
                    last = mm(bank(4, 16, P, t * 16), lt[0:C, t * P:(t + 1) * P], rot_s[:, :], start=True, stop=True)
                last.then_inc(rot_done, 1)
                pe.wait_ge(oneh_ready, after(oneh_ready, b))
                apart(pe, gate_pe, b)
                for t in range(NT):
                    last = mm(bank(5, C + 1, M_LSH), oneh[:, t, :, :].rearrange("p i j -> p (i j)"), xh[:, t, :],
                              start=(t == 0), stop=(t == NT - 1))
                last.then_inc(pooled, 1)
                for c in range(2):
                    last = mm(bank(2 + c, HALF, C), qw_s[:, :], lt[0:C, c * HALF:(c + 1) * HALF],
                              start=True, stop=True)
                last.then_inc(lq_done, 1)
                pe.wait_ge(pool_ready, after(pool_ready, b))
                apart(pe, gate_pe, b)
                nc.tensor.transpose(bank(5, M_LSH, C + 1), pool_s[:, :], ident[0:M_LSH, 0:M_LSH]
                                    ).then_inc(rp_turned, 1)
                pe.wait_ge(rpt_ready, after(rpt_ready, b))
                apart(pe, gate_pe, b)
                mm(bank(5, M_LSH, C), kvw_s[:, 0:C], rpt[0:C, :], start=True, stop=True)
                mm(bank(6, C), rpt4[:, :, :].rearrange("c a m -> c (a m)"), kvw_s[:, C:2 * C],
                   start=True, stop=True).then_inc(kvl_done, 1)
                pe.wait_ge(kbd_ready, after(kbd_ready, b))
                apart(pe, gate_pe, b)
                pe.wait_ge(lqt_ready, after(lqt_ready, b))
                apart(pe, gate_pe, b)

            def lsh_b(b, beat):
                def logits(t):
                    if t >= 2:
                        pe.wait_ge(lmax_ready, at(lmax_ready, b, t - 1))
                        apart(pe, gate_pe, b)
                    mm(bank(4 + t % 2, HEADS * M_LSH), lqt[:, t * P:(t + 1) * P],
                       kbd[:, :, :].rearrange("c h m -> c (h m)"), start=True, stop=True
                       ).then_inc(logit_done, 1)

                beat(0)
                logits(0)
                for t in range(NT):
                    if t + 1 < NT:
                        logits(t + 1)
                    pe.wait_ge(lexp_ready, at(lexp_ready, b, t + 1))
                    apart(pe, gate_pe, b)
                    for g in range(2):
                        last = nc.tensor.transpose(bank(0, P, P, g * P), prob[:, 0, g * P:(g + 1) * P], ident[:, :])
                    last.then_inc(lp_turned, 1)
                    pe.wait_ge(lpt_ready, at(lpt_ready, b, t + 1))
                    apart(pe, gate_pe, b)
                    for g in range(2):
                        last = mm(bank(6, C, P, t * C), lpt[:, g, :], vbd[:, g, :], start=(g == 0), stop=(g == 1))
                    last.then_inc(lo_done, 1)

            def mlp(b, beat):
                pe.wait_ge(y2_ready, after(y2_ready, b))
                apart(pe, gate_pe, b)
                turn(lambda t: tmp[:, t, :], C, lt_turned)
                pe.wait_ge(lt_ready, at(lt_ready, b, 4))
                apart(pe, gate_pe, b)
                for f in range(2):
                    for c in range(2):
                        last = mm(bank(2 + 2 * f + c, HALF), fc1_s[:, f * P:(f + 1) * P],
                                  lt[0:C, c * HALF:(c + 1) * HALF], start=True, stop=True)
                    last.then_inc(fc1_done, 1)
                pe.wait_ge(hid_ready, after(hid_ready, b))
                apart(pe, gate_pe, b)
                for t in range(NT):
                    for f in range(2):
                        mm(bank(6, C, P, t * C), hidden[:, f, t * P:(t + 1) * P], fc2_s[:, f, :],
                           start=(f == 0), stop=False)
                    last = mm(bank(6, C, P, t * C), ones_row[:, :], fc2b_row[:, :], start=False, stop=True)
                last.then_inc(fc2_done, 1)

            def moe_a(b, beat):
                pe.wait_ge(n3_ready, after(n3_ready, b))
                apart(pe, gate_pe, b)
                turn(lambda t: n2[:, t, :], C, lt_turned)
                pe.wait_ge(lt_ready, at(lt_ready, b, 6))
                apart(pe, gate_pe, b)
                for t in range(NT):
                    last = mm(bank(7, EXPERTS, P, t * EXPERTS), lt[:, t * P:(t + 1) * P], gate_aug[:, :],
                              start=True, stop=True)
                last.then_inc(gate_done, 1)

            def experts(b, e0, e1, beats, beat):
                def expert_in(e):
                    if e >= 2:
                        pe.wait_ge(e_relu, at(e_relu, b, e - 1))
                        apart(pe, gate_pe, b)
                    for c in range(2):
                        last = mm(bank(2 + 2 * (e % 2) + c, HALF), w1_aug[:, e, :],
                                  lt[:, c * HALF:(c + 1) * HALF], start=True, stop=True)
                    last.then_inc(e_hid, 1)

                if e0 in beats:
                    beat(beats[e0])
                expert_in(e0)
                for e in range(e0, e1):
                    if e in beats and e > e0:
                        beat(beats[e])
                    if e + 1 < e1:
                        expert_in(e + 1)
                    pe.wait_ge(e_relu, at(e_relu, b, e + 1))
                    apart(pe, gate_pe, b)
                    if e == 1:
                        pe.wait_ge(gsoft_in, after(gsoft_in, b))
                        apart(pe, gate_pe, b)
                    if e >= 2:
                        pe.wait_ge(e_used, at(e_used, b, e - 1))
                        apart(pe, gate_pe, b)
                    for t in range(NT):
                        last = mm(bank(6 + e % 2, C, P, t * C), hexp[:, e % 2, t * P:(t + 1) * P], w2_s[:, e, :],
                                  start=True, stop=True)
                    last.then_inc(e_out, 1)

            def moe_b(b):
                pe.wait_ge(coef_ready, after(coef_ready, b))
                apart(pe, gate_pe, b)
                for t in range(NT):
                    last = nc.tensor.transpose(bank(t // 4, P, EXPERTS, (t % 4) * P), coef[:, t, :], ident[:, :])
                    if t == 3 or t == NT - 1:
                        last.then_inc(coef_turned, 1)
                pe.wait_ge(coeft_ready, after(coeft_ready, b))
                apart(pe, gate_pe, b)
                pe.wait_ge(e_used, at(e_used, b, EXPERTS - 1))
                apart(pe, gate_pe, b)
                for t in range(NT):
                    last = mm(bank(6, C, P, t * C), coeft[:, t * P:(t + 1) * P], b2_row[:, :], start=True, stop=True)
                last.then_inc(eb_out, 1)

            def rest(b, t, beat):
                if t == 0:
                    attention(b, 0, beat)
                    attention(b, 1, beat)
                    attention(b, 2, beat)
                elif t == 1:
                    attention(b, 3, beat)
                    attention(b, 4, beat)
                elif t == 2:
                    attention(b, 5, beat)
                    lsh_a(b, beat)
                elif t == 3:
                    lsh_b(b, beat)
                    mlp(b, beat)
                    moe_a(b, beat)
                    experts(b, 0, MID, {1: 6, 3: 7}, beat)
                elif t == 4:
                    experts(b, MID, LATE, {e: e for e in range(MID, LATE)}, beat)
                elif t == 5:
                    experts(b, LATE, EXPERTS, {e: e for e in range(LATE, EXPERTS)}, beat)
                    moe_b(b)

            pipeline(pe, stage_a, topk, weigh, kv_final, rest)

        @block.vector
        def _(dve):
            vv = nc.vector
            TT, TS, STT = vv.tensor_tensor, vv.tensor_scalar, vv.scalar_tensor_tensor
            zeroed = [0]

            def first(ins):
                ins.then_inc(set_vec, 1)
                zeroed[0] += 1

            first(vv.memset(xrow[:, :, :], 0.0))
            assert zeroed[0] == SET_ZEROED
            first(vv.memset(xt[:, :], 0.0))
            first(vv.memset(ones_row[:, :], 1.0))
            first(vv.memset(zt[C:C + 1, :], 1.0))
            first(vv.memset(lt[C:C + 1, :], 1.0))
            first(vv.memset(xh[:, :, C:C + 1], 1.0))
            first(vv.memset(kv[:, NT - 1, :, :, :], 0.0))
            dve.wait_ge(w_loaded, ALL_W)
            first(TT(wc[:, :, :], wc[:, :, :], filt_c[:, :].unsqueeze(2).to_broadcast([P, TAPS, C]), ALU.mult))
            assert zeroed[0] == SET_CONV, zeroed[0]
            dve.wait_ge(set_pool, SET_POOL)

            def exact_exp(dst, src, a, n, r, p, whole):
                first(TS(n, src, 1.0 / math.log(2.0), ROUND, ALU.mult, ALU.add))
                dve.wait_ge(set_vec, zeroed[0])
                first(TS(n, n, -ROUND, None, ALU.add))
                dve.wait_ge(set_vec, zeroed[0])
                first(STT(out=r, in0=n, scalar=-0.693359375, in1=src, op0=ALU.mult, op1=ALU.add))
                dve.wait_ge(set_vec, zeroed[0])
                first(STT(out=r, in0=n, scalar=2.12194440e-4, in1=r, op0=ALU.mult, op1=ALU.add))
                dve.wait_ge(set_vec, zeroed[0])
                first(TS(p, r, 1.0 / math.factorial(8), 1.0 / math.factorial(7), ALU.mult, ALU.add))
                for k in range(6, -1, -1):
                    dve.wait_ge(set_vec, zeroed[0])
                    first(TT(p, p, r, ALU.mult))
                    dve.wait_ge(set_vec, zeroed[0])
                    first(TS(p, p, 1.0 / math.factorial(k), None, ALU.add))
                first(TS(n, n, 127.0, 8388608.0, ALU.add, ALU.mult))
                dve.wait_ge(set_vec, zeroed[0])
                first(vv.tensor_copy(whole, n))
                dve.wait_ge(set_vec, zeroed[0])
                first(TT(dst, p, whole.bitcast(F32), ALU.mult))
                dve.wait_ge(set_vec, zeroed[0])

            exact_exp(lam[:, 0:3], logs[:, :], None, small[:, 0:3], small[:, 3:6], small[:, 6:9], small_i[:, 0:3])
            first(TS(small[:, 9:10], lam[:, 0:1], -1.0, None, ALU.mult))
            dve.wait_ge(set_vec, zeroed[0])
            exact_exp(lam[:, 3:4], small[:, 9:10], None, small[:, 0:1], small[:, 3:4], small[:, 6:7],
                      small_i[:, 0:1])
            hi, lo = small[:, 10:11], small[:, 11:12]
            HI_ROUND = 1.5 * 2.0 ** 11
            first(TS(hi, lam[:, 1:2], 1.0 / TWO_PI, HI_ROUND, ALU.mult, ALU.add))
            dve.wait_ge(set_vec, zeroed[0])
            first(TS(hi, hi, -HI_ROUND, None, ALU.add))
            dve.wait_ge(set_vec, zeroed[0])
            first(STT(out=lo, in0=hi, scalar=-6.28125, in1=lam[:, 1:2], op0=ALU.mult, op1=ALU.add))
            dve.wait_ge(set_vec, zeroed[0])
            first(STT(out=lo, in0=hi, scalar=-(TWO_PI - 6.28125), in1=lo, op0=ALU.mult, op1=ALU.add))
            dve.wait_ge(set_vec, zeroed[0])
            first(TS(lo, lo, 1.0 / TWO_PI, None, ALU.mult))
            dve.wait_ge(set_vec, zeroed[0])

            def to_turn(dst, scratch):
                first(TS(scratch, dst, ROUND, None, ALU.add))
                dve.wait_ge(set_vec, zeroed[0])
                first(TS(scratch, scratch, -ROUND, None, ALU.add))
                dve.wait_ge(set_vec, zeroed[0])
                first(TT(dst, dst, scratch, ALU.subtract))
                dve.wait_ge(set_vec, zeroed[0])

            w0, w1_, w2_ = wide[:, 0, :], wide[:, 1, :], wide[:, 2, :]
            first(TS(w0, cos_t[:, :], hi, None, ALU.mult))
            dve.wait_ge(set_vec, zeroed[0])
            to_turn(w0, w2_)
            first(STT(out=sin_t[:, :], in0=cos_t[:, :], scalar=lo, in1=w0, op0=ALU.mult, op1=ALU.add))
            dve.wait_ge(set_vec, zeroed[0])
            to_turn(sin_t[:, :], w2_)
            first(TS(cos_t[:, :], sin_t[:, :], 0.25, None, ALU.add))
            dve.wait_ge(set_vec, zeroed[0])
            to_turn(cos_t[:, :], w2_)
            first(TS(wo_g[:, :, :], wo_g[:, :, :], lam[:, 2:3], None, ALU.mult))
            assert zeroed[0] == SET_VEC, zeroed[0]
            for s in ring_free:
                dve.sem_inc(s, 1)

            va = Steps(vec_a, STEPS["vec_a"])
            vt = Steps(vec_t, STEPS["vec_t"])
            vc = Steps(vec_c, STEPS["vec_c"])

            def norm(st, x_in, xo, sq, buf, i, n, b):
                vv.tensor_reduce(buf[:, 0, :], x_in, AX.X, ALU.add).then_inc(st.sem, st.up())
                dve.wait_ge(st.sem, st.now())
                TS(buf[:, 0, :], buf[:, 0, :], -1.0 / C, None, ALU.mult).then_inc(st.sem, st.up())
                dve.wait_ge(st.sem, st.now())
                TT(xo, x_in, buf[:, 0, :].unsqueeze(2).to_broadcast([P, NT, C]), ALU.add).then_inc(st.sem, st.up())
                dve.wait_ge(st.sem, st.now())
                TT(sq, xo, xo, ALU.mult).then_inc(st.sem, st.up())
                dve.wait_ge(st.sem, st.now())
                vv.tensor_reduce(buf[:, 1, :], sq, AX.X, ALU.add).then_inc(st.sem, st.up())
                dve.wait_ge(st.sem, st.now())
                TS(buf[:, 1, :], buf[:, 1, :], 1.0 / C, EPS, ALU.mult, ALU.add).then_inc(std[i], 1)
                dve.wait_ge(root[i], at(root[i], b, n))
                vv.reciprocal(buf[:, 3, :], buf[:, 2, :]).then_inc(st.sem, st.up())
                dve.wait_ge(st.sem, st.now())
                return TT(xo, xo, buf[:, 3, :].unsqueeze(2).to_broadcast([P, NT, C]), ALU.mult)

            def stage_a(b, total):
                va.begin(b)
                sq = wide[:, 5, 0:NT * C].rearrange("p (t c) -> p t c", c=C)
                dve.wait_ge(h0_ready, after(h0_ready, b))
                norm(va, h0[:, :, :], z[:, :, :], sq, lnv, 0, 1, b).then_inc(z_ready, 1)
                total(4)
                dve.wait_ge(u_done, after(u_done, b))
                halves = lambda x: x.rearrange("p (g n) -> p g n", g=2)
                ur = halves(ps[:, 1024:2048])[:, :, 0:HALF]
                ui = halves(ps[:, 2048:3072])[:, :, 0:HALF]
                cos_h, sin_h = halves(cos_t[:, :]), halves(sin_t[:, :])
                w = [wide[:, k, :] for k in range(6)]
                if is_first(b):
                    dve.wait_ge(set_act, 3)
                TT(halves(w[2]), ur, cos_h, ALU.mult).then_inc(vec_a, va.up())
                TT(halves(w[3]), ui, sin_h, ALU.mult).then_inc(vec_a, va.up())
                TT(halves(w[4]), ui, cos_h, ALU.mult).then_inc(vec_a, va.up())
                TT(halves(w[5]), ur, sin_h, ALU.mult).then_inc(vec_a, va.up())
                dve.wait_ge(vec_a, va.now())
                TT(w[2], w[2], w[3], ALU.add).then_inc(vec_a, va.up())
                TT(w[4], w[4], w[5], ALU.subtract).then_inc(vec_a, va.up())
                dve.wait_ge(vec_a, va.now())
                decay = lam[:, 3:4].to_broadcast([P, NP_])
                vv.tensor_tensor_scan(w[3], decay, w[2], 0.0, ALU.mult, ALU.add).then_inc(vec_a, va.up())
                vv.tensor_tensor_scan(w[5], decay, w[4], 0.0, ALU.mult, ALU.add).then_inc(vec_a, va.up())
                dve.wait_ge(vec_a, va.now())
                TT(w[0], w[3], cos_t[:, :], ALU.mult).then_inc(vec_a, va.up())
                TT(w[2], w[5], sin_t[:, :], ALU.mult).then_inc(vec_a, va.up())
                TT(w[1], w[3], sin_t[:, :], ALU.mult).then_inc(vec_a, va.up())
                TT(w[4], w[5], cos_t[:, :], ALU.mult).then_inc(vec_a, va.up())
                dve.wait_ge(vec_a, va.now())
                TT(w[0], w[0], w[2], ALU.subtract).then_inc(vec_a, va.up())
                TT(w[1], w[1], w[4], ALU.add).then_inc(y_ready, 1)
                total(5)
                dve.wait_ge(lru_done, after(lru_done, b))
                if not is_first(b):
                    dve.wait_ge(a_stored, after(a_stored, b - 1))
                TT(h1a[:, :, :], h0[:, :, :], bank(2, NT * C).rearrange("p (t c) -> p t c", c=C),
                   ALU.add).then_inc(h1_ready, 1)
                dve.wait_ge(h1_ready, after(h1_ready, b))
                norm(va, h1a[:, :, :], z[:, :, :], sq, lnv, 1, 1, b).then_inc(n1_ready, 1)
                total(6)
                total(7)
                va.end()

            def top_keys(b, t):
                vt.begin(b, t * TILE_STEPS)
                dve.wait_ge(sims_copied, at(sims_copied, b, t + 1))
                apart(dve, gate_vec, b)
                sims = [trest[:, g, :] for g in range(2 * HEADS)]
                for g in range(2 * HEADS):
                    vv.max(tv[:, g, 0:8], sims[g]).then_inc(vec_t, vt.up())
                dve.wait_ge(vec_t, vt.now())
                apart(dve, gate_vec, b)
                for g in range(2 * HEADS):
                    vv.max_index(ti[:, g, 0:8], tv[:, g, 0:8], sims[g]).then_inc(vec_t, vt.up())
                dve.wait_ge(vec_t, vt.now())
                apart(dve, gate_vec, b)
                for g in range(2 * HEADS):
                    vv.match_replace(trest[:, g, :], tv[:, g, 0:8], sims[g], LOWEST).then_inc(vec_t, vt.up())

            def next_keys(b, t):
                dve.wait_ge(vec_t, vt.now())
                apart(dve, gate_vec, b)
                for g in range(2 * HEADS):
                    vv.max(tv[:, g, 8:16], trest[:, g, :]).then_inc(vec_t, vt.up())
                dve.wait_ge(vec_t, vt.now())
                apart(dve, gate_vec, b)
                for g in range(2 * HEADS):
                    vv.max_index(ti[:, g, 8:16], tv[:, g, 8:16], trest[:, g, :]).then_inc(vec_t, vt.up())
                dve.wait_ge(vec_t, vt.now())
                vv.tensor_copy(tif[:, :, :], ti[:, :, :]).then_inc(vec_t, vt.up())
                dve.wait_ge(vec_t, vt.now())
                TS(tif[:, HEADS:2 * HEADS, :], tif[:, HEADS:2 * HEADS, :], float(NKEY), None,
                   ALU.mult).then_inc(vec_t, vt.up())
                dve.wait_ge(vec_t, vt.now())
                for dst, src in ((cs, tv), (ci, tif)):
                    for a0, na, ln in CAND_RUNS:
                        off = CAND_OFF[a0]
                        TT(dst[:, :, off:off + na * ln].rearrange("p h (a l) -> p h a l", l=ln),
                                   src[:, 0:HEADS, a0:a0 + na].unsqueeze(3).to_broadcast([P, HEADS, na, ln]),
                                   src[:, HEADS:2 * HEADS, 0:ln].unsqueeze(2).to_broadcast([P, HEADS, na, ln]),
                                   ALU.add).then_inc(vec_t, vt.up())

            def top_pairs(b, t):
                dve.wait_ge(vec_t, vt.now())
                apart(dve, gate_vec, b)
                for h in range(HEADS):
                    vv.max(fs[:, h, 0:8], cs[:, h, :]).then_inc(vec_t, vt.up())
                dve.wait_ge(vec_t, vt.now())
                apart(dve, gate_vec, b)
                for h in range(HEADS):
                    vv.max_index(fp[:, h, 0:8], fs[:, h, 0:8], cs[:, h, :]).then_inc(vec_t, vt.up())
                dve.wait_ge(vec_t, vt.now())
                apart(dve, gate_vec, b)
                for h in range(HEADS):
                    vv.match_replace(cs[:, h, :], fs[:, h, 0:8], cs[:, h, :], LOWEST).then_inc(vec_t, vt.up())
                dve.wait_ge(vec_t, vt.now())
                apart(dve, gate_vec, b)
                for h in range(HEADS):
                    vv.max(fs[:, h, 8:16], cs[:, h, :]).then_inc(vec_t, vt.up())
                dve.wait_ge(vec_t, vt.now())
                apart(dve, gate_vec, b)
                for h in range(HEADS):
                    vv.max_index(fp[:, h, 8:16], fs[:, h, 8:16], cs[:, h, :]).then_inc(vec_t, vt.up())
                TT(fe[:, :, :], fs[:, :, :], fs[:, :, 0:1].to_broadcast([P, HEADS, TOPK]),
                   ALU.subtract).then_inc(soft_in, 1)
                dve.wait_ge(soft_in, at(soft_in, b, t + 1))
                vv.tensor_copy(fpf[:, :, :], fp[:, :, :]).then_inc(vec_t, vt.up())
                dve.wait_ge(vec_t, vt.now())
                TS(fpf[:, :, :], fpf[:, :, :], SPREAD, None, ALU.mult).then_inc(vec_t, vt.up())
                TT(ci[:, :, :], ci[:, :, :], iota_c[:, :].unsqueeze(1).to_broadcast([P, HEADS, NCAND]),
                   ALU.add).then_inc(vec_t, vt.up())
                dve.wait_ge(vec_t, vt.now())

            def row_numbers(k):
                HH = HEADS // 2
                oh = onehot.rearrange("p (h r c) -> p h r c", h=HH, c=NCAND)
                hs = slice(k * HH, (k + 1) * HH)
                TT(oh, fpf[:, hs, :].unsqueeze(3).to_broadcast([P, HH, TOPK, NCAND]),
                   ci[:, hs, :].unsqueeze(2).to_broadcast([P, HH, TOPK, NCAND]),
                   ALU.subtract).then_inc(vec_t, vt.up())
                dve.wait_ge(vec_t, vt.now())
                vv.tensor_reduce(fpf[:, hs, :], oh, AX.X, ALU.min, apply_absolute_value=True
                                 ).then_inc(vec_t, vt.up())
                dve.wait_ge(vec_t, vt.now())

            def rows_out(b, t):
                TT(fpf[:, :, :], fpf[:, :, :], head_base[:, :].unsqueeze(2).to_broadcast([P, HEADS, TOPK]),
                   ALU.add).then_inc(vec_t, vt.up())
                dve.wait_ge(vec_t, vt.now())
                dve.wait_ge(soft_exp, at(soft_exp, b, t + 1))
                vv.tensor_reduce(fsum[:, 0, :], fe[:, :, :], AX.X, ALU.add).then_inc(vec_t, vt.up())
                dve.wait_ge(vec_t, vt.now())
                vv.reciprocal(fsum[:, 1, :], fsum[:, 0, :]).then_inc(vec_t, vt.up())
                dve.wait_ge(vec_t, vt.now())
                if t == NT - 1:
                    TT(fe[:, :, :], fe[:, :, :], fsum[:, 1, :].unsqueeze(2).to_broadcast([P, HEADS, TOPK]),
                       ALU.mult).then_inc(tail_chosen, 1)
                    flat_rows = fpf[0:TAIL, :, :].rearrange("p h r -> p (h r)")
                    flat_w = fe[0:TAIL, :, :].rearrange("p h r -> p (h r)")
                    dve.wait_ge(tail_turned, after(tail_turned, b))
                    vv.tensor_copy(row_i[SPARE0:P, t, 0:TAIL], bank(0, P)[SPARE0:P, 0:TAIL]
                                   ).then_inc(vec_t, vt.up())
                    vv.tensor_copy(row_w[SPARE0:P, t, 0:TAIL], bank(0, P, P, P)[SPARE0:P, 0:TAIL]
                                   ).then_inc(vec_t, vt.up())
                    dve.wait_ge(vec_t, vt.now())
                    vv.tensor_copy(row_w[0:TAIL, t, 0:TAIL], flat_w[:, 0:TAIL]).then_inc(vec_t, vt.up())
                    vv.tensor_copy(row_i[0:TAIL, t, 0:TAIL], flat_rows[:, 0:TAIL]).then_inc(rows_ready, 1)
                    vt.end()
                    return
                TT(row_w[:, t, :].rearrange("p (h r) -> p h r", r=TOPK), fe[:, :, :],
                           fsum[:, 1, :].unsqueeze(2).to_broadcast([P, HEADS, TOPK]), ALU.mult).then_inc(vec_t, vt.up())
                vv.tensor_copy(row_i[:, t, :], fpf[:, :, :].rearrange("p h r -> p (h r)")
                               ).then_inc(rows_ready, 1)
                assert vt.n == (t + 1) * TILE_STEPS

            def topk(b, t, part):
                if part == 1:
                    top_keys(b, t)
                elif part == 2:
                    next_keys(b, t)
                elif part == 3:
                    top_pairs(b, t)
                elif part == 4:
                    row_numbers(0)
                elif part == 5:
                    row_numbers(1)
                    rows_out(b, t)

            def weigh(b, t, h):
                if t == 0 and h == 0 and not is_first(b):
                    dve.wait_ge(k_turned, after(k_turned, b - 1))
                    dve.wait_ge(v_ready, after(v_ready, b - 1))
                if not ranks(t, h):
                    dve.wait_ge(spare_turned, after(spare_turned, b))
                    for k in range(SPARE_HEADS):
                        dst = kv[0:TAIL, t, :, DIRECT + k, :]
                        src = bank(1, P, TAIL, k * P).rearrange("p (k c) -> p k c", k=2)
                        if ranks(t, DIRECT + k):
                            dve.wait_ge(ring_free[(t * HEADS + DIRECT + k) % RING],
                                        b * uses((t * HEADS + DIRECT + k) % RING, NT)
                                        + uses((t * HEADS + DIRECT + k) % RING, NT) + 1)
                            TT(dst, dst, src, ALU.add).then_inc(vec_s, 1)
                        else:
                            vv.tensor_copy(dst, src).then_inc(spare_in, 1)
                    return
                dve.wait_ge(weighed, at(weighed, b, t * HEADS + h + 1))
                if t == NT - 1:
                    dve.wait_ge(spare_summed, at(spare_summed, b, h + 1))
                slot = (t * HEADS + h) % RING
                vv.tensor_reduce(kv[:, t, :, h, :], ring[:, slot, :, :].rearrange("p r (k c) -> p k c r", k=2)[:, :, :, 0:ranks(t, h)],
                                 AX.X, ALU.add).then_inc(ring_free[slot], 1)

            def attention(b, i, beat):
                n = (i + 1) * P
                if i == 0:
                    vc.begin(b)
                for h in range(HEADS):
                    beat_at(beat, i, h)
                    u = i * HEADS + h
                    dve.wait_ge(s_done, at(s_done, b, u + 1))
                    vv.tensor_reduce(nmax[:, h:h + 1], bank(2 + 2 * (u % 2), n), AX.X, ALU.max, negate=True
                                     ).then_inc(max_ready, 1)
                dve.wait_ge(p_ready, at(p_ready, b, (i + 1) * HEADS))
                vv.reciprocal(rinv[:, :], rsum[:, :]).then_inc(vec_c, vc.up())
                dve.wait_ge(vec_c, vc.now())
                dve.wait_ge(o_done, at(o_done, b, (i + 1) * HEADS))
                if i > 0:
                    dve.wait_ge(on_turned, at(on_turned, b, i))
                TT(on[:, :].rearrange("p (h c) -> p h c", c=C), bank(6, 512).rearrange("p (h c) -> p h c", c=C),
                   rinv[:, :].unsqueeze(2).to_broadcast([P, HEADS, C]), ALU.mult).then_inc(on_ready, 1)

            tiles = lambda x: x.rearrange("p (t c) -> p t c", c=C)

            def lsh_a(b, beat):
                beat(4)
                dve.wait_ge(ffn_done, after(ffn_done, b))
                vv.memset(lqt[C:C + 1, :], 1.0).then_inc(vec_c, vc.up())
                TT(h1c[:, :, :], h1c[:, :, :], tiles(bank(7, NT * C)), ALU.add).then_inc(vec_c, vc.up())
                dve.wait_ge(vec_c, vc.now())
                norm(vc, h1c[:, :, :], n2[:, :, :], sq2[:, :, :], ln2, 2, 1, b).then_inc(vec_c, vc.up())
                dve.wait_ge(vec_c, vc.now())
                norm(vc, n2[:, :, :], xh[:, :, 0:C], sq2[:, :, :], ln2, 2, 2, b).then_inc(vec_c, vc.up())
                dve.wait_ge(vec_c, vc.now())
                TT(xh[:, :, 0:C], xh[:, :, 0:C], n1gb[:, 0:1, :].to_broadcast([P, NT, C]), ALU.mult).then_inc(vec_c, vc.up())
                dve.wait_ge(vec_c, vc.now())
                TT(xh[:, :, 0:C], xh[:, :, 0:C], n1gb[:, 1:2, :].to_broadcast([P, NT, C]), ALU.add
                   ).then_inc(xh_ready, 1)
                beat(5)
                dve.wait_ge(rot_done, after(rot_done, b))
                rp = bank(4, NT * 16).rearrange("p (t i j) -> p t i j", t=NT, j=BUCKETS // 2)
                vv.tensor_copy(rots[:, :, :, 0:4], rp).then_inc(vec_c, vc.up())
                TS(rots[:, :, :, 4:8], rp, -1.0, None, ALU.mult).then_inc(vec_c, vc.up())
                dve.wait_ge(vec_c, vc.now())
                vv.tensor_reduce(rmx[:, :, :], rots[:, :, :, :], AX.X, ALU.max).then_inc(vec_c, vc.up())
                dve.wait_ge(vec_c, vc.now())
                full = [P, NT * HASHES, BUCKETS]
                r3 = rots[:, :, :, :].rearrange("p t i j -> p (t i) j")
                o3 = oneh[:, :, :, :].rearrange("p t i j -> p (t i) j")
                m3 = rmx[:, :, :].rearrange("p t i -> p (t i)").unsqueeze(2).to_broadcast(full)
                k3 = rank8[:, :].unsqueeze(1).to_broadcast(full)
                TT(o3, r3, m3, ALU.is_equal).then_inc(vec_c, vc.up())
                dve.wait_ge(vec_c, vc.now())
                TT(r3, o3, k3, ALU.mult).then_inc(vec_c, vc.up())
                dve.wait_ge(vec_c, vc.now())
                vv.tensor_reduce(rmx[:, :, :], rots[:, :, :, :], AX.X, ALU.max).then_inc(vec_c, vc.up())
                dve.wait_ge(vec_c, vc.now())
                TT(o3, r3, m3, ALU.is_equal).then_inc(vec_c, vc.up())
                dve.wait_ge(vec_c, vc.now())
                TT(oneh[:, NT - 1, :, :], oneh[:, NT - 1, :, :],
                   valid[:, NT - 1:NT].unsqueeze(2).to_broadcast([P, HASHES, BUCKETS]), ALU.mult
                   ).then_inc(oneh_ready, 1)
                beat(6)
                dve.wait_ge(pooled, after(pooled, b))
                cnt = bank(5, 1, M_LSH, C)
                TS(pinv[:, 0:1], cnt, 1e-20, None, ALU.add).then_inc(vec_c, vc.up())
                TS(pool_s[:, C:C + 1], cnt, 1.0, NEG, ALU.is_lt, ALU.mult).then_inc(vec_c, vc.up())
                dve.wait_ge(vec_c, vc.now())
                vv.reciprocal(pinv[:, 1:2], pinv[:, 0:1]).then_inc(vec_c, vc.up())
                dve.wait_ge(vec_c, vc.now())
                TS(pool_s[:, 0:C], bank(5, C, M_LSH), pinv[:, 1:2], None, ALU.mult).then_inc(pool_ready, 1)
                dve.wait_ge(rpt_ready, after(rpt_ready, b))
                vv.tensor_copy(kbd[C:C + 1, :, :],
                                       rpt[C:C + 1, :].unsqueeze(1).to_broadcast([1, HEADS, M_LSH])).then_inc(vec_c, vc.up())
                dve.wait_ge(kvl_done, after(kvl_done, b))
                TT(kbd[0:C, :, :], bank(5, M_LSH, C).unsqueeze(1).to_broadcast([C, HEADS, M_LSH]),
                           head_mask[:, :].unsqueeze(2).to_broadcast([C, HEADS, M_LSH]), ALU.mult).then_inc(vec_c, vc.up())
                TT(vbd[:, :, :], bank(6, C).unsqueeze(1).to_broadcast([P, 2, C]), v_mask[:, :, :], ALU.mult
                   ).then_inc(kbd_ready, 1)
                beat(7)

            def lsh_b(b, beat):
                for t in range(NT):
                    if t % 2 == 0:
                        beat(t // 2)
                    dve.wait_ge(logit_done, at(logit_done, b, t + 1))
                    lg = bank(4 + t % 2, HEADS * M_LSH).rearrange("p (h m) -> p h m", m=M_LSH)
                    vv.tensor_reduce(lmx[:, 0, :], lg, AX.X, ALU.max).then_inc(vec_c, vc.up())
                    dve.wait_ge(vec_c, vc.now())
                    if t >= 1:
                        dve.wait_ge(lp_turned, at(lp_turned, b, t))
                    TT(lp, lg, lmx[:, 0, :].unsqueeze(2).to_broadcast([P, HEADS, M_LSH]), ALU.subtract
                       ).then_inc(lmax_ready, 1)
                    dve.wait_ge(lexp_ready, at(lexp_ready, b, t + 1))
                    vv.tensor_reduce(lmx[:, 1, :], lp, AX.X, ALU.add).then_inc(vec_c, vc.up())
                    dve.wait_ge(vec_c, vc.now())
                    vv.reciprocal(lmx[:, 2, :], lmx[:, 1, :]).then_inc(vec_c, vc.up())
                    dve.wait_ge(vec_c, vc.now())
                    dve.wait_ge(lo_done, at(lo_done, b, t + 1))
                    TT(tmp[:, t, :].rearrange("p (h d) -> p h d", d=DH_LSH),
                               bank(6, C, P, t * C).rearrange("p (h d) -> p h d", d=DH_LSH),
                               lmx[:, 2, :].unsqueeze(2).to_broadcast([P, HEADS, DH_LSH]), ALU.mult).then_inc(vec_c, vc.up())

            def mlp(b, beat):
                dve.wait_ge(vec_c, vc.now())
                TT(n2[:, :, :], n2[:, :, :], tmp[:, :, :], ALU.add).then_inc(vec_c, vc.up())
                dve.wait_ge(vec_c, vc.now())
                norm(vc, n2[:, :, :], tmp[:, :, :], sq2[:, :, :], ln2, 2, 3, b).then_inc(vec_c, vc.up())
                dve.wait_ge(vec_c, vc.now())
                TT(tmp[:, :, :], tmp[:, :, :], n2gb[:, 0:1, :].to_broadcast([P, NT, C]), ALU.mult).then_inc(vec_c, vc.up())
                dve.wait_ge(vec_c, vc.now())
                TT(tmp[:, :, :], tmp[:, :, :], n2gb[:, 1:2, :].to_broadcast([P, NT, C]), ALU.add
                   ).then_inc(y2_ready, 1)
                beat(3)
                TT(h1c[:, :, :], h1c[:, :, :], n2[:, :, :], ALU.add).then_inc(vec_c, vc.up())
                dve.wait_ge(vec_c, vc.now())
                dve.wait_ge(fc2_done, after(fc2_done, b))
                beat(4)
                TT(h1c[:, :, :], h1c[:, :, :], tiles(bank(6, NT * C)), ALU.add).then_inc(vec_c, vc.up())
                dve.wait_ge(vec_c, vc.now())
                norm(vc, h1c[:, :, :], n2[:, :, :], sq2[:, :, :], ln2, 2, 4, b).then_inc(n3_ready, 1)

            def moe_a(b, beat):
                beat(5)
                dve.wait_ge(gate_done, after(gate_done, b))
                vv.tensor_copy(gl[:, :, :], bank(7, NT * EXPERTS).rearrange("p (t e) -> p t e", t=NT)).then_inc(vec_c, vc.up())
                dve.wait_ge(vec_c, vc.now())
                apart(dve, gate_vec, b)
                for t in range(NT):
                    vv.max(gtop[:, t, :], gl[:, t, :]).then_inc(vec_c, vc.up())
                dve.wait_ge(vec_c, vc.now())
                apart(dve, gate_vec, b)
                for t in range(NT):
                    vv.max_index(gidx[:, t, :], gtop[:, t, :], gl[:, t, :]).then_inc(vec_c, vc.up())
                TT(gw[:, 0, :], gtop[:, :, 1], gtop[:, :, 0], ALU.subtract).then_inc(gsoft_in, 1)
                dve.wait_ge(gsoft_in, after(gsoft_in, b))
                vv.tensor_copy(gidf[:, :, :], gidx[:, :, :]).then_inc(vec_c, vc.up())
                dve.wait_ge(gsoft_out, after(gsoft_out, b))
                TS(gw[:, 3, :], gw[:, 1, :], 1.0, None, ALU.add).then_inc(vec_c, vc.up())
                dve.wait_ge(vec_c, vc.now())
                vv.reciprocal(gw[:, 2, :], gw[:, 3, :]).then_inc(vec_c, vc.up())
                dve.wait_ge(vec_c, vc.now())
                TT(gw[:, 3, :], gw[:, 2, :], gw[:, 1, :], ALU.mult).then_inc(vec_c, vc.up())
                te = [P, NT, EXPERTS]
                ie = iota_e[:, :].unsqueeze(1).to_broadcast(te)
                TT(coef[:, :, :], gidf[:, :, 0:1].to_broadcast(te), ie, ALU.is_equal).then_inc(vec_c, vc.up())
                TT(coef2[:, :, :], gidf[:, :, 1:2].to_broadcast(te), ie, ALU.is_equal).then_inc(vec_c, vc.up())
                dve.wait_ge(vec_c, vc.now())
                TT(coef[:, :, :], coef[:, :, :], gw[:, 2, :].unsqueeze(2).to_broadcast(te), ALU.mult).then_inc(vec_c, vc.up())
                TT(coef2[:, :, :], coef2[:, :, :], gw[:, 3, :].unsqueeze(2).to_broadcast(te), ALU.mult).then_inc(vec_c, vc.up())
                dve.wait_ge(vec_c, vc.now())
                TT(coef[:, :, :], coef[:, :, :], coef2[:, :, :], ALU.add).then_inc(coef_ready, 1)
                dve.wait_ge(coef_ready, after(coef_ready, b))

            def experts(b, e0, e1, beats, beat):
                for e in range(e0, e1):
                    if e in beats:
                        beat(beats[e])
                    dve.wait_ge(e_out, at(e_out, b, e + 1))
                    dst = moe if e == 0 else tmp
                    dve.wait_ge(vec_c, vc.now())
                    TT(dst[:, :, :], tiles(bank(6 + e % 2, NT * C)), coef[:, :, e:e + 1].to_broadcast([P, NT, C]),
                       ALU.mult).then_inc(e_used, 1)
                    dve.wait_ge(e_used, at(e_used, b, e + 1))
                    if e > 0:
                        TT(moe[:, :, :], moe[:, :, :], tmp[:, :, :], ALU.add).then_inc(vec_c, vc.up())

            def moe_b(b):
                dve.wait_ge(vec_c, vc.now())
                TT(moe[:, :, :], moe[:, :, :], n2[:, :, :], ALU.add).then_inc(vec_c, vc.up())
                dve.wait_ge(vec_c, vc.now())
                dve.wait_ge(eb_out, after(eb_out, b))
                TT(moe[:, :, :], moe[:, :, :], tiles(bank(6, NT * C)), ALU.add).then_inc(vec_c, vc.up())
                dve.wait_ge(vec_c, vc.now())
                norm(vc, moe[:, :, :], tmp[:, :, :], sq2[:, :, :], ln2, 2, 5, b).then_inc(vec_c, vc.up())
                dve.wait_ge(vec_c, vc.now())
                TT(tmp[:, :, :], tmp[:, :, :], ngb[:, 0:1, :].to_broadcast([P, NT, C]), ALU.mult).then_inc(vec_c, vc.up())
                dve.wait_ge(vec_c, vc.now())
                TT(tmp[:, :, :], tmp[:, :, :], ngb[:, 1:2, :].to_broadcast([P, NT, C]), ALU.add).then_inc(vec_c, vc.up())
                dve.wait_ge(vec_c, vc.now())
                if not is_first(b):
                    dve.wait_ge(out_stored, after(out_stored, b - 1))
                TT(outb[:, :, :], tmp[:, :, :], h1c[:, :, :], ALU.add).then_inc(out_ready, 1)
                dve.wait_ge(out_ready, after(out_ready, b))
                dve.sem_inc(c_used, 1)
                vc.end()

            def rest(b, t, beat):
                if t == 0:
                    attention(b, 0, beat)
                    attention(b, 1, beat)
                    attention(b, 2, beat)
                elif t == 1:
                    attention(b, 3, beat)
                    attention(b, 4, beat)
                elif t == 2:
                    attention(b, 5, beat)
                    lsh_a(b, beat)
                elif t == 3:
                    lsh_b(b, beat)
                    mlp(b, beat)
                    moe_a(b, beat)
                    experts(b, 0, MID, {1: 6, 3: 7}, beat)
                elif t == 4:
                    experts(b, MID, LATE, {e: e for e in range(MID, LATE)}, beat)
                elif t == 5:
                    experts(b, LATE, EXPERTS, {e: e for e in range(LATE, EXPERTS)}, beat)
                    moe_b(b)

            pipeline(dve, stage_a, topk, weigh, lambda b, t0, t1: None, rest)


TILE_STEPS = 147
STEPS = dict(vec_a=25, vec_t=6 * TILE_STEPS + 2, vec_c=123)
SET_POOL = 21
SET_ZEROED = 1
SET_CONV = 8
SET_VEC = 71


def kernel(x, L0_tok_filt, L0_tok_W_k, L0_tok_b_k, L0_attn_Wi, L0_attn_bi, L0_attn_Wo, L0_attn_bo,
           L0_attn_params_log, L0_ffn_Wq_pk, L0_ffn_pk_keys, L0_ffn_Wq, L0_ffn_keys_table, L0_ffn_values_table,
           L0_ffn_Wo, L1_attn_rotations, L1_attn_norm1_g, L1_attn_norm1_b, L1_attn_q_w, L1_attn_kv_w,
           L1_attn_norm2_g, L1_attn_norm2_b, L1_attn_fc1_w, L1_attn_fc1_b, L1_attn_fc2_w, L1_attn_fc2_b,
           L1_ffn_gate_w, L1_ffn_gate_b, L1_ffn_w1, L1_ffn_b1, L1_ffn_w2, L1_ffn_b2, L1_ffn_gamma, L1_ffn_beta):
    import concourse.bacc as bacc
    from concourse.bass_utils import run_bass_kernel_spmd

    row = lambda a: np.asarray(a).reshape(1, -1)
    arrays = dict(
        x=np.asarray(x), filt=np.asarray(L0_tok_filt).T, w_k=np.asarray(L0_tok_W_k), b_k=row(L0_tok_b_k),
        wi_t=np.asarray(L0_attn_Wi).T, bi=row(L0_attn_bi), wo_t=np.asarray(L0_attn_Wo).T, bo=row(L0_attn_bo),
        lru_log=np.asarray(L0_attn_params_log).T,
        wqpk_t=np.asarray(L0_ffn_Wq_pk).T.reshape(2 * HEADS, C // 2, C),
        keys_t=np.asarray(L0_ffn_pk_keys).transpose(0, 2, 3, 1).reshape(2 * HEADS, C // 2, NKEY),
        wq=np.asarray(L0_ffn_Wq),
        kv_rows=np.concatenate([np.asarray(L0_ffn_keys_table), np.asarray(L0_ffn_values_table)], axis=1),
        wo_pk=np.asarray(L0_ffn_Wo), rot=np.asarray(L1_attn_rotations).reshape(C, -1),
        n1g=row(L1_attn_norm1_g), n1b=row(L1_attn_norm1_b), q_w=np.asarray(L1_attn_q_w),
        kv_w=np.asarray(L1_attn_kv_w), n2g=row(L1_attn_norm2_g), n2b=row(L1_attn_norm2_b),
        fc1_w=np.asarray(L1_attn_fc1_w), fc1_b=np.asarray(L1_attn_fc1_b).reshape(2, P).T, fc2_w=np.asarray(L1_attn_fc2_w),
        fc2_b=row(L1_attn_fc2_b), gate_w=np.asarray(L1_ffn_gate_w), gate_b=row(L1_ffn_gate_b),
        w1=np.asarray(L1_ffn_w1), b1=np.asarray(L1_ffn_b1)[None], w2=np.asarray(L1_ffn_w2),
        b2=np.asarray(L1_ffn_b2), gamma=row(L1_ffn_gamma), beta=row(L1_ffn_beta),
    )
    arrays = {name: np.ascontiguousarray(a) for name, a in arrays.items()}
    nc = bacc.Bacc("TRN2", target_bir_lowering=False, num_devices=1)
    args = {name: nc.dram_tensor(f"in_{name}", a.shape, mybir.dt.from_np(a.dtype), kind="ExternalInput").ap()
            for name, a in arrays.items()}
    B, L, _ = x.shape
    nt = -(-(L - TAPS) // P)
    out = nc.dram_tensor("tokens_out", (B, L - TAPS, C), F32, kind="ExternalOutput").ap()
    h1_dram = nc.dram_tensor("h1_scratch", (B, P, nt, C), F32, kind="Internal").ap()
    n1t_dram = nc.dram_tensor("n1t_scratch", (B, C, nt * P), F32, kind="Internal").ap()
    audio_tower(nc, **args, out=out, h1_dram=h1_dram, n1t_dram=n1t_dram)
    r = run_bass_kernel_spmd(nc, [{f"in_{name}": a for name, a in arrays.items()}], core_ids=[0])
    return r.results[0]["tokens_out"]
```
